# Optimizing a Trainium2 kernel written in Bass

```python
import numpy as np
import jax
import jax.numpy as jnp

def _softmax(x, axis=-1):
    return jax.nn.softmax(x, axis=axis)

def _gelu(x):
    return jax.nn.gelu(x, approximate=True)

def _silu(x):
    return jax.nn.silu(x)

def _sigmoid(x):
    return jax.nn.sigmoid(x)

def _layernorm(x, axis=-1, eps=1e-05):
    m = jnp.mean(x, axis=axis, keepdims=True)
    v = jnp.var(x, axis=axis, keepdims=True)
    return (x - m) / jnp.sqrt(v + eps)

def _scatter_add(tgt, idx, src, axis=0):
    return tgt.at[idx].add(src)

def _segment_sum(src, seg, n):
    return jax.ops.segment_sum(src, seg, n)
kernel_name = 'mk_gps_d1_gnn_r32_e1087d'

def setup_inputs(seed: int=0):
    np.random.seed(seed)
    _w = jnp.asarray

    def _rec_inputs():
        import jax
        import jax.numpy as jnp
        _gk = jax.random.key(seed)
        x = -0.0003713 + 1 * jax.random.normal(jax.random.fold_in(_gk, 1), (3125, 256), jnp.float32)
        src = jax.random.randint(jax.random.fold_in(_gk, 2), (50000,), 0, 3125, jnp.int32)
        dst = jax.random.randint(jax.random.fold_in(_gk, 3), (50000,), 0, 3125, jnp.int32)
        _o = jnp.argsort(dst, stable=True)
        src = src[_o]
        dst = dst[_o]
        edge_attr_16 = 0.000398945 + 1.00003 * jax.random.normal(jax.random.fold_in(_gk, 11), (50000, 16), jnp.float32)
        edge_type_3 = jax.random.randint(jax.random.fold_in(_gk, 13), (50000,), 0, 3, jnp.int32)
        node_type_6 = jax.random.randint(jax.random.fold_in(_gk, 14), (3125,), 0, 6, jnp.int32)
        return (x, src, dst, edge_attr_16, edge_type_3, node_type_6)
    x, src, dst, edge_attr_16, edge_type_3, node_type_6 = _rec_inputs()

    def _L0_gnn_setup():
        import jax, jax.numpy as jnp
        import numpy as np
        N, E = (50000, 12500)
        IN_DIM = OUT_DIM = 256
        H, DK = (8, 32)
        NT, ET = (6, 3)
        LN_EPS = 1e-05

        def _type_proj(x, node_types, W, b):
            y_all = jnp.einsum('ni,tio->tno', x, W) + b[:, None, :]
            return y_all[node_types, jnp.arange(x.shape[0])]

        def _forward(node_features, edge_index, node_types, edge_types, Wk, bk, Wq, bq, Wv, bv, relation_pri, Wa, Wm, ln_g, ln_b):
            n = node_features.shape[0]
            K = _type_proj(node_features, node_types, Wk, bk).reshape(n, H, DK)
            Q = _type_proj(node_features, node_types, Wq, bq).reshape(n, H, DK)
            V = _type_proj(node_features, node_types, Wv, bv).reshape(n, H, DK)
            src, tgt = (edge_index[0], edge_index[1])
            Ks, Qt, Vs = (K[src], Q[tgt], V[src])
            inv_sqrt_dk = 1.0 / np.sqrt(DK).astype(np.float32)
            msgs = jnp.zeros((edge_types.shape[0], H, DK), jnp.float32)
            for t in range(ET):
                mask = edge_types == t
                Ke = jnp.einsum('ehd,dk->ehk', Ks, Wa[t])
                Ve = jnp.einsum('ehd,dk->ehk', Vs, Wm[t])
                scores = jnp.sum(Ke * Qt, -1) * inv_sqrt_dk * relation_pri[t]
                scores = jnp.where(mask[:, None], scores, -jnp.inf)
                w = jax.nn.softmax(scores, axis=0)
                msgs = msgs + jnp.where(mask[:, None, None], w[..., None] * Ve, 0.0)
            agg = jax.ops.segment_sum(msgs.reshape(-1, OUT_DIM), tgt, num_segments=n)
            out = agg + node_features
            mu = jnp.mean(out, -1, keepdims=True)
            var = jnp.var(out, -1, keepdims=True)
            return (out - mu) * jax.lax.rsqrt(var + LN_EPS) * ln_g + ln_b
        key = jax.random.key(seed)
        ks = jax.random.split(key, 16)
        glorot = lambda k, shape: jax.random.normal(k, shape, jnp.float32) * np.sqrt(2.0 / (shape[-2] + shape[-1]))
        return {'node_features': jax.random.normal(ks[0], (N, IN_DIM), jnp.float32), 'edge_index': jax.random.randint(ks[1], (2, E), 0, N, jnp.int32), 'edge_features': jax.random.normal(ks[2], (E, 16), jnp.float32), 'node_types': jax.random.randint(ks[3], (N,), 0, NT, jnp.int32), 'edge_types': jax.random.randint(ks[4], (E,), 0, ET, jnp.int32), 'Wk': glorot(ks[5], (NT, IN_DIM, OUT_DIM)), 'bk': jnp.zeros((NT, OUT_DIM), jnp.float32), 'Wq': glorot(ks[6], (NT, IN_DIM, OUT_DIM)), 'bq': jnp.zeros((NT, OUT_DIM), jnp.float32), 'Wv': glorot(ks[7], (NT, IN_DIM, OUT_DIM)), 'bv': jnp.zeros((NT, OUT_DIM), jnp.float32), 'relation_pri': jnp.ones((ET, H), jnp.float32), 'Wa': glorot(ks[8], (ET, DK, DK)), 'Wm': glorot(ks[9], (ET, DK, DK)), 'ln_g': jnp.ones((OUT_DIM,), jnp.float32), 'ln_b': jnp.zeros((OUT_DIM,), jnp.float32)}
    _L0_gnn_all = _L0_gnn_setup()
    _L0_gnn_in = {k: v for k, v in _L0_gnn_all.items() if k in ('Wk', 'bk', 'Wq', 'bq', 'Wv', 'bv', 'relation_pri', 'Wa', 'Wm', 'ln_g', 'ln_b')}
    del _L0_gnn_all

    def _L0_mix_setup():
        import jax, jax.numpy as jnp
        import numpy as np
        N, F, C, H = (32, 128, 256, 8)
        D = C // H
        EPS_ATTN = 1e-06
        EPS_LN = 1e-05

        def layer_norm(x, g, b):
            mu = jnp.mean(x, axis=-1, keepdims=True)
            var = jnp.var(x, axis=-1, keepdims=True)
            return (x - mu) * jax.lax.rsqrt(var + EPS_LN) * g + b
        key = jax.random.key(seed)
        ks = jax.random.split(key, 8)
        s = 1.0 / np.sqrt(C)
        return {'x': jax.random.normal(ks[0], (N, F, C), jnp.float32), 'Wqkv': jax.random.uniform(ks[1], (3 * C, C), jnp.float32, -s, s), 'ln1_g': jnp.ones((C,), jnp.float32), 'ln1_b': jnp.zeros((C,), jnp.float32), 'W1': jax.random.uniform(ks[2], (C, C), jnp.float32, -s, s), 'b1': jax.random.uniform(ks[3], (C,), jnp.float32, -s, s), 'W2': jax.random.uniform(ks[4], (C, C), jnp.float32, -s, s), 'b2': jax.random.uniform(ks[5], (C,), jnp.float32, -s, s), 'ln2_g': jnp.ones((C,), jnp.float32), 'ln2_b': jnp.zeros((C,), jnp.float32)}
    _L0_mix_all = _L0_mix_setup()
    _L0_mix_in = {k: v for k, v in _L0_mix_all.items() if k in ('Wqkv', 'ln1_g', 'ln1_b', 'W1', 'b1', 'W2', 'b2', 'ln2_g', 'ln2_b')}
    del _L0_mix_all

    def _L0_ffn_setup():
        import jax, jax.numpy as jnp
        import numpy as np
        B, S, D = (8, 128, 256)
        H = 4 * D
        CAPACITY = 0.5
        key = jax.random.key(seed)
        ks = jax.random.split(key, 6)
        x = jax.random.normal(ks[0], (B, S, D), dtype=jnp.float32)
        attention_mask = jnp.zeros((B, 1, 1, S), dtype=jnp.float32)
        wr = jax.random.normal(ks[1], (D, 1), dtype=jnp.float32) * 0.02
        br = jnp.zeros((1,), dtype=jnp.float32)
        w1 = jax.random.normal(ks[2], (D, H), dtype=jnp.float32) * 0.02
        b1 = jnp.zeros((H,), dtype=jnp.float32)
        w2 = jax.random.normal(ks[3], (H, D), dtype=jnp.float32) * 0.02
        b2 = jnp.zeros((D,), dtype=jnp.float32)
        return {'x': x, 'attention_mask': attention_mask, 'wr': wr, 'br': br, 'w1': w1, 'b1': b1, 'w2': w2, 'b2': b2}
    _L0_ffn_all = _L0_ffn_setup()
    _L0_ffn_in = {k: v for k, v in _L0_ffn_all.items() if k in ('attention_mask', 'wr', 'br', 'w1', 'b1', 'w2', 'b2')}
    del _L0_ffn_all
    return {'x': x, 'src': src, 'dst': dst, 'edge_attr_16': edge_attr_16, 'edge_type_3': edge_type_3, 'node_type_6': node_type_6, 'L0_gnn_Wk': _L0_gnn_in['Wk'], 'L0_gnn_bk': _L0_gnn_in['bk'], 'L0_gnn_Wq': _L0_gnn_in['Wq'], 'L0_gnn_bq': _L0_gnn_in['bq'], 'L0_gnn_Wv': _L0_gnn_in['Wv'], 'L0_gnn_bv': _L0_gnn_in['bv'], 'L0_gnn_relation_pri': _L0_gnn_in['relation_pri'], 'L0_gnn_Wa': _L0_gnn_in['Wa'], 'L0_gnn_Wm': _L0_gnn_in['Wm'], 'L0_gnn_ln_g': _L0_gnn_in['ln_g'], 'L0_gnn_ln_b': _L0_gnn_in['ln_b'], 'L0_mix_Wqkv': _L0_mix_in['Wqkv'], 'L0_mix_ln1_g': _L0_mix_in['ln1_g'], 'L0_mix_ln1_b': _L0_mix_in['ln1_b'], 'L0_mix_W1': _L0_mix_in['W1'], 'L0_mix_b1': _L0_mix_in['b1'], 'L0_mix_W2': _L0_mix_in['W2'], 'L0_mix_b2': _L0_mix_in['b2'], 'L0_mix_ln2_g': _L0_mix_in['ln2_g'], 'L0_mix_ln2_b': _L0_mix_in['ln2_b'], 'L0_ffn_attention_mask': _L0_ffn_in['attention_mask'], 'L0_ffn_wr': _L0_ffn_in['wr'], 'L0_ffn_br': _L0_ffn_in['br'], 'L0_ffn_w1': _L0_ffn_in['w1'], 'L0_ffn_b1': _L0_ffn_in['b1'], 'L0_ffn_w2': _L0_ffn_in['w2'], 'L0_ffn_b2': _L0_ffn_in['b2']}

def reference(x, src, dst, edge_attr_16, edge_type_3, node_type_6, L0_gnn_Wk, L0_gnn_bk, L0_gnn_Wq, L0_gnn_bq, L0_gnn_Wv, L0_gnn_bv, L0_gnn_relation_pri, L0_gnn_Wa, L0_gnn_Wm, L0_gnn_ln_g, L0_gnn_ln_b, L0_mix_Wqkv, L0_mix_ln1_g, L0_mix_ln1_b, L0_mix_W1, L0_mix_b1, L0_mix_W2, L0_mix_b2, L0_mix_ln2_g, L0_mix_ln2_b, L0_ffn_attention_mask, L0_ffn_wr, L0_ffn_br, L0_ffn_w1, L0_ffn_b1, L0_ffn_w2, L0_ffn_b2):
    import jax
    import jax.numpy as jnp

    def _L0_gnn_ref(node_features, edge_index, edge_features, node_types, edge_types, Wk, bk, Wq, bq, Wv, bv, relation_pri, Wa, Wm, ln_g, ln_b):
        import jax, jax.numpy as jnp
        import numpy as np
        N, E = (50000, 12500)
        IN_DIM = OUT_DIM = 256
        H, DK = (8, 32)
        NT, ET = (6, 3)
        LN_EPS = 1e-05

        def _type_proj(x, node_types, W, b):
            y_all = jnp.einsum('ni,tio->tno', x, W) + b[:, None, :]
            return y_all[node_types, jnp.arange(x.shape[0])]

        def _forward(node_features, edge_index, node_types, edge_types, Wk, bk, Wq, bq, Wv, bv, relation_pri, Wa, Wm, ln_g, ln_b):
            n = node_features.shape[0]
            K = _type_proj(node_features, node_types, Wk, bk).reshape(n, H, DK)
            Q = _type_proj(node_features, node_types, Wq, bq).reshape(n, H, DK)
            V = _type_proj(node_features, node_types, Wv, bv).reshape(n, H, DK)
            src, tgt = (edge_index[0], edge_index[1])
            Ks, Qt, Vs = (K[src], Q[tgt], V[src])
            inv_sqrt_dk = 1.0 / np.sqrt(DK).astype(np.float32)
            msgs = jnp.zeros((edge_types.shape[0], H, DK), jnp.float32)
            for t in range(ET):
                mask = edge_types == t
                Ke = jnp.einsum('ehd,dk->ehk', Ks, Wa[t])
                Ve = jnp.einsum('ehd,dk->ehk', Vs, Wm[t])
                scores = jnp.sum(Ke * Qt, -1) * inv_sqrt_dk * relation_pri[t]
                scores = jnp.where(mask[:, None], scores, -jnp.inf)
                w = jax.nn.softmax(scores, axis=0)
                msgs = msgs + jnp.where(mask[:, None, None], w[..., None] * Ve, 0.0)
            agg = jax.ops.segment_sum(msgs.reshape(-1, OUT_DIM), tgt, num_segments=n)
            out = agg + node_features
            mu = jnp.mean(out, -1, keepdims=True)
            var = jnp.var(out, -1, keepdims=True)
            return (out - mu) * jax.lax.rsqrt(var + LN_EPS) * ln_g + ln_b
        return _forward(node_features, edge_index, node_types, edge_types, Wk, bk, Wq, bq, Wv, bv, relation_pri, Wa, Wm, ln_g, ln_b)

    def _L0_mix_ref(x, Wqkv, ln1_g, ln1_b, W1, b1, W2, b2, ln2_g, ln2_b):
        import jax, jax.numpy as jnp
        import numpy as np
        N, F, C, H = (32, 128, 256, 8)
        D = C // H
        EPS_ATTN = 1e-06
        EPS_LN = 1e-05

        def layer_norm(x, g, b):
            mu = jnp.mean(x, axis=-1, keepdims=True)
            var = jnp.var(x, axis=-1, keepdims=True)
            return (x - mu) * jax.lax.rsqrt(var + EPS_LN) * g + b
        n, f, c = x.shape
        qkv = jnp.einsum('nfc,oc->nfo', x, Wqkv)
        q, k, v = jnp.split(qkv, 3, axis=-1)
        q = q.reshape(n, f, H, D)
        k = k.reshape(n, f, H, D)
        v = v.reshape(n, f, H, D)
        q = jax.nn.elu(q) + 1.0
        k = jax.nn.elu(k) + 1.0
        kv = jnp.einsum('nshd,nshm->nhmd', k, v)
        ksum = jnp.sum(k, axis=1)
        z = 1.0 / (jnp.einsum('nlhd,nhd->nlh', q, ksum) + EPS_ATTN)
        t = jnp.einsum('nlhd,nhmd,nlh->nlhm', q, kv, z)
        t = t.reshape(n, f, c)
        x1 = layer_norm(t + x, ln1_g, ln1_b)
        h = jax.nn.gelu(jnp.einsum('nfc,oc->nfo', x1, W1) + b1, approximate=False)
        y = jnp.einsum('nfc,oc->nfo', h, W2) + b2
        return layer_norm(y + x1, ln2_g, ln2_b)

    def _L0_ffn_ref(x, attention_mask, wr, br, w1, b1, w2, b2):
        import jax, jax.numpy as jnp
        import numpy as np
        B, S, D = (8, 128, 256)
        H = 4 * D
        CAPACITY = 0.5
        b, s, d = x.shape
        weights = (jnp.einsum('bsd,do->bso', x, wr) + br)[..., 0]
        k = max(1, int(CAPACITY * s))
        kk = k - 1 if k > 1 else 1
        _, idx = jax.lax.top_k(weights, k)
        sel_idx = idx[:, :kk]
        sel = jnp.take_along_axis(x, sel_idx[:, :, None], axis=1)
        h = jax.nn.gelu(jnp.einsum('bkd,dh->bkh', sel, w1) + b1)
        y = jnp.einsum('bkh,hd->bkd', h, w2) + b2
        w_sel = jnp.take_along_axis(weights, sel_idx, axis=1)
        y = y * w_sel[..., None]
        batch_idx = jnp.arange(b)[:, None]
        processed = jnp.zeros_like(x).at[batch_idx, sel_idx].set(y)
        return processed + x
    edge_index = jnp.stack([src, dst])
    xn = _layernorm(x, axis=-1)
    x = x + _L0_gnn_ref(xn, edge_index, edge_attr_16, node_type_6, edge_type_3, L0_gnn_Wk, L0_gnn_bk, L0_gnn_Wq, L0_gnn_bq, L0_gnn_Wv, L0_gnn_bv, L0_gnn_relation_pri, L0_gnn_Wa, L0_gnn_Wm, L0_gnn_ln_g, L0_gnn_ln_b) + _L0_mix_ref(xn[None], L0_mix_Wqkv, L0_mix_ln1_g, L0_mix_ln1_b, L0_mix_W1, L0_mix_b1, L0_mix_W2, L0_mix_b2, L0_mix_ln2_g, L0_mix_ln2_b)[0]
    x = x + _L0_ffn_ref(_layernorm(x, axis=-1)[None], L0_ffn_attention_mask, L0_ffn_wr, L0_ffn_br, L0_ffn_w1, L0_ffn_b1, L0_ffn_w2, L0_ffn_b2)[0]
    return x

_drawn_inputs = setup_inputs


def setup_inputs(seed=0):
    import zlib

    import numpy as np

    out = dict(_drawn_inputs(seed))
    spreads = {'L0_gnn_bk': (0.0, 2.0),
     'L0_gnn_bq': (0.0, 2.0),
     'L0_gnn_bv': (0.0, 2.0),
     'L0_gnn_relation_pri': (1.0, 0.6),
     'L0_gnn_ln_g': (1.0, 0.2),
     'L0_gnn_ln_b': (0.0, 0.1),
     'L0_mix_ln1_g': (1.0, 0.2),
     'L0_mix_ln1_b': (0.0, 0.1),
     'L0_mix_ln2_g': (1.0, 0.2),
     'L0_mix_ln2_b': (0.0, 0.1),
     'L0_ffn_b1': (0.0, 0.8),
     'L0_ffn_b2': (0.0, 0.8)}
    factors = {'L0_gnn_Wk': 8.0,
     'L0_gnn_Wq': 8.0,
     'L0_gnn_Wv': 8.0,
     'L0_gnn_Wa': 8.0,
     'L0_gnn_Wm': 8.0,
     'L0_mix_Wqkv': 8.0,
     'L0_mix_b1': 8.0,
     'L0_mix_b2': 4.842,
     'L0_ffn_wr': 7.819,
     'L0_ffn_w1': 8.0,
     'L0_ffn_w2': 8.0}
    for name, (base, spread) in spreads.items():
        noise = np.random.default_rng([zlib.crc32(name.encode()), seed]).standard_normal(out[name].shape)
        drawn = base * np.exp(spread * noise) if base else spread * noise
        out[name] = jnp.asarray(drawn.astype(out[name].dtype))
    for name, factor in factors.items():
        out[name] = (out[name] * factor).astype(out[name].dtype)
    return out
```

```python
from contextlib import ExitStack

import numpy as np

import concourse.bass as bass
import concourse.mybir as mybir

F32 = mybir.dt.float32
I32 = mybir.dt.int32
BF16 = mybir.dt.bfloat16
ALU = mybir.AluOpType
ACT = mybir.ActivationFunctionType
AX = mybir.AxisListType.X
RMAX = bass.bass_isa.ReduceOp.max
RADD = bass.bass_isa.ReduceOp.add
ds = bass.ds

P = 128
N, D = 3125, 256
C = D // P
H, DK = 8, 32
NTY, ETY = 6, 3
NT = -(-N // P)
NP = NT * P
LAST = N - (NT - 1) * P
E = 50000
EG = 4
EB = 8
ET = -(-E // (P * EB)) * EB
NG = ET // EG
NB = ET // EB
WIN = 64
NPASS = -(-N // WIN)
ERAW = -(-ET // P)
F = 4 * D
FJ = F // P
KSEL = max(1, int(0.5 * N)) - 1
EPS_LN, EPS_ATTN = 1e-5, 1e-6
BIG = -3.0e38
HALF = NT // 2


def build(nc, a, out):
    kt_d = nc.dram_tensor("kt_scratch", (ETY * NP, D), F32, kind="Internal").ap()
    vt_d = nc.dram_tensor("vt_scratch", (ETY * NP, D), F32, kind="Internal").ap()
    q_d = nc.dram_tensor("q_scratch", (NP, D), F32, kind="Internal").ap()
    w_d = nc.dram_tensor("w_scratch", (NT, P), F32, kind="Internal").ap()
    x_d = a["x"]

    with ExitStack() as ctx:
        def sb(name, shape, dt=F32):
            return ctx.enter_context(nc.sbuf_tensor(name, shape, dt))

        def sem(name):
            return ctx.enter_context(nc.semaphore(name))

        def pair(name):
            return [sem(f"{name}0"), sem(f"{name}1")]

        class Arena:

            def __init__(self, name, size):
                self.t, self.size, self.at = sb(name, [P, size]), size, 0

            def reset(self):
                self.at = 0

            def take(self, *shape):
                n = int(np.prod(shape))
                v = self.t[:, self.at:self.at + n]
                self.at += n
                assert self.at <= self.size
                if len(shape) == 2:
                    return v.rearrange("p (a b) -> p a b", b=shape[1])
                if len(shape) == 3:
                    return v.rearrange("p (a b c) -> p a b c", b=shape[1], c=shape[2])
                return v

        rows = sb("rows", [P, NT, D])
        cols = sb("cols", [P, C, NP])
        big = Arena("big", ETY * ET * H)
        mid = Arena("mid", NP)
        work = Arena("work", 11264)

        ident = sb("ident", [P, P])
        ones = sb("ones", [P, P])
        wqkvT = sb("wqkvT", [P, C, 3 * D])
        w1T = sb("w1T", [P, C, D])
        w2T = sb("w2T", [P, C, D])
        vec_names = ["L0_gnn_ln_g", "L0_gnn_ln_b", "L0_mix_ln1_g", "L0_mix_ln1_b", "L0_mix_ln2_g",
                     "L0_mix_ln2_b", "L0_mix_b2", "L0_ffn_b2"]
        vecs = {n: sb("v_" + n, [P, D]) for n in vec_names}
        wr = sb("wr", [P, D])
        br = sb("br", [P, 1])
        b1c = sb("b1c", [P, C])
        fb1 = sb("fb1", [P, FJ])
        pri = sb("pri", [P, ETY * H])
        bias = sb("bias", [NTY, 3, D])
        bd_a = sb("bd_a", [P, ETY, P])
        bd_m = sb("bd_m", [P, ETY, P])
        iota_p = sb("iota_p", [P, 1])
        iota_i = sb("iota_i", [P, WIN], I32)
        iota_w = sb("iota_w", [P, WIN])
        ip_i = sb("ip_i", [P, 1], I32)
        nhalf = sb("nhalf", [P, 1])
        idx = sb("idx", [P, ET], I32)
        dstf = sb("dstf", [P, ET])
        typf = sb("typf", [P, ET])
        rel = sb("rel", [P, ET])
        base0 = sb("base0", [P, NG])
        base_f = sb("base_f", [P, NG])
        base_i = sb("base_i", [P, NG], I32)
        bad = sb("bad", [P, 4])
        good = sb("good", [P, 1])
        off = sb("off", [P, 1])
        npass_i = sb("npass_i", [P, 1], I32)
        stats = sb("stats", [P, 2, 6])
        mv = sb("mv", [P, 2, 2])
        rstd = sb("rstd", [P, 2, 2])
        smax = sb("smax", [P, ETY * H])
        gmax = sb("gmax", [P, ETY * H])
        ssum = sb("ssum", [P, ETY * H])
        gsum = sb("gsum", [P, ETY * H])
        kvd = sb("kvd", [P, C, 132])
        hmask = sb("hmask", [P, 132])
        w_all = sb("w_all", [P, NT])
        sel = sb("sel", [P, NT])
        rank = sb("rank", [P, 2, 2])
        idxb = sb("idxb", [P, 2, EG], I32)

        wkqv = [big.take(NTY, C, D) for _ in range(3)]
        big.reset()
        sty = [big.take(ET, H) for _ in range(ETY)]
        big.reset()
        fw1 = big.take(C, F)
        fw2 = big.take(FJ, D)
        before = big.take((2 * NT - 1) * P // 2).bitcast(BF16)
        typ_b = mid.take(NP)
        mid.reset()
        scores = mid.take(ET, H)
        mid.reset()
        w_b = mid.take(NP)
        x_in = work.take(2, D)
        xs = work.take(2, D)
        masked = [work.take(NTY, C, P) for _ in range(2)]
        kvT = [work.take(4, P) for _ in range(2)]
        kt_s = [work.take(ETY, D) for _ in range(2)]
        vt_s = work.take(ETY, D)
        q_s = work.take(1, D)
        xT_s = work.take(2, D)
        onehot6 = work.take(2, P)
        assert work.at <= work.size
        work.reset()
        raw = work.take(3 * ERAW * P).bitcast(I32).rearrange("p (a b c) -> p a b c", b=ERAW, c=P)
        rawf = work.take(3, ERAW * P)
        valid = work.take(ET)
        work.reset()
        xs2 = work.take(2, D)
        kmin = work.take(2, D)
        kexp = work.take(2, D)
        kf = work.take(2, D)
        vf = [work.take(C, 129) for _ in range(2)]
        zero = work.take(2 * 132)
        den = work.take(2, H)
        tx = work.take(2, D)
        work.reset()
        gath = work.take(EB, D)
        qwin = work.take(2, D)
        onehot = [work.take(EG, WIN) for _ in range(2)]
        ohT = work.take(2, EG * P)
        prod = work.take(2, 2 * D)
        part = work.take(2, 2 * H)
        msgs = [work.take(EG, D) for _ in range(2)]
        assert work.at <= work.size
        work.reset()
        cs = work.take(2, D)
        csT = work.take(2, D)
        hT = work.take(2, D)
        ga = work.take(2, D)
        gb = work.take(2, D)
        xo = work.take(2, D)
        x3 = work.take(2, D)
        work.reset()
        xfT = work.take(2, D)
        fh = work.take(2, F)
        yw = work.take(NT, D)

        ps = [ctx.enter_context(nc.psum_tensor(f"ps{i}", [P, 512], F32)) for i in range(8)]

        s_settled = [None]

        def rounds(eng, body):
            with eng.Fori(0, HALF) as i:
                body(i, 0)
                body(i, 1)
            body(HALF, 0)

        def settle(eng):
            eng.sem_inc(s_settled[0], 1)

        def all_rounds(eng, sems, unit=1):
            eng.wait_ge(sems[0], unit * (HALF + 1))
            eng.wait_ge(sems[1], unit * HALF)

        class Chain:

            def __init__(self, eng, s):
                self.eng, self.s, self.base, self.n, self.start = eng, s, 0, 0, 0

            def __call__(self, ins):
                ins.then_inc(self.s, 1)
                self.n += 1
                self.eng.wait_ge(self.s, self.base + self.n)

            def turn(self, t, steps):
                self.base, self.n = self.start + t * steps, 0

            def close(self, runs, steps):
                assert self.n == steps, (self.n, steps)
                self.start = self.start + runs * steps
                self.base, self.n = self.start, 0

            def straight(self):
                self.start = self.base + self.n
                self.base, self.n = self.start, 0

        def grouped(v):
            return v.rearrange("p (g k) -> p g k", k=EG)

        def relative(bases):
            return nc.vector.tensor_tensor(grouped(rel[:, :]), grouped(dstf[:, :]),
                                     bases[:, :].rearrange("p (g k) -> p g k", k=1).to_broadcast([P, NG, EG]),
                                     ALU.subtract)

        def rsqrt(c, i, k, var, done, col):
            c.eng.wait_ge(var[k], i + 1)
            settle(c.eng)
            c(nc.gpsimd.tensor_scalar(rstd[:, k, 1:2], mv[:, k, 1:2], EPS_LN, None, ALU.add))
            nc.gpsimd.tensor_tensor(rstd[:, k, 0:1], rstd[:, k, 1:2], nhalf[:, :], ALU.pow).then_inc(done[k], 1)

        def variance(c, src, k, done):
            c(nc.vector.bn_stats(stats[:, k, :], src))
            settle(c.eng)
            nc.vector.bn_aggr(mv[:, k, :], stats[:, k, :]).then_inc(done[k], 1)

        stage_sems = []
        with ExitStack() as stage:
            def sem(name):
                stage_sems.append(nc.alloc_semaphore(name="s1_" + name))
                return stage_sems[-1]

            def pair(name):
                return [sem(f"{name}0"), sem(f"{name}1")]

            s_pc, s_vc = sem("pool_step"), sem("vector_step")
            s_settled[0] = sem("settled")
            s_edges, s_raw0, s_w, s_vec, s_typ, s_bd, s_prep = (sem(n) for n in (
                "edges_loaded", "raw_cleared", "weights_loaded", "vectors_loaded", "types_loaded", "blocks_loaded",
                "bias_loaded"))
            s_const = sem("constants_made")
            s_rawf, s_eT, s_edge = sem("edge_lists_float"), sem("edge_lists_turned"), sem("edge_lists_ready")
            s_bb, s_bad, s_badall, s_np = sem("bases_spread"), sem("bad_marked"), sem("bad_reduced"), sem("npass_ready")

            x_loaded, var_done, rstd_done, xn_kept, xnT_kept, xn_done, xnT_ps, xnT_cp = (pair(n) for n in (
                "x_loaded", "var_done", "rstd_done", "xn_kept", "xnT_kept", "xn_done", "xnT_turned", "xnT_copied"))
            masks_done, kv_ps, kv_cp, q_ps, q_cp, kt_ps, kt_cp, vt_ps, vt_cp = (pair(n) for n in (
                "masks_done", "kv_summed", "kv_copied", "q_summed", "q_copied", "kt_summed", "kt_copied",
                "vt_summed", "vt_copied"))
            kt_st, vt_st, q_st = pair("kt_stored"), pair("vt_stored"), pair("q_stored")

            ma_x, ma_ps, ma_min, ma_exp, ma_kf, ma_v, ma_acc = (pair(n) for n in (
                "mixa_x_copied", "mixa_kv", "mixa_min", "mixa_exp", "mixa_k_done", "mixa_v_done", "mixa_summed"))
            s_zero, s_closed, s_kvd = sem("mixa_zero"), sem("mixa_closed"), sem("mix_state_ready")
            mb_ps, mb_min, mb_exp, mb_q, mb_t, mb_var, mb_rs, mb_done = (pair(n) for n in (
                "mixb_q", "mixb_min", "mixb_exp", "mixb_q_done", "mixb_t", "mixb_var", "mixb_rstd", "mixb_done"))


            block = stage.enter_context(nc.Block())

            @block.sync
            def _(sp):
                for j, (name) in enumerate(("src", "dst", "edge_type_3")):
                    sp.wait_ge(s_raw0, 1)
                    flat = a[name]
                    full = (ERAW - 1) * P * P
                    sp.dma_start(raw[:, j, 0:ERAW - 1, :],
                                 flat[0:full].rearrange("(b r c) -> r b c", r=P, c=P)).then_inc(s_edges, 16)
                    rest = (E - full) // P
                    sp.dma_start(raw[0:rest, j, ERAW - 1, :],
                                 flat[full:full + rest * P].rearrange("(r c) -> r c", c=P)).then_inc(s_edges, 16)
                    tail = E - full - rest * P
                    sp.dma_start(raw[rest:rest + 1, j, ERAW - 1, 0:tail],
                                 flat[full + rest * P:E].rearrange("(r c) -> r c", r=1)).then_inc(s_edges, 16)
                for n, name in enumerate(("L0_gnn_Wk", "L0_gnn_Wv", "L0_gnn_Wq")):
                    sp.dma_start(wkqv[n], a[name].rearrange("t (c p) o -> p (t c) o", p=P)
                                 if False else a[name].rearrange("t (c p) o -> p t c o", p=P)).then_inc(s_w, 16)
                sp.dma_start(typ_b.bitcast(I32)[:, 0:N],
                             a["node_type_6"].rearrange("(r n) -> r n", r=1).to_broadcast([P, N])).then_inc(s_typ, 16)
                for n, name in enumerate(("L0_gnn_bk", "L0_gnn_bv", "L0_gnn_bq")):
                    sp.dma_start(bias[:, n, :], a[name]).then_inc(s_prep, 16)
                sp.wait_ge(s_const, 1)
                for m, name in ((bd_a, "L0_gnn_Wa"), (bd_m, "L0_gnn_Wm")):
                    for g in range(P // DK):
                        sp.dma_start(m[g * DK:(g + 1) * DK, :, g * DK:(g + 1) * DK],
                                     a[name].rearrange("t d k -> d t k")).then_inc(s_bd, 16)
                sp.dma_start(pri[:, :], a["L0_gnn_relation_pri"].rearrange("(r t) h -> r (t h)", r=1)
                             .to_broadcast([P, ETY * H])).then_inc(s_vec, 16)
                for n in vec_names:
                    sp.dma_start(vecs[n][:, :], a[n].rearrange("(r d) -> r d", r=1).to_broadcast([P, D])).then_inc(s_vec, 16)
                sp.dma_start(wr[:, :], a["L0_ffn_wr"].rearrange("(r d) o -> r (d o)", r=1).to_broadcast([P, D])).then_inc(s_vec, 16)
                sp.dma_start(br[:, :], a["L0_ffn_br"].rearrange("(r d) -> r d", r=1).to_broadcast([P, 1])).then_inc(s_vec, 16)
                sp.dma_start(b1c[:, :], a["mix_b1_cols"]).then_inc(s_vec, 16)
                sp.dma_start(fb1[:, :], a["ffn_b1_cols"]).then_inc(s_vec, 16)
                sp.dma_start(wqkvT[:, :, :], a["mix_WqkvT"].rearrange("(c p) o -> p c o", p=P)).then_inc(s_vec, 16)
                sp.dma_start(w1T[:, :, :], a["mix_W1T"].rearrange("(c p) o -> p c o", p=P)).then_inc(s_vec, 16)
                sp.dma_start(w2T[:, :, :], a["mix_W2T"].rearrange("(c p) o -> p c o", p=P)).then_inc(s_vec, 16)

                def load_x(i, k, rows_n=P):
                    sp.wait_ge(xn_done[k], i)
                    sp.dma_start(x_in[0:rows_n, k, :], x_d[ds((2 * i + k) * P, rows_n), :]).then_inc(x_loaded[k], 16)

                def store_tables(i, k):
                    t = (2 * i + k) * P
                    sp.wait_ge(q_cp[k], i + 1)
                    sp.dma_start(q_d[ds(t, P), :], q_s[:, 0, :]).then_inc(q_st[k], 16)
                    sp.wait_ge(kt_cp[k], i + 1)
                    sp.dma_start(kt_d.rearrange("(t n) d -> n t d", n=NP)[ds(t, P)], kt_s[k]).then_inc(kt_st[k], 16)
                    sp.wait_ge(vt_cp[k], i + 1)
                    sp.dma_start(vt_d.rearrange("(t n) d -> n t d", n=NP)[ds(t, P)], vt_s).then_inc(vt_st[k], 16)

                sp.wait_ge(s_edge, 1)
                load_x(0, 0)
                load_x(0, 1)
                with sp.Fori(1, HALF) as i:
                    load_x(i, 0)
                    store_tables(i - 1, 0)
                    load_x(i, 1)
                    store_tables(i - 1, 1)
                load_x(HALF, 0, LAST)
                store_tables(HALF - 1, 0)
                store_tables(HALF - 1, 1)
                store_tables(HALF, 0)

                all_rounds(sp, q_st, 16)
                all_rounds(sp, kt_st, 16)
                all_rounds(sp, vt_st, 16)

            @block.gpsimd
            def _(pool):
                c = Chain(pool, s_pc)
                pool.memset(raw[:, 0:2, ERAW - 1, :], 0)
                pool.memset(raw[:, 2, ERAW - 1, :], ETY).then_inc(s_raw0, 1)
                pool.memset(bd_a[:, :, :], 0.0)
                c(pool.memset(bd_m[:, :, :], 0.0))
                pool.memset(ones[:, :], 1.0)
                pool.memset(nhalf[:, :], -0.5)
                pool.memset(typ_b[:, N:NP], 0.0)
                pool.memset(scores[:, 0:1, 0:1], 0.0) if False else None
                c(pool.memset(ident[:, :], 0.0))
                c(pool.affine_select(out=ident[:, :], in_=ident[:, :], compare_op=ALU.not_equal, fill=1.0, base=0,
                                     pattern=[[-1, P]], channel_multiplier=1))
                c(pool.memset(valid[:, :], 1.0))
                c(pool.affine_select(out=valid[:, :], in_=valid[:, :], compare_op=ALU.is_ge, fill=0.0, base=E - 1,
                                     pattern=[[-P, ET]], channel_multiplier=-1))
                c(pool.memset(hmask[:, :], 1.0))
                for v, pat in ((hmask[:, 0:P].rearrange("p (g m) -> p g m", m=DK), [[-DK, 4], [0, DK]]),
                               (hmask[:, P:P + 4], [[-DK, 4]])):
                    c(pool.affine_select(out=v, in_=v, compare_op=ALU.is_ge, fill=0.0, base=0, pattern=pat,
                                         channel_multiplier=1))
                for v, pat in ((hmask[:, 0:P].rearrange("p (g m) -> p g m", m=DK), [[DK, 4], [0, DK]]),
                               (hmask[:, P:P + 4], [[DK, 4]])):
                    c(pool.affine_select(out=v, in_=v, compare_op=ALU.is_ge, fill=0.0, base=DK - 1, pattern=pat,
                                         channel_multiplier=-1))
                c(pool.iota(iota_i[:, :], pattern=[[1, WIN]], base=0, channel_multiplier=0))
                c(pool.iota(ip_i[:, :], pattern=[[0, 1]], base=0, channel_multiplier=1))
                pool.tensor_copy(iota_w[:, :], iota_i[:, :])
                pool.tensor_copy(iota_p[:, :], ip_i[:, :]).then_inc(s_const, 1)

                pool.wait_ge(s_bad, 1)
                pool.partition_all_reduce(bad[:, 1:2], bad[:, 0:1], P, RMAX).then_inc(s_badall, 1)

                c.straight()

                def node(i, k):
                    c.turn(2 * i + k, 1)
                    rsqrt(c, i, k, var_done, rstd_done, 0)
                    pool.wait_ge(xn_done[k], i + 1)
                    pool.tensor_copy(rows[:, ds(2 * i + k, 1), :], xs[:, ds(k, 1), :]).then_inc(xn_kept[k], 1)
                    pool.wait_ge(xnT_cp[k], i + 1)
                    settle(pool)
                    pool.tensor_copy(cols[:, :, ds((2 * i + k) * P, P)],
                                     xT_s[:, k, :].rearrange("p (c n) -> p c n", c=C)).then_inc(xnT_kept[k], 1)

                rounds(pool, node)
                c.close(NT, 1)

                def mixb(i, k):
                    c.turn(2 * i + k, 1)
                    rsqrt(c, i, k, mb_var, mb_rs, 0)

                rounds(pool, mixb)
                c.close(NT, 1)

            @block.scalar
            def _(act):
                def node(i, k):
                    t = (2 * i + k) * P
                    act.wait_ge(xnT_ps[k], i + 1)
                    act.wait_ge(masks_done[k], i)
                    act.wait_ge(xnT_kept[k], i)
                    act.activation(xT_s[:, k, :], ps[k][:, 0:D], ACT.Copy).then_inc(xnT_cp[k], 1)
                    act.wait_ge(kv_ps[k], i + 1)
                    act.wait_ge(vt_ps[k], i)
                    act.activation(kvT[k], ps[2][:, :].rearrange("p (f n) -> p f n", f=4), ACT.Copy).then_inc(kv_cp[k], 1)
                    act.wait_ge(q_ps[k], i + 1)
                    act.wait_ge(q_st[1 - k], 16 * (i + k))
                    act.activation(q_s[:, 0, :], ps[3][:, 0:D], ACT.Copy).then_inc(q_cp[k], 1)
                    act.wait_ge(vt_ps[k], i + 1)
                    act.wait_ge(vt_st[1 - k], 16 * (i + k))
                    for ch in range(C):
                        ins = act.activation(vt_s[:, :, ch * P:(ch + 1) * P],
                                             ps[6 + ch][:, 0:ETY * P].rearrange("p (t n) -> p t n", t=ETY), ACT.Copy)
                    ins.then_inc(vt_cp[k], 1)

                rounds(act, node)
                all_rounds(act, vt_st, 16)
                all_rounds(act, kt_st, 16)

                def mixa(i, k):
                    t = (2 * i + k) * P
                    act.wait_ge(ma_ps[k], i)
                    settle(act)
                    act.activation(xs2[:, k, :].rearrange("p (c n) -> p c n", c=C), cols[:, :, ds(t, P)],
                                   ACT.Copy).then_inc(ma_x[k], 1)
                    act.wait_ge(ma_ps[k], i + 1)
                    act.wait_ge(ma_acc[k], i)
                    act.activation(vf[k][:, :, 0:P], ps[3 + k][:, 0:D].rearrange("p (c n) -> p c n", c=C),
                                   ACT.Copy).then_inc(ma_v[k], 1)
                    act.wait_ge(ma_min[k], i + 1)
                    act.activation(kexp[:, k, :], kmin[:, k, :], ACT.Exp).then_inc(ma_exp[k], 1)

                all_rounds(act, xnT_kept)
                act.wait_ge(s_zero, 1)
                rounds(act, mixa)

                def mixb(i, k):
                    act.wait_ge(mb_min[k], i + 1)
                    act.activation(kexp[:, k, :], kmin[:, k, :], ACT.Exp).then_inc(mb_exp[k], 1)

                rounds(act, mixb)

            @block.tensor
            def _(pe):
                pe.wait_ge(s_const, 1)
                pe.wait_ge(s_rawf, 1)
                for j in range(3):
                    for b in range(ERAW):
                        r = min(P, ET - b * P)
                        ins = pe.transpose(ps[j][:, b * P:b * P + r], rawf[0:r, j, b * P:(b + 1) * P], ident[0:r, 0:r])
                ins.then_inc(s_eT, 1)
                pe.wait_ge(s_edge, 1)
                pe.matmul(ps[3][:, 0:NG], ones[0:1, :], dstf[0:1, :].rearrange("p (g k) -> p g k", k=EG)[:, :, 0],
                          start=True, stop=True).then_inc(s_bb, 1)

                pe.wait_ge(s_w, 48)
                pe.wait_ge(s_prep, 48)
                pe.wait_ge(s_bd, 16 * 8)
                pe.wait_ge(s_bad, 1)

                def node(i, k):
                    pe.wait_ge(xn_done[k], i + 1)
                    pe.wait_ge(xnT_cp[k], i)
                    for ch in range(C):
                        ins = pe.transpose(ps[k][:, ch * P:(ch + 1) * P], xs[:, k, ch * P:(ch + 1) * P],
                                           ident[:, :])
                    ins.then_inc(xnT_ps[k], 1)
                    pe.wait_ge(masks_done[k], i + 1)
                    pe.wait_ge(kv_cp[1 - k], i + k)
                    for n in range(2):
                        for o in range(C):
                            dst = ps[2][:, (2 * n + o) * P:(2 * n + o + 1) * P]
                            pe.matmul(dst, bias[:, n, o * P:(o + 1) * P], onehot6[0:NTY, k, :], start=True, stop=False)
                            for t in range(NTY):
                                for ch in range(C):
                                    ins = pe.matmul(dst, wkqv[n][:, t, ch, o * P:(o + 1) * P], masked[k][:, t, ch, :],
                                                    start=False, stop=(t == NTY - 1 and ch == C - 1))
                    ins.then_inc(kv_ps[k], 1)
                    pe.wait_ge(q_cp[1 - k], i + k)
                    dst = ps[3][:, 0:D]
                    pe.matmul(dst, onehot6[0:NTY, k, :], bias[:, 2, :], start=True, stop=False)
                    for t in range(NTY):
                        for ch in range(C):
                            ins = pe.matmul(dst, masked[k][:, t, ch, :], wkqv[2][:, t, ch, :], start=False,
                                            stop=(t == NTY - 1 and ch == C - 1))
                    ins.then_inc(q_ps[k], 1)
                    pe.wait_ge(kv_cp[k], i + 1)
                    pe.wait_ge(kt_cp[1 - k], i + k)
                    for ch in range(C):
                        ins = pe.matmul(ps[4 + ch][:, 0:ETY * P], kvT[k][:, ch, :], bd_a[:, :, :].rearrange("p t m -> p (t m)"),
                                        start=True, stop=True)
                    ins.then_inc(kt_ps[k], 1)
                    pe.wait_ge(vt_cp[1 - k], i + k)
                    for ch in range(C):
                        ins = pe.matmul(ps[6 + ch][:, 0:ETY * P], kvT[k][:, 2 + ch, :],
                                        bd_m[:, :, :].rearrange("p t m -> p (t m)"), start=True, stop=True)
                    ins.then_inc(vt_ps[k], 1)

                rounds(pe, node)

                pe.wait_ge(s_vec, 16 * (1 + len(vec_names) + 7))
                pe.wait_ge(s_zero, 2)
                for copied in (kt_cp, kv_cp, q_cp, xnT_cp):
                    all_rounds(pe, copied)
                pe.matmul(ps[2][:, 0:2 * 129], zero[:, 0:P], zero[:, 0:2 * 129], start=True, stop=False)

                def mixa(i, k, n=P):
                    pe.wait_ge(ma_x[k], i + 1)
                    pe.wait_ge(ma_kf[k], i)
                    pe.wait_ge(ma_v[k], i)
                    for j in range(2):
                        for ch in range(C):
                            ins = pe.matmul(ps[3 * j + k][:, 0:D], xs2[:, k, ch * P:(ch + 1) * P],
                                            wqkvT[:, ch, (1 + j) * D:(2 + j) * D], start=(ch == 0), stop=(ch == C - 1))
                    ins.then_inc(ma_ps[k], 1)
                    pe.wait_ge(ma_kf[k], i + 1)
                    pe.wait_ge(ma_v[k], i + 1)
                    for ch in range(C):
                        ins = pe.matmul(ps[2][:, ch * 129:(ch + 1) * 129], kf[0:n, k, ch * P:(ch + 1) * P], vf[k][0:n, ch, :],
                                        start=False, stop=False, skip_group_check=True)
                    ins.then_inc(ma_acc[k], 1)

                with pe.Fori(0, HALF) as i:
                    mixa(i, 0)
                    mixa(i, 1)
                mixa(HALF, 0, LAST)
                pe.matmul(ps[2][:, 0:2 * 129], zero[:, 0:P], zero[:, 0:2 * 129], start=False, stop=True).then_inc(s_closed, 1)

                pe.wait_ge(s_kvd, 1)
                all_rounds(pe, ma_v)
                all_rounds(pe, xnT_kept)

                def mixb(i, k):
                    t = (2 * i + k) * P
                    pe.wait_ge(mb_q[k], i)
                    for o in range(C):
                        for ch in range(C):
                            ins = pe.matmul(ps[k][:, o * P:(o + 1) * P], wqkvT[:, ch, o * P:(o + 1) * P],
                                            cols[:, ch, ds(t, P)], start=(ch == 0), stop=(ch == C - 1))
                    ins.then_inc(mb_ps[k], 1)
                    pe.wait_ge(mb_q[k], i + 1)
                    pe.wait_ge(mb_var[k], i)
                    for ch in range(C):
                        ins = pe.matmul(ps[4 + k][:, ch * 132:(ch + 1) * 132], kf[:, k, ch * P:(ch + 1) * P], kvd[:, ch, :],
                                        start=True, stop=True)
                    ins.then_inc(mb_t[k], 1)

                rounds(pe, mixb)

            @block.vector
            def _(dve):
                c = Chain(dve, s_vc)
                c(dve.memset(off[:, :], 0.0))
                dve.wait_ge(s_edges, 16 * 9)
                dve.wait_ge(s_raw0, 1)
                dve.tensor_copy(rawf.rearrange("p a b -> p (a b)"), raw.rearrange("p a b c -> p (a b c)")).then_inc(s_rawf, 1)
                dve.wait_ge(s_eT, 1)
                c(dve.tensor_copy(typf[:, :], ps[2][:, 0:ET]))
                c(dve.tensor_scalar(rel[:, :], typf[:, :], float(ETY - 1), float(NP), ALU.min, ALU.mult))
                c(dve.tensor_tensor(idx[:, :], rel[:, :], ps[0][:, 0:ET], ALU.add))
                dve.tensor_copy(dstf[:, :], ps[1][:, 0:ET]).then_inc(s_edge, 1)
                dve.wait_ge(s_edge, 1)
                dve.wait_ge(s_const, 1)
                dve.wait_ge(s_bb, 1)
                c(dve.tensor_copy(base0[:, :], ps[3][:, 0:NG]))

                c(relative(base0))
                c(dve.tensor_tensor(rel[:, :], rel[:, :], valid[:, :], ALU.mult))
                c(dve.tensor_reduce(bad[:, 2:3], rel[:, :], AX, ALU.max))
                c(dve.tensor_reduce(bad[:, 3:4], rel[:, :], AX, ALU.min))
                c(dve.tensor_scalar(bad[:, 2:3], bad[:, 2:3], float(WIN), None, ALU.is_ge))
                c(dve.tensor_scalar(bad[:, 3:4], bad[:, 3:4], 0.0, None, ALU.is_lt))
                dve.tensor_tensor(bad[:, 0:1], bad[:, 2:3], bad[:, 3:4], ALU.max).then_inc(s_bad, 1)
                dve.wait_ge(s_badall, 1)
                c(dve.tensor_scalar(good[:, :], bad[:, 1:2], -1.0, 1.0, ALU.mult, ALU.add))
                dve.tensor_scalar(npass_i[:, :], bad[:, 1:2], float(NPASS - 1), 1.0, ALU.mult, ALU.add).then_inc(s_np, 1)
                dve.wait_ge(s_np, 1)
                n = dve.value_load(npass_i[0:1, 0:1], min_val=1, max_val=NPASS)
                dve.wait_ge(s_typ, 16)
                c(dve.tensor_copy(typ_b[:, 0:N], typ_b[:, 0:N].bitcast(I32)))
                dve.wait_ge(s_vec, 16 * (1 + len(vec_names) + 7))
                c(dve.tensor_scalar(pri[:, :], pri[:, :], float(1.0 / np.sqrt(DK).astype(np.float32)), None, ALU.mult))
                c.straight()

                def node(i, k):
                    c.turn(2 * i + k, 1)
                    t = (2 * i + k) * P
                    dve.wait_ge(x_loaded[k], 16 * (i + 1))
                    dve.wait_ge(rstd_done[k], i)
                    variance(c, x_in[:, k, :], k, var_done)
                    dve.wait_ge(var_done[k], i + 1)
                    dve.wait_ge(rstd_done[k], i + 1)
                    dve.wait_ge(xnT_ps[k], i)
                    dve.wait_ge(xn_kept[k], i)
                    dve.tensor_scalar(xs[:, k, :], x_in[:, k, :], mv[:, k, 0:1], rstd[:, k, 0:1], ALU.subtract,
                                      ALU.mult).then_inc(xn_done[k], 1)
                    dve.wait_ge(q_ps[k], i)
                    dve.wait_ge(xnT_cp[k], i + 1)
                    dve.tensor_scalar(onehot6[0:NTY, k, :], typ_b[0:NTY, ds(t, P)], iota_p[0:NTY, :], None, ALU.is_equal)
                    for ty in range(NTY):
                        ins = dve.scalar_tensor_tensor(masked[k][:, ty, :, :],
                                                       typ_b[:, ds(t, P)].rearrange("p (c n) -> p c n", c=1).to_broadcast([P, C, P]),
                                                       float(ty), xT_s[:, k, :].rearrange("p (c n) -> p c n", c=C),
                                                       ALU.is_equal, ALU.mult)
                    ins.then_inc(masks_done[k], 1)
                    dve.wait_ge(kt_ps[k], i + 1)
                    dve.wait_ge(kt_st[k], 16 * i)
                    for ch in range(C):
                        ins = dve.tensor_tensor(
                            kt_s[k][:, :, ch * P:(ch + 1) * P].rearrange("p t (h d) -> p (t h) d", d=DK) if False else
                            kt_s[k].rearrange("p t (h d) -> p t h d", d=DK)[:, :, 4 * ch:4 * ch + 4, :],
                            ps[4 + ch][:, 0:ETY * P].rearrange("p (t h d) -> p t h d", t=ETY, d=DK),
                            pri[:, :].rearrange("p (t h d) -> p t h d", t=ETY, d=1)[:, :, 4 * ch:4 * ch + 4, :]
                            .to_broadcast([P, ETY, 4, DK]), ALU.mult)
                    ins.then_inc(kt_cp[k], 1)

                rounds(dve, node)
                c.close(NT, 1)

                all_rounds(dve, kt_st, 16)
                all_rounds(dve, vt_st, 16)
                dve.memset(vf[0][:, :, P:P + 1], 1.0)
                dve.memset(vf[1][:, :, P:P + 1], 1.0)
                c(dve.memset(zero[:, :], 0.0))
                dve.tensor_copy(den[:, 0, :], zero[:, 0:H]).then_inc(s_zero, 2)
                c.straight()

                def elu(i, k, src, mins, exps, done):
                    dve.tensor_scalar(kmin[:, k, :], src, 0.0, None, ALU.min).then_inc(mins[k], 1)
                    dve.wait_ge(exps[k], i + 1)
                    dve.scalar_tensor_tensor(kf[:, k, :], src, 0.0, kexp[:, k, :], ALU.max, ALU.add).then_inc(done[k], 1)

                def mixa(i, k):
                    dve.wait_ge(ma_ps[k], i + 1)
                    dve.wait_ge(ma_exp[k], i)
                    dve.wait_ge(ma_acc[k], i)
                    elu(i, k, ps[k][:, 0:D], ma_min, ma_exp, ma_kf)

                rounds(dve, mixa)
                dve.wait_ge(s_closed, 1)
                for ch in range(C):
                    c(dve.tensor_tensor(kvd[:, ch, 0:P], ps[2][:, ch * 129:ch * 129 + P], hmask[:, 0:P], ALU.mult))
                    c(dve.tensor_copy(zero[:, ch:ch + 1], ps[2][:, ch * 129 + P:ch * 129 + P + 1]))
                    c(dve.tensor_scalar(kvd[:, ch, P:P + 4], hmask[:, P:P + 4], zero[:, ch:ch + 1], None, ALU.mult))
                dve.tensor_copy(zero[:, 2:3], zero[:, 0:1]).then_inc(s_kvd, 1)
                c.straight()

                def mixb(i, k):
                    c.turn(2 * i + k, 6)
                    dve.wait_ge(mb_ps[k], i + 1)
                    dve.wait_ge(mb_exp[k], i)
                    dve.wait_ge(mb_t[k], i)
                    elu(i, k, ps[k][:, 0:D], mb_min, mb_exp, mb_q)
                    dve.wait_ge(mb_t[k], i + 1)
                    t3 = ps[4 + k][:, 0:2 * 132].rearrange("p (c m) -> p c m", c=C)
                    dk = den[:, k, :].rearrange("p (c h) -> p c h", c=C)
                    c(dve.tensor_scalar(dk, t3[:, :, P:P + 4], EPS_ATTN, None, ALU.add))
                    c(dve.reciprocal(den[:, k, :], den[:, k, :]))
                    c(dve.tensor_tensor(tx[:, k, :].rearrange("p (c h d) -> p c h d", c=C, d=DK),
                                        t3[:, :, 0:P].rearrange("p c (h d) -> p c h d", d=DK),
                                        den[:, k, :].rearrange("p (c h d) -> p c h d", c=C, d=1).to_broadcast([P, C, 4, DK]),
                                        ALU.mult))
                    c(dve.tensor_tensor(tx[:, ds(k, 1), :], tx[:, ds(k, 1), :], rows[:, ds(2 * i + k, 1), :], ALU.add))
                    dve.wait_ge(mb_rs[k], i)
                    variance(c, tx[:, k, :], k, mb_var)
                    dve.wait_ge(mb_var[k], i + 1)
                    c(dve.scalar_tensor_tensor(tx[:, k, :], tx[:, k, :], mv[:, k, 0:1], vecs["L0_mix_ln1_g"][:, :],
                                               ALU.subtract, ALU.mult))
                    dve.wait_ge(mb_rs[k], i + 1)
                    dve.scalar_tensor_tensor(rows[:, ds(2 * i + k, 1), :], tx[:, ds(k, 1), :], rstd[:, k, 0:1],
                                             vecs["L0_mix_ln1_b"][:, :].rearrange("p (a d) -> p a d", a=1),
                                             ALU.mult, ALU.add).then_inc(mb_done[k], 1)

                rounds(dve, mixb)
                c.close(NT, 6)

        nc.clear_and_free_semaphores(stage_sems)
        nc.all_engine_barrier()
        stage_sems = []
        with ExitStack() as stage:
            def sem(name):
                stage_sems.append(nc.alloc_semaphore(name="s2_" + name))
                return stage_sems[-1]

            def pair(name):
                return [sem(f"{name}0"), sem(f"{name}1")]

            s_pc, s_vc = sem("pool_step"), sem("vector_step")
            s_settled[0] = sem("settled")
            s_vc1, s_vc2 = sem("softmax_step"), sem("message_step")
            s_fw, s_fwfree = sem("ffn_weights"), sem("ffn_space")
            def edge_sems(tag):
                names = dict(idx=pair(f"{tag}_idx"), base=sem(f"{tag}_bases"),
                             got=[sem(f"{tag}_row{k}") for k in range(EB)],
                             pad=sem(f"{tag}_pool_turn"),
                             win=pair(f"{tag}_window"), oh=pair(f"{tag}_onehot"), tp=pair(f"{tag}_turned"),
                             tc=pair(f"{tag}_turned_copied"), q=[sem(f"{tag}_q{k}") for k in range(4)],
                             pr=[sem(f"{tag}_prod{k}") for k in range(4)], m=pair(f"{tag}_msgs"),
                             ag=pair(f"{tag}_summed"), add=pair(f"{tag}_added"), end=sem(f"{tag}_bodies"))
                return names

            e1, e2 = edge_sems("e1"), edge_sems("e2")
            s_st, s_gm, s_ex, s_gs, s_wt = (sem(n) for n in (
                "type_max", "type_max_all", "type_exp", "type_sum_all", "edge_weights_ready"))

            block = stage.enter_context(nc.Block())

            @block.sync
            def _(sp):
                n = sp.value_load(npass_i[0:1, 0:1], min_val=1, max_val=NPASS)
                with sp.Fori(0, n) as r:
                    sp.wait_ge(e1["base"], r + 1)
                    settle(sp)
                    with sp.Fori(0, NB) as b:
                        i = r * NB + b
                        for g in range(2):
                            at = sp.value_load(base_i[0:1, ds(2 * b + g, 1)], min_val=0, max_val=NP - WIN)
                            sp.wait_ge(e1["q"][2 * g + 1], i)
                            sp.dma_start(qwin[0:WIN, g, :], q_d[ds(at, WIN), :]).then_inc(e1["win"][g], 16)

                sp.wait_ge(s_fwfree, 1)
                sp.dma_start(fw1, a["L0_ffn_w1"].rearrange("(c p) f -> p c f", p=P)).then_inc(s_fw, 16)
                sp.dma_start(fw2, a["L0_ffn_w2"].rearrange("(j p) d -> p j d", p=P)).then_inc(s_fw, 16)

                sp.wait_ge(s_fw, 32)

            @block.gpsimd
            def _(pool):
                c = Chain(pool, s_pc)

                def gather(e, table, used, stored, first):
                    n = pool.value_load(npass_i[0:1, 0:1], min_val=1, max_val=NPASS)
                    with pool.Fori(0, n) as r:
                        with pool.Fori(0, NB) as b:
                            i = r * NB + b
                            for g in range(2):
                                for k in range(EG):
                                    pool.wait_ge(e["got"][EG * g + k], 16 * i)
                                c(pool.tensor_copy(idxb[:, g, :], idx[:, ds(b * EB + g * EG, EG)])) if False else \
                                    pool.tensor_copy(idxb[:, g, :], idx[:, ds(b * EB + g * EG, EG)]).then_inc(e["idx"][g], 1)
                                pool.wait_ge(e["idx"][g], i + 1)
                                for k in range(EG):
                                    s, per = used(g, k)
                                    pool.wait_ge(s, i * per)
                                    pool.sem_inc(e["pad"], 1)
                                    pool.indirect_dma_start(gath[:, EG * g + k, :], None, table[:, :],
                                                            bass.IndirectOffsetOnAxis(ap=idxb[:, g, k:k + 1], axis=0)
                                                            ).then_inc(e["got"][EG * g + k], 16)
                    return n

                gather(e1, kt_d, lambda g, k: (e1["pr"][2 * g + k // 2], 1), None, None)

                pool.wait_ge(s_st, 1)
                pool.partition_all_reduce(gmax[:, :], smax[:, :], P, RMAX).then_inc(s_gm, 1)
                pool.wait_ge(s_ex, ETY * H)
                pool.partition_all_reduce(gsum[:, :], ssum[:, :], P, RADD).then_inc(s_gs, 1)
                gather(e2, vt_d, lambda g, k: (e2["m"][g], 1), None, None)

            @block.scalar
            def _(act):
                n = act.value_load(npass_i[0:1, 0:1], min_val=1, max_val=NPASS)
                with act.Fori(0, n) as r:
                    with act.Fori(0, NB) as b:
                        i = r * NB + b
                        for g in range(2):
                            act.wait_ge(e1["tp"][g], i + 1)
                            act.wait_ge(e1["q"][2 * g + 1], i)
                            act.activation(ohT[0:WIN, g, :], ps[g][0:WIN, :], ACT.Copy).then_inc(e1["tc"][g], 1)

                act.wait_ge(s_gm, 2)
                for t in range(ETY):
                    for h in range(H):
                        act.activation(sty[t][:, :, h], sty[t][:, :, h], ACT.Exp, bias=smax[:, t * H + h:t * H + h + 1],
                                       accum_out=ssum[:, t * H + h:t * H + h + 1]).then_inc(s_ex, 1)

            @block.tensor
            def _(pe):
                n = pe.value_load(npass_i[0:1, 0:1], min_val=1, max_val=NPASS)
                with pe.Fori(0, n) as r:
                    with pe.Fori(0, NB) as b:
                        i = r * NB + b
                        for g in range(2):
                            pe.wait_ge(e1["oh"][g], i + 1)
                            pe.wait_ge(e1["tc"][g], i)
                            settle(pe)
                            for k in range(EG):
                                ins = pe.transpose(ps[g][0:WIN, k * P:(k + 1) * P], onehot[g][:, k, :], ident[:, :])
                            ins.then_inc(e1["tp"][g], 1)
                            pe.wait_ge(e1["tc"][g], i + 1)
                            pe.wait_ge(e1["win"][g], 16 * (i + 1))
                            for u in range(2):
                                pe.wait_ge(e1["pr"][2 * g + u], i)
                                for k in range(2):
                                    kk = 2 * u + k
                                    ins = pe.matmul(ps[2 + 2 * g + u][:, k * D:(k + 1) * D], ohT[0:WIN, g, kk * P:(kk + 1) * P],
                                                    qwin[0:WIN, g, :], start=True, stop=True)
                                ins.then_inc(e1["q"][2 * g + u], 1)

                with pe.Fori(0, n) as r:
                    with pe.Fori(0, NB) as b:
                        i = r * NB + b
                        for g in range(2):
                            pe.wait_ge(e2["oh"][g], i + 1)
                            pe.wait_ge(e2["m"][g], i + 1)
                            pe.wait_ge(e2["add"][g], i)
                            for ch in range(C):
                                for k in range(EG):
                                    ins = pe.matmul(ps[g][:, ch * WIN:(ch + 1) * WIN], msgs[g][:, k, ch * P:(ch + 1) * P],
                                                    onehot[g][:, k, :], start=(k == 0), stop=(k == EG - 1))
                            ins.then_inc(e2["ag"][g], 1)

            @block.vector
            def _(dve):
                c = Chain(dve, s_vc)
                n = dve.value_load(npass_i[0:1, 0:1], min_val=1, max_val=NPASS)
                c(dve.memset(scores, 0.0))

                def windows(e):
                    c(dve.tensor_scalar(base_f[:, :], base0[:, :], good[:, :], off[:, :], ALU.mult, ALU.add))
                    c(relative(base_f))
                    c(dve.scalar_tensor_tensor(off[:, :], bad[:, 1:2], float(WIN), off[:, :], ALU.mult, ALU.add))
                    dve.tensor_copy(base_i[:, :], base_f[:, :]).then_inc(e["base"], 1)

                def one_hot(e, b, i, g):
                    dve.tensor_tensor(onehot[g],
                                      iota_w[:, :].rearrange("p (a w) -> p a w", a=1).to_broadcast([P, EG, WIN]),
                                      rel[:, ds(b * EB + g * EG, EG)].rearrange("p (k w) -> p k w", w=1)
                                      .to_broadcast([P, EG, WIN]), ALU.is_equal).then_inc(e["oh"][g], 1)

                c.straight()
                start = c.start
                with dve.Fori(0, n) as r:
                    c.base, c.n = start + r * (3 + 4 * NB), 0
                    windows(e1)
                    with dve.Fori(0, NB) as b:
                        i = r * NB + b
                        c.base, c.n = start + r * (3 + 4 * NB) + 3 + b * 4, 0
                        for g in range(2):
                            dve.wait_ge(e1["tp"][g], i)
                            one_hot(e1, b, i, g)
                        for q in range(4):
                            for k in range(2):
                                dve.wait_ge(e1["got"][2 * q + k], 16 * (i + 1))
                            dve.wait_ge(e1["q"][q], i + 1)
                            dve.tensor_tensor(prod[:, q % 2, :], gath[:, 2 * q:2 * q + 2, :].rearrange("p k d -> p (k d)"),
                                              ps[2 + q][:, :], ALU.mult).then_inc(e1["pr"][q], 1)
                            dve.wait_ge(e1["pr"][q], i + 1)
                            c(dve.tensor_reduce(part[:, q % 2, :], prod[:, q % 2, :].rearrange("p (s d) -> p s d", d=DK), AX,
                                                ALU.add))
                            sc = scores[:, ds(b * EB + 2 * q, 2), :]
                            ins = dve.tensor_tensor(sc, sc, part[:, q % 2, :].rearrange("p (k h) -> p k h", k=2), ALU.add)
                        ins.then_inc(e1["end"], 1)
                assert c.n == 4
                c.base, c.n = start + n * (3 + 4 * NB), 0
                dve.wait_ge(e1["end"], n * NB)
                c = Chain(dve, s_vc1)

                for t in range(ETY):
                    c(dve.tensor_scalar(rel[:, :], typf[:, :], float(t), BIG, ALU.not_equal, ALU.mult))
                    for h in range(H):
                        ins = dve.tensor_tensor_reduce(sty[t][:, :, h], scores[:, :, h], rel[:, :], 1.0, BIG, ALU.add,
                                                       ALU.max, smax[:, t * H + h:t * H + h + 1])
                    c(ins)
                dve.sem_inc(s_st, 1)
                dve.wait_ge(s_gm, 1)
                dve.tensor_scalar(smax[:, :], gmax[:, :], -1.0, None, ALU.mult).then_inc(s_gm, 1)
                dve.wait_ge(s_gs, 1)
                c(dve.tensor_scalar(gsum[:, :], gsum[:, :], 1.0e-30, None, ALU.max))
                c(dve.reciprocal(ssum[:, :], gsum[:, :]))

                def inv(t):
                    return ssum[:, t * H:(t + 1) * H].rearrange("p (a h) -> p a h", a=1).to_broadcast([P, ET, H])

                c(dve.tensor_tensor(scores, sty[0], inv(0), ALU.mult))
                for t in range(1, ETY):
                    c(dve.tensor_tensor(sty[t], sty[t], inv(t), ALU.mult))
                    c(dve.tensor_tensor(scores, scores, sty[t], ALU.add))
                c(dve.memset(off[:, :], 0.0))
                dve.sem_inc(s_fwfree, 1)
                dve.sem_inc(s_wt, 1)

                c = Chain(dve, s_vc2)
                start = 0
                with dve.Fori(0, n) as r:
                    c.base, c.n = start + r * 3, 0
                    windows(e2)
                    dve.wait_ge(e2["base"], r + 1)
                    settle(dve)
                    with dve.Fori(0, NB) as b:
                        i = r * NB + b
                        for g in range(2):
                            dve.wait_ge(e2["ag"][g], i)
                            one_hot(e2, b, i, g)
                            for k in range(EG):
                                dve.wait_ge(e2["got"][EG * g + k], 16 * (i + 1))
                            dve.tensor_tensor(msgs[g].rearrange("p k (h d) -> p k h d", d=DK),
                                              gath[:, EG * g:EG * (g + 1), :].rearrange("p k (h d) -> p k h d", d=DK),
                                              scores[:, ds(b * EB + EG * g, EG), :].rearrange("p k (h d) -> p k h d", d=1)
                                              .to_broadcast([P, EG, H, DK]), ALU.mult).then_inc(e2["m"][g], 1)
                        for g in range(2):
                            at = dve.value_load(base_i[0:1, ds(2 * b + g, 1)], min_val=0, max_val=NP - WIN)
                            dve.wait_ge(e2["ag"][g], i + 1)
                            if g == 0:
                                dve.wait_ge(e2["add"][1], i)
                            else:
                                dve.wait_ge(e2["add"][0], i + 1)
                            win = cols[:, :, ds(at, WIN)]
                            ins = dve.tensor_tensor(win, win, ps[g][:, 0:C * WIN].rearrange("p (c w) -> p c w", c=C),
                                                    ALU.add).then_inc(e2["add"][g], 1)
                        dve.wait_ge(e2["add"][1], i + 1)
                        dve.sem_inc(e2["end"], 1)
                c.base, c.n = start + n * 3, 0
                dve.wait_ge(e2["end"], n * NB)
                settle(dve)

        nc.clear_and_free_semaphores(stage_sems)
        nc.all_engine_barrier()
        stage_sems = []
        with ExitStack() as stage:
            def sem(name):
                stage_sems.append(nc.alloc_semaphore(name="s3_" + name))
                return stage_sems[-1]

            def pair(name):
                return [sem(f"{name}0"), sem(f"{name}1")]

            s_pc, s_vc = sem("pool_step"), sem("vector_step")
            s_settled[0] = sem("settled")
            mc_c, mc_T, mc_Tc, mc_h, mc_g, mc_y, mc_x = (pair(n) for n in (
                "mlp_rows", "mlp_turned", "mlp_turned_copied", "mlp_h", "mlp_gelu", "mlp_y", "x_again"))
            mc_v2, mc_r2, mc_ag, mc_gT, mc_v3, mc_r3, mc_v4, mc_r4, mc_xf, mc_fT, mc_fc, mc_x1 = (pair(n) for n in (
                "ln2_var", "ln2_rstd", "agg_copied", "agg_turned", "gnn_var", "gnn_rstd", "ffn_var", "ffn_rstd",
                "xf_done", "xf_turned", "xf_copied", "x1_used"))
            s_wT, s_wTc, s_wst, s_wb, s_tri = (sem(n) for n in (
                "gate_turned", "gate_copied", "gate_stored", "gate_spread", "before_made"))
            ff_x, ff_h, ff_g, ff_y, ff_yw = (pair(n) for n in ("ffn_x", "ffn_h", "ffn_gelu", "ffn_y", "ffn_yw"))
            o_x, o_done, o_st = (pair(n) for n in ("out_base", "out_done", "out_stored"))

            block = stage.enter_context(nc.Block())

            @block.sync
            def _(sp):
                def load_again(i, k, rows_n=P):
                    sp.wait_ge(mc_xf[k], i)
                    sp.dma_start(xo[0:rows_n, k, :], x_d[ds((2 * i + k) * P, rows_n), :]).then_inc(mc_x[k], 16)

                with sp.Fori(0, HALF) as i:
                    load_again(i, 0)
                    load_again(i, 1)
                load_again(HALF, 0, LAST)

                sp.wait_ge(s_wTc, 1)
                sp.dma_start(w_d, cs[0:NT, 0, 0:P]).then_inc(s_wst, 16)
                sp.wait_ge(s_wst, 16)
                sp.dma_start(w_b[:, :], w_d.rearrange("(r t) n -> r (t n)", r=1).to_broadcast([P, NP])).then_inc(s_wb, 16)

                def store_out(i, k, rows_n=P):
                    sp.wait_ge(o_done[k], i + 1)
                    sp.dma_start(out[ds((2 * i + k) * P, rows_n), :], rows[0:rows_n, ds(2 * i + k, 1), :]
                                 .rearrange("p a d -> p (a d)")).then_inc(o_st[k], 16)

                with sp.Fori(0, HALF) as i:
                    store_out(i, 0)
                    store_out(i, 1)
                store_out(HALF, 0, LAST)
                all_rounds(sp, o_st, 16)

            @block.gpsimd
            def _(pool):
                c = Chain(pool, s_pc)

                def closing(i, k):
                    c.turn(2 * i + k, 3)
                    rsqrt(c, i, k, mc_v3, mc_r3, 0)
                    rsqrt(c, i, k, mc_v2, mc_r2, 0)
                    rsqrt(c, i, k, mc_v4, mc_r4, 0)

                c(pool.memset(before[:, :], 1.0))
                c(pool.affine_select(out=before[:, :], in_=before[:, :], compare_op=ALU.is_ge, fill=0.0,
                                     base=(NT - 1) * P - 1, pattern=[[-1, (2 * NT - 1) * P]], channel_multiplier=1))
                pool.engine_nop().then_inc(s_tri, 1) if False else pool.sem_inc(s_tri, 1)
                c.straight()
                rounds(pool, closing)
                c.close(NT, 3)

            @block.scalar
            def _(act):
                def closing(i, k):
                    act.wait_ge(mc_T[k], i)
                    settle(act)
                    act.activation(cs[:, ds(k, 1), :], rows[:, ds(2 * i + k, 1), :], ACT.Copy).then_inc(mc_c[k], 1)
                    act.wait_ge(mc_gT[k], i)
                    settle(act)
                    act.activation(ga[:, k, :].rearrange("p (c n) -> p c n", c=C), cols[:, :, ds((2 * i + k) * P, P)],
                                   ACT.Copy).then_inc(mc_ag[k], 1)
                    act.wait_ge(mc_T[k], i + 1)
                    act.wait_ge(mc_h[k], i)
                    act.activation(csT[:, k, :], ps[0][:, 0:D], ACT.Copy).then_inc(mc_Tc[k], 1)
                    act.wait_ge(mc_h[k], i + 1)
                    act.wait_ge(mc_y[k], i)
                    for j in range(C):
                        ins = act.activation(hT[:, k, j * P:(j + 1) * P], ps[1 + 4 * k][:, j * P:(j + 1) * P],
                                             ACT.Gelu, bias=b1c[:, j:j + 1])
                    ins.then_inc(mc_g[k], 1)
                    act.wait_ge(mc_fT[k], i + 1)
                    settle(act)
                    act.activation(cols[:, :, ds((2 * i + k) * P, P)],
                                   ps[4][:, 0:D].rearrange("p (c n) -> p c n", c=C),
                                   ACT.Copy).then_inc(mc_fc[k], 1)

                rounds(act, closing)
                act.wait_ge(s_wT, 1)
                act.activation(cs[0:NT, 0, 0:P], ps[5][0:NT, 0:P], ACT.Copy).then_inc(s_wTc, 1)
                all_rounds(act, mc_fc)
                act.wait_ge(s_wst, 16)

                def ffn(i, k):
                    act.wait_ge(ff_h[k], i + 1)
                    act.wait_ge(ff_y[k], i)
                    for j in range(FJ):
                        ins = act.activation(fh[:, k, j * P:(j + 1) * P], ps[4 * k // 2 + j // 4][:, (j % 4) * P:(j % 4 + 1) * P],
                                             ACT.Gelu_apprx_tanh, bias=fb1[:, j:j + 1])
                    ins.then_inc(ff_g[k], 1)

                rounds(act, ffn)

            @block.tensor
            def _(pe):
                def closing(i, k):
                    pe.wait_ge(mc_c[k], i + 1)
                    pe.wait_ge(mc_Tc[1 - k], i + k)
                    for ch in range(C):
                        ins = pe.transpose(ps[0][:, ch * P:(ch + 1) * P], cs[:, k, ch * P:(ch + 1) * P],
                                           ident[:, :])
                    ins.then_inc(mc_T[k], 1)
                    pe.wait_ge(mc_ag[k], i + 1)
                    pe.wait_ge(mc_v3[k], i)
                    for ch in range(C):
                        ins = pe.transpose(ps[3 + 4 * k][:, ch * P:(ch + 1) * P], ga[:, k, ch * P:(ch + 1) * P],
                                           ident[:, :])
                    ins.then_inc(mc_gT[k], 1)
                    pe.wait_ge(mc_Tc[k], i + 1)
                    pe.wait_ge(mc_g[k], i)
                    for o in range(C):
                        for ch in range(C):
                            ins = pe.matmul(ps[1 + 4 * k][:, o * P:(o + 1) * P], w1T[:, ch, o * P:(o + 1) * P],
                                            csT[:, k, ch * P:(ch + 1) * P], start=(ch == 0), stop=(ch == C - 1))
                    ins.then_inc(mc_h[k], 1)
                    pe.wait_ge(mc_g[k], i + 1)
                    pe.wait_ge(mc_v2[k], i)
                    for ch in range(C):
                        ins = pe.matmul(ps[2 + 4 * k][:, 0:D], hT[:, k, ch * P:(ch + 1) * P], w2T[:, ch, :],
                                        start=(ch == 0), stop=(ch == C - 1))
                    ins.then_inc(mc_y[k], 1)
                    pe.wait_ge(mc_xf[k], i + 1)
                    pe.wait_ge(mc_fc[1 - k], i + k)
                    for ch in range(C):
                        ins = pe.transpose(ps[4][:, ch * P:(ch + 1) * P], x3[:, k, ch * P:(ch + 1) * P],
                                           ident[:, :])
                    ins.then_inc(mc_fT[k], 1)

                rounds(pe, closing)
                all_rounds(pe, mc_xf)
                pe.transpose(ps[5][0:NT, 0:P], w_all[:, :], ident[:, :]).then_inc(s_wT, 1)
                all_rounds(pe, mc_fc)
                all_rounds(pe, mc_v2)

                def ffn(i, k):
                    t = (2 * i + k) * P
                    pe.wait_ge(ff_g[k], i)
                    for j in range(FJ):
                        for ch in range(C):
                            ins = pe.matmul(ps[2 * k + j // 4][:, (j % 4) * P:(j % 4 + 1) * P], fw1[:, ch, j * P:(j + 1) * P],
                                            cols[:, ch, ds(t, P)], start=(ch == 0), stop=(ch == C - 1))
                    ins.then_inc(ff_h[k], 1)
                    pe.wait_ge(ff_g[k], i + 1)
                    pe.wait_ge(ff_yw[k], i)
                    for j in range(FJ):
                        ins = pe.matmul(ps[6 + k][:, 0:D], fh[:, k, j * P:(j + 1) * P], fw2[:, j, :],
                                        start=(j == 0), stop=(j == FJ - 1))
                    ins.then_inc(ff_y[k], 1)

                rounds(pe, ffn)

            @block.vector
            def _(dve):
                c = Chain(dve, s_vc)

                def affine(k, src, dst, var, rs, g, b, i):
                    c(dve.scalar_tensor_tensor(src, src, mv[:, k, 0:1], vecs[g][:, :], ALU.subtract, ALU.mult))
                    dve.wait_ge(rs[k], i + 1)
                    c(dve.scalar_tensor_tensor(dst, src, rstd[:, k, 0:1], vecs[b][:, :], ALU.mult, ALU.add))

                c.straight()

                def closing(i, k):
                    c.turn(2 * i + k, 13)
                    dve.wait_ge(mc_gT[k], i + 1)
                    dve.wait_ge(mc_r4[k], i)
                    variance(c, ps[3 + 4 * k][:, 0:D], k, mc_v3)
                    dve.wait_ge(mc_v3[k], i + 1)
                    c(dve.scalar_tensor_tensor(gb[:, k, :], ps[3 + 4 * k][:, 0:D], mv[:, k, 0:1], vecs["L0_gnn_ln_g"][:, :],
                                               ALU.subtract, ALU.mult))
                    dve.wait_ge(mc_r3[k], i + 1)
                    c(dve.scalar_tensor_tensor(gb[:, k, :], gb[:, k, :], rstd[:, k, 0:1], vecs["L0_gnn_ln_b"][:, :],
                                               ALU.mult, ALU.add))
                    dve.wait_ge(mc_x[k], 16 * (i + 1))
                    c(dve.tensor_tensor(gb[:, k, :], gb[:, k, :], xo[:, k, :], ALU.add))
                    dve.wait_ge(mc_y[k], i + 1)
                    dve.wait_ge(mc_fT[k], i)
                    c(dve.tensor_tensor(x3[:, k, :], ps[2 + 4 * k][:, 0:D], vecs["L0_mix_b2"][:, :], ALU.add))
                    c(dve.tensor_tensor(x3[:, ds(k, 1), :], x3[:, ds(k, 1), :], rows[:, ds(2 * i + k, 1), :], ALU.add))
                    variance(c, x3[:, k, :], k, mc_v2)
                    dve.wait_ge(mc_v2[k], i + 1)
                    affine(k, x3[:, k, :], x3[:, k, :], mc_v2, mc_r2, "L0_mix_ln2_g", "L0_mix_ln2_b", i)
                    c(dve.tensor_tensor(gb[:, k, :], gb[:, k, :], x3[:, k, :], ALU.add))
                    variance(c, gb[:, k, :], k, mc_v4)
                    dve.wait_ge(mc_v4[k], i + 1)
                    dve.wait_ge(mc_r4[k], i + 1)
                    c(dve.tensor_scalar(x3[:, k, :], gb[:, k, :], mv[:, k, 0:1], rstd[:, k, 0:1], ALU.subtract, ALU.mult))
                    c(dve.scalar_tensor_tensor(rows[:, ds(2 * i + k, 1), :], gb[:, ds(k, 1), :], 1.0, x3[:, ds(k, 1), :],
                                               ALU.mult, ALU.add))
                    dve.tensor_tensor_reduce(gb[:, k, :], x3[:, k, :], wr[:, :], 1.0, 0.0, ALU.mult, ALU.add,
                                             rank[:, k, 0:1]).then_inc(mc_x1[k], 1)
                    dve.wait_ge(mc_x1[k], i + 1)
                    dve.tensor_tensor(w_all[:, ds(2 * i + k, 1)], rank[:, k, 0:1], br[:, :], ALU.add).then_inc(mc_xf[k], 1)

                rounds(dve, closing)
                c.close(NT, 13)
                all_rounds(dve, mc_xf)
                all_rounds(dve, mc_fc)
                all_rounds(dve, mc_fT)
                dve.wait_ge(s_wb, 16)
                dve.wait_ge(s_tri, 1)
                c.straight()

                def ffn(i, k):
                    c.turn(2 * i + k, 6)
                    w_i = w_all[:, ds(2 * i + k, 1)]
                    c(dve.tensor_scalar(scr[:, :], w_b[:, 0:N], w_i, 0.0, ALU.is_gt, ALU.add, accum_out=rank[:, k, 0:1]))
                    start_b = (NT - 1) * P - (2 * i + k) * P
                    c(dve.scalar_tensor_tensor(scr[:, :], w_b[:, 0:N], w_i, before[:, ds(start_b, N)], ALU.is_equal, ALU.mult,
                                               accum_out=rank[:, k, 1:2]))
                    c(dve.tensor_tensor(rank[:, k, 0:1], rank[:, k, 0:1], rank[:, k, 1:2], ALU.add))
                    c(dve.scalar_tensor_tensor(sel[:, ds(2 * i + k, 1)], rank[:, k, 0:1], float(KSEL), w_i, ALU.is_lt, ALU.mult))
                    dve.wait_ge(ff_y[k], i + 1)
                    c(dve.tensor_tensor(yb[:, k, :], ps[6 + k][:, 0:D], vecs["L0_ffn_b2"][:, :], ALU.add))
                    c(dve.scalar_tensor_tensor(rows[:, ds(2 * i + k, 1), :], yb[:, ds(k, 1), :], sel[:, ds(2 * i + k, 1)],
                                               rows[:, ds(2 * i + k, 1), :], ALU.mult, ALU.add))
                    dve.sem_inc(ff_yw[k], 1)
                    dve.sem_inc(o_done[k], 1)

                work.reset()
                work.take(2 * D + 2 * F)
                yb = work.take(2, D)
                scr = work.take(N)
                rounds(dve, ffn)
                c.close(NT, 6)


_INS = ["x", "src", "dst", "edge_type_3", "node_type_6", "L0_gnn_Wk", "L0_gnn_bk", "L0_gnn_Wq", "L0_gnn_bq",
        "L0_gnn_Wv", "L0_gnn_bv", "L0_gnn_relation_pri", "L0_gnn_Wa", "L0_gnn_Wm", "L0_gnn_ln_g", "L0_gnn_ln_b",
        "L0_mix_ln1_g", "L0_mix_ln1_b", "L0_mix_b2", "L0_mix_ln2_g", "L0_mix_ln2_b", "L0_ffn_wr", "L0_ffn_br",
        "L0_ffn_w1", "L0_ffn_w2", "L0_ffn_b2"]


def kernel(**inputs):
    import concourse.bacc as _bacc
    from concourse.bass_utils import run_bass_kernel_spmd as _run

    nc = _bacc.Bacc("TRN2", target_bir_lowering=False, num_devices=1)
    lay = {name: np.ascontiguousarray(inputs[name]) for name in _INS}
    lay["mix_WqkvT"] = np.ascontiguousarray(np.asarray(inputs["L0_mix_Wqkv"]).T)
    lay["mix_W1T"] = np.ascontiguousarray(np.asarray(inputs["L0_mix_W1"]).T)
    lay["mix_W2T"] = np.ascontiguousarray(np.asarray(inputs["L0_mix_W2"]).T)
    lay["mix_b1_cols"] = np.ascontiguousarray(np.asarray(inputs["L0_mix_b1"]).reshape(-1, P).T)
    lay["ffn_b1_cols"] = np.ascontiguousarray(np.asarray(inputs["L0_ffn_b1"]).reshape(-1, P).T)
    arrays, args = {}, {}
    for name, v in lay.items():
        arrays[f"in_{name}"] = v
        args[name] = nc.dram_tensor(f"in_{name}", v.shape, mybir.dt.from_np(v.dtype), kind="ExternalInput").ap()
    out = nc.dram_tensor("out_0", (N, D), F32, kind="ExternalOutput").ap()
    build(nc, args, out)
    r = _run(nc, [arrays], core_ids=[0])
    return r.results[0]["out_0"]
```

```python
from contextlib import ExitStack

import numpy as np

import concourse.bass as bass
import concourse.mybir as mybir

F32 = mybir.dt.float32
I32 = mybir.dt.int32
BF16 = mybir.dt.bfloat16
ALU = mybir.AluOpType
ACT = mybir.ActivationFunctionType
AX = mybir.AxisListType.X
RMAX = bass.bass_isa.ReduceOp.max
RADD = bass.bass_isa.ReduceOp.add
ds = bass.ds

P = 128
N, D = 3125, 256
C = D // P
H, DK = 8, 32
NTY, ETY = 6, 3
NT = -(-N // P)
NP = NT * P
LAST = N - (NT - 1) * P
NS = (N + NTY * (P - 1)) // P
TW = (2 * ETY + 1) * D
E = 50000
EG = 4
GB = 3
EB = EG * GB
NB = -(-E // (P * EB))
ET = NB * EB
NG = ET // EG
WIN = 64
NPASS = -(-N // WIN)
ERAW = -(-ET // P)
F = 4 * D
FJ = F // P
KSEL = max(1, int(0.5 * N)) - 1
EPS_LN, EPS_ATTN = 1e-5, 1e-6
BIG = -3.0e38


def build(nc, a, out):
    def scratch(name, shape, dt=F32):
        return nc.dram_tensor(name, shape, dt, kind="Internal").ap()

    tab_d = scratch("table_scratch", (NP + NS * P, TW))
    xn_d = scratch("xn_scratch", (NP, D))
    dst_d = scratch("dst_scratch", (ET, P), I32)
    perm_d = scratch("perm_scratch", (NS * P, 1), I32)
    w_d = scratch("gate_scratch", (NT, P))
    x_d = a["x"]

    with ExitStack() as ctx:
        def sb(name, shape, dt=F32):
            return ctx.enter_context(nc.sbuf_tensor(name, shape, dt))

        class Arena:

            def __init__(self, name, size):
                self.t, self.size, self.at = sb(name, [P, size]), size, 0

            def reset(self):
                self.at = 0

            def take(self, *shape):
                n = int(np.prod(shape))
                v = self.t[:, self.at:self.at + n]
                self.at += n
                assert self.at <= self.size, self.at
                if len(shape) == 2:
                    return v.rearrange("p (a b) -> p a b", b=shape[1])
                if len(shape) == 3:
                    return v.rearrange("p (a b c) -> p a b c", b=shape[1], c=shape[2])
                return v

        rows = sb("rows", [P, NT, D])
        cols = sb("cols", [P, C, NP])
        big = Arena("big", ETY * ET * H)
        mid = Arena("mid", NP)
        work = Arena("work", 10240)

        ident = sb("ident", [P, P])
        ones = sb("ones", [P, P])
        wqkvT = sb("wqkvT", [P, C, 3 * D])
        w1T = sb("w1T", [P, C, D])
        w2T = sb("w2T", [P, C, D])
        vec_names = ["L0_gnn_ln_g", "L0_gnn_ln_b", "L0_mix_ln1_g", "L0_mix_ln1_b", "L0_mix_ln2_g",
                     "L0_mix_ln2_b", "L0_mix_b2", "L0_ffn_b2"]
        vecs = {n: sb("v_" + n, [P, D]) for n in vec_names}
        wr = sb("wr", [P, D])
        br = sb("br", [P, 1])
        b1c = sb("b1c", [P, C])
        fb1 = sb("fb1", [P, FJ])
        pri = sb("pri", [P, ETY * H])
        bd_a = sb("bd_a", [P, ETY, P])
        bd_m = sb("bd_m", [P, ETY, P])
        iota_p = sb("iota_p", [P, 1])
        iota_w = sb("iota_w", [P, WIN])
        nhalf = sb("nhalf", [P, NT])
        idx_k = sb("idx_k", [P, ET], I32)
        idx_v = sb("idx_v", [P, ET], I32)
        dstf = sb("dstf", [P, ET])
        typf = sb("typf", [P, ET])
        rel = sb("rel", [P, ET])
        base0 = sb("base0", [P, NG])
        base_f = sb("base_f", [P, NG])
        base_n = sb("base_n", [P, NG])
        base_i = sb("base_i", [P, NG], I32)
        bad = sb("bad", [P, 4])
        good = sb("good", [P, 1])
        eps = sb("eps", [P, 1])
        off = sb("off", [P, 1])
        npass_i = sb("npass_i", [P, 1], I32)
        kvd = sb("kvd", [P, C, 132])
        w_all = sb("w_all", [P, NT])
        sel = sb("sel", [P, NT])
        idxb = sb("idxb", [P, GB, EG], I32)

        wall = big.take(NTY, C, 3 * D)
        big.reset()
        sty = [big.take(ET, H) for _ in range(ETY)]
        big.reset()
        fw1 = big.take(C, F)
        fw2 = big.take(FJ, D)
        scores = mid.take(ET, H)
        mid.reset()
        w_b = mid.take(NP)

        raw = work.take(3 * ERAW * P).bitcast(I32).rearrange("p (a b c) -> p a b c", b=ERAW, c=P)
        rawf = work.take(3, ERAW * P)
        valid = work.take(ET)
        iota_wi = work.take(WIN).bitcast(I32)
        iota_pi = work.take(1).bitcast(I32)
        perm_i = work.take(P).bitcast(I32)
        perm_f = work.take(P)
        hmask = work.take(132)
        tri = work.take(P)
        slot_i = work.take(NS).bitcast(I32)
        slot_j = work.take(NS)
        typ_i = work.take(P).bitcast(I32)
        typ_t = work.take(P)
        is_ty = work.take(NTY, NT)
        before_ty = work.take(NTY, NT)
        total_ty = work.take(NTY, NT)
        scan = [work.take(NTY, NT) for _ in range(2)]
        tiles_i = work.take(NTY).bitcast(I32)
        tiles_f = work.take(NTY)
        start_f = work.take(NTY + 1)
        pos_f = work.take(NT)
        node_i = work.take(NT).bitcast(I32)
        stats = work.take(NT, 6)
        mv_all = work.take(NT, 2)
        var_all = work.take(NT)
        rstd_all = work.take(NT)
        xs = work.take(2, D)
        xT_s = work.take(2, D)
        kmin = work.take(2, D)
        kexp = work.take(2, D)
        kf = work.take(2, D)
        vf = [work.take(C, 129) for _ in range(2)]
        zero = work.take(2 * 132)
        work.reset()
        xg = work.take(2, D)
        xgT = work.take(2, D)
        kv_s = work.take(2, 2 * D)
        kvT = work.take(2, 2 * D)
        tab = work.take(2, TW)
        oh6 = work.take(2, P)
        work.reset()
        smax, gmax, ssum, gsum = (sb(n, [P, ETY * H]) for n in ("smax", "gmax", "ssum", "gsum"))
        pos_i = sb("pos_i", [P, NT], I32)
        slot_ty = sb("slot_ty", [P, NS])
        slot_tyi = sb("slot_tyi", [P, NS], I32)
        from_i = sb("from_i", [P, NS], I32)
        to_i = sb("to_i", [P, NS], I32)
        idx_from = sb("idx_from", [P, 2], I32)
        idx_to = sb("idx_to", [P, 2], I32)
        bias6 = sb("bias6", [NTY, 3 * D])
        gath = work.take(EB, D)
        qwin = work.take(GB, D)
        dst_b = work.take(GB, EG * P).bitcast(I32)
        dist = work.take(GB, EG * P)
        ohT = work.take(GB, EG * P)
        prod = work.take(2, 2 * D)
        part = work.take(2, 2 * H)
        work.reset()
        gath2 = work.take(EB, D)
        onehot = [work.take(EG, WIN) for _ in range(GB)]
        msgs = [work.take(EG, D) for _ in range(GB)]
        qmin = work.take(D)
        qexp = work.take(D)
        qf = work.take(D)
        tx = work.take(D)
        x1 = work.take(D)
        hT = work.take(D)
        x2m = work.take(D)
        xa = work.take(D)
        xT2 = work.take(2 * D)
        den = work.take(H)
        sts, mvs, sd, rss = work.take(2, 6), work.take(2, 2), work.take(2), work.take(2)
        work.reset()
        ga = work.take(2, D)
        gb = work.take(2, D)
        xo = work.take(2, D)
        x3 = work.take(2, D)
        st3, mv3, rs3 = work.take(2, 6), work.take(2, 2), work.take(2, 2)
        st4, mv4, rs4 = work.take(2, 6), work.take(2, 2), work.take(2, 2)
        gate = work.take(2, 2)
        w_t = work.take(P)
        xo2 = work.take(D)
        fh = work.take(2, F)
        yb = work.take(2, D)
        rank = work.take(2, 2)
        nw = work.take(NT)
        scr_a = work.take(N // 2 + 1).bitcast(BF16)
        scr_d = work.take(N // 2 + 1).bitcast(BF16)
        assert big.at + (2 * NT - 1) * P // 2 <= big.size
        before = big.take((2 * NT - 1) * P // 2).bitcast(BF16)

        ps = [ctx.enter_context(nc.psum_tensor(f"ps{i}", [P, 512], F32)) for i in range(8)]

        stage_sems, stage_no, settled = [], [0], [None]

        def sem(name):
            stage_sems.append(nc.alloc_semaphore(name=f"s{stage_no[0]}_{name}"))
            return stage_sems[-1]

        def pair(name):
            return [sem(f"{name}0"), sem(f"{name}1")]

        def new_stage():
            if stage_sems:
                nc.clear_and_free_semaphores(stage_sems)
                nc.all_engine_barrier()
            stage_sems.clear()
            stage_no[0] += 1
            settled[0] = sem("settled")

        def settle(eng):
            eng.sem_inc(settled[0], 1)

        class Tile:

            def __init__(self, i, k, n):
                self.i, self.k, self.n, self.t = i, k, n, 2 * i + k

            def at(self, d):
                j = self.k + d
                v = Tile(self.i + j // 2, j % 2, self.n)
                return None if isinstance(v.t, int) and not 0 <= v.t < self.n else v

        def over(eng, n, body):
            for t in range(2):
                body(Tile(0, t, n))
            end = (n - 1) // 2
            with eng.Fori(1, end) as i:
                body(Tile(i, 0, n))
                body(Tile(i, 1, n))
            for t in range(2 * end, n):
                body(Tile(t // 2, t % 2, n))

        def seen(eng, event, tile, unit=1):
            if tile is not None:
                eng.wait_ge(event[tile.k], unit * (tile.i + 1))

        def seen_all(eng, event, n, unit=1):
            seen(eng, event, Tile((n - 1) // 2, (n - 1) % 2, n), unit)
            seen(eng, event, Tile((n - 2) // 2, (n - 2) % 2, n), unit)

        class Chain:

            def __init__(self, eng, s):
                self.eng, self.s, self.base, self.n, self.start, self.per = eng, s, 0, 0, 0, None

            def __call__(self, ins):
                ins.then_inc(self.s, 1)
                self.n += 1
                self.eng.wait_ge(self.s, self.base + self.n)

            def turn(self, t, per):
                self.base, self.n, self.per = self.start + t * per, 0, per

            def close(self, runs):
                assert self.n == self.per, (self.n, self.per)
                self.start = self.start + runs * self.per
                self.base, self.n = self.start, 0

            def straight(self):
                self.start = self.base + self.n
                self.base, self.n = self.start, 0

        def chunks(v):
            return v.rearrange("p (c n) -> p c n", c=C)

        def grouped(v):
            return v.rearrange("p (g k) -> p g k", k=EG)

        def relative(bases):
            return nc.vector.tensor_tensor(grouped(rel[:, :]), grouped(dstf[:, :]),
                                           bases[:, :].rearrange("p (g k) -> p g k", k=1).to_broadcast([P, NG, EG]),
                                           ALU.subtract)

        new_stage()
        vc, pc, vc2 = sem("vector_step"), sem("pool_step"), sem("vector_step_2")
        s_const, s_clear, s_const2 = sem("constants"), sem("cleared"), sem("masks")
        s_edges, s_types, s_x, s_w, s_bias, s_bd, s_vec = (sem(n) for n in (
            "edges_in", "types_in", "x_in", "weights_in", "bias_in", "blocks_in", "vectors_in"))
        s_xc = [sem(f"x_in{j}") for j in range(5)]
        s_dst, s_pinit, s_scat, s_pback, s_xnst = (sem(n) for n in (
            "dst_stored", "slots_cleared", "slots_scattered", "slots_back", "xn_stored"))
        s_tyf, s_tyT, s_isty, s_tysum, s_pos = (sem(n) for n in (
            "types_float", "types_turned", "types_marked", "types_summed", "slots_known"))
        s_rawf, s_eT, s_edge, s_bb, s_bad, s_badall, s_np = (sem(n) for n in (
            "edges_float", "edges_turned", "edges_ready", "bases_spread", "bad_marked", "bad_reduced", "passes_known"))
        s_permf, s_permT, s_perm = sem("slots_float"), sem("slots_turned"), sem("slots_ready")
        s_var, s_rstd = sem("variances"), sem("rstds")
        s_zero, s_closed, s_kvd = sem("zeroed"), sem("state_summed"), sem("state_ready")
        xn_done, xs_done, T_ps, xT_done, cols_done, k_ps, v_done, min_done, exp_done, kf_done, acc_done = (
            pair(n) for n in ("xn", "xs", "xT_ps", "xT", "cols", "kv_ps", "v", "kmin", "kexp", "kf", "acc"))
        g_in, g_T, g_Tc, g_kv, g_kvc, g_qc, g_kvT, g_kvTc, g_tab, g_ktc, g_vtc, g_oh, g_out, g_ix, g_iy = (
            pair(n) for n in ("g_rows", "g_T", "g_Tc", "g_kv", "g_kvc", "g_qc", "g_kvT", "g_kvTc", "g_tab", "g_ktc",
                              "g_vtc", "g_onehot", "g_stored", "g_index", "g_index_out"))

        with nc.Block() as block:
            @block.sync
            def _(sp):
                sp.wait_ge(s_clear, 1)
                sp.dma_start(typ_i[0:NT - 1, :], a["node_type_6"][0:(NT - 1) * P].rearrange("(r c) -> r c", c=P)
                             ).then_inc(s_types, 16)
                sp.dma_start(typ_i[NT - 1:NT, 0:LAST], a["node_type_6"][(NT - 1) * P:N].rearrange("(r c) -> r c", r=1)
                             ).then_inc(s_types, 16)
                for j in range(5):
                    n = 5 if j < 4 else 4
                    sp.dma_start(rows[:, 5 * j:5 * j + n, :],
                                 x_d[5 * j * P:(5 * j + n) * P, :].rearrange("(t p) d -> p t d", p=P)).then_inc(s_xc[j], 16)
                sp.dma_start(rows[0:LAST, NT - 1, :], x_d[(NT - 1) * P:N, :]).then_inc(s_x, 16)
                full, per = (ERAW - 1) * P * P, ERAW - 1
                rest = (E - full) // P
                tail = E - full - rest * P
                for j, name in enumerate(("src", "dst", "edge_type_3")):
                    flat = a[name]
                    sp.dma_start(raw[:, j, 0:per, :], flat[0:full].rearrange("(b r c) -> r b c", r=P, c=P)
                                 ).then_inc(s_edges, 16)
                    sp.dma_start(raw[0:rest, j, per, :], flat[full:full + rest * P].rearrange("(r c) -> r c", c=P)
                                 ).then_inc(s_edges, 16)
                    sp.dma_start(raw[rest:rest + 1, j, per, 0:tail],
                                 flat[full + rest * P:E].rearrange("(r c) -> r c", r=1)).then_inc(s_edges, 16)
                sp.wait_ge(s_const2, 1)
                sp.dma_start(perm_d.rearrange("(j p) o -> j (p o)", p=P), perm_i[0:NS, :]).then_inc(s_pinit, 16)
                sp.dma_start(wqkvT[:, :, :], a["mix_WqkvT"].rearrange("(c p) o -> p c o", p=P)).then_inc(s_vec, 16)
                for n, name in enumerate(("L0_gnn_Wk", "L0_gnn_Wv", "L0_gnn_Wq")):
                    sp.dma_start(wall[:, :, :, n * D:(n + 1) * D].rearrange("p t c o -> p (t c) o"),
                                 a[name].rearrange("t (c p) o -> p (t c) o", p=P)).then_inc(s_w, 16)
                for n, name in enumerate(("L0_gnn_bk", "L0_gnn_bv", "L0_gnn_bq")):
                    sp.dma_start(bias6[:, n * D:(n + 1) * D], a[name]).then_inc(s_bias, 16)
                for m, name in ((bd_a, "L0_gnn_Wa"), (bd_m, "L0_gnn_Wm")):
                    for g in range(P // DK):
                        sp.dma_start(m[g * DK:(g + 1) * DK, :, g * DK:(g + 1) * DK],
                                     a[name].rearrange("t d k -> d t k")).then_inc(s_bd, 16)

                def spread(dst, src, n):
                    sp.dma_start(dst, src.to_broadcast([P, n])).then_inc(s_vec, 16)

                spread(pri[:, :], a["L0_gnn_relation_pri"].rearrange("(r t) h -> r (t h)", r=1), ETY * H)
                for n in vec_names:
                    spread(vecs[n][:, :], a[n].rearrange("(r d) -> r d", r=1), D)
                spread(wr[:, :], a["L0_ffn_wr"].rearrange("(r d) o -> r (d o)", r=1), D)
                spread(br[:, :], a["L0_ffn_br"].rearrange("(r d) -> r d", r=1), 1)
                sp.dma_start(b1c[:, :], a["mix_b1_cols"]).then_inc(s_vec, 16)
                sp.dma_start(fb1[:, :], a["ffn_b1_cols"]).then_inc(s_vec, 16)
                sp.dma_start(w1T[:, :, :], a["mix_W1T"].rearrange("(c p) o -> p c o", p=P)).then_inc(s_vec, 16)
                sp.dma_start(w2T[:, :, :], a["mix_W2T"].rearrange("(c p) o -> p c o", p=P)).then_inc(s_vec, 16)
                sp.wait_ge(s_edges, 16 * 9)
                sp.dma_start(dst_d[0:per * P, :].rearrange("(b r) c -> r b c", r=P), raw[:, 1, 0:per, :]).then_inc(s_dst, 16)
                sp.dma_start(dst_d[per * P:ET, :], raw[0:ET - per * P, 1, per, :]).then_inc(s_dst, 16)
                for j in range(5):
                    last = 5 * j + 4
                    sp.wait_ge(xn_done[last % 2], last // 2 + 1)
                    sp.wait_ge(xn_done[1 - last % 2], (last - 1) // 2 + 1)
                    sp.dma_start(xn_d[5 * j * P:(5 * j + 5) * P, :].rearrange("(t p) d -> p t d", p=P),
                                 rows[:, 5 * j:5 * j + 5, :]).then_inc(s_xnst, 16)
                sp.dma_start(tab_d[N:NP, 2 * ETY * D:TW], rows[LAST:P, NT - 1, :]).then_inc(s_xnst, 16)
                sp.wait_ge(s_scat, 16 * NT)
                sp.dma_start(perm_i[0:NS, :], perm_d.rearrange("(j p) o -> j (p o)", p=P)).then_inc(s_pback, 16)
                sp.wait_ge(s_dst, 32)
                sp.wait_ge(s_xnst, 16 * 6)

            @block.gpsimd
            def _(pool):
                c = Chain(pool, pc)
                pool.memset(raw[:, 0:2, ERAW - 1, :], 0)
                pool.memset(raw[:, 2, ERAW - 1, :], ETY)
                pool.memset(typ_i[:, :], NTY)
                pool.memset(rows[:, NT - 1, :], 0.0).then_inc(s_clear, 1)
                pool.memset(bd_a[:, :, :], 0.0)
                pool.memset(bd_m[:, :, :], 0.0)
                pool.memset(ones[:, :], 1.0)
                pool.memset(nhalf[:, :], -0.5)
                c(pool.memset(ident[:, :], 0.0))
                c(pool.affine_select(out=ident[:, :], in_=ident[:, :], compare_op=ALU.not_equal, fill=1.0, base=0,
                                     pattern=[[-1, P]], channel_multiplier=1))
                c(pool.memset(tri, 1.0))
                c(pool.affine_select(out=tri, in_=tri, compare_op=ALU.is_ge, fill=0.0, base=-1,
                                     pattern=[[1, P]], channel_multiplier=-1))
                c(pool.iota(iota_pi, pattern=[[0, 1]], base=0, channel_multiplier=1))
                c(pool.iota(slot_i, pattern=[[1, NS]], base=0, channel_multiplier=0))
                c(pool.iota(node_i, pattern=[[P, NT]], base=0, channel_multiplier=1))
                pool.tensor_copy(slot_j, slot_i)
                pool.tensor_copy(iota_p[:, :], iota_pi).then_inc(s_const, 1)
                pool.iota(perm_i, pattern=[[1, P]], base=NP, channel_multiplier=P).then_inc(s_const2, 1)
                c(pool.memset(valid, 1.0))
                c(pool.affine_select(out=valid, in_=valid, compare_op=ALU.is_ge, fill=0.0, base=E - 1,
                                     pattern=[[-P, ET]], channel_multiplier=-1))
                c(pool.memset(hmask, 1.0))
                for v, pat in ((hmask[:, 0:P].rearrange("p (g m) -> p g m", m=DK), [[-DK, 4], [0, DK]]),
                               (hmask[:, P:P + 4], [[-DK, 4]])):
                    c(pool.affine_select(out=v, in_=v, compare_op=ALU.is_ge, fill=0.0, base=0, pattern=pat,
                                         channel_multiplier=1))
                    c(pool.affine_select(out=v, in_=v, compare_op=ALU.is_ge, fill=0.0, base=DK - 1,
                                         pattern=[[-q[0], q[1]] for q in pat], channel_multiplier=-1))
                c(pool.iota(iota_wi, pattern=[[1, WIN]], base=0, channel_multiplier=0))
                pool.tensor_copy(iota_w[:, :], iota_wi).then_inc(s_const2, 1)

                pool.wait_ge(s_pos, 1)
                pool.wait_ge(s_pinit, 16)
                for t in range(NT):
                    n = P if t < NT - 1 else LAST
                    pool.indirect_dma_start(perm_d[:, :], bass.IndirectOffsetOnAxis(ap=pos_i[0:n, t:t + 1], axis=0),
                                            node_i[0:n, t:t + 1], None).then_inc(s_scat, 16)
                    if t == 1:
                        pool.wait_ge(s_var, 1)
                        c(pool.tensor_scalar(var_all, mv_all[:, :, 1], EPS_LN, None, ALU.add))
                        pool.tensor_tensor(rstd_all, var_all, nhalf[:, :], ALU.pow).then_inc(s_rstd, 1)
                pool.wait_ge(s_bad, 1)
                pool.partition_all_reduce(bad[:, 1:2], bad[:, 0:1], P, RMAX).then_inc(s_badall, 1)

                pool.wait_ge(s_perm, 1)
                pool.wait_ge(s_xnst, 16 * 6)
                seen_all(pool, acc_done, NT)
                pool.wait_ge(s_kvd, 1)

                def load(t):
                    if t is None:
                        return
                    seen(pool, g_T, t.at(-2))
                    settle(pool)
                    pool.tensor_copy(idx_from[:, t.k:t.k + 1], from_i[:, ds(t.t, 1)]).then_inc(g_ix[t.k], 1)
                    seen(pool, g_ix, t)
                    settle(pool)
                    pool.indirect_dma_start(xg[:, t.k, :], None, xn_d[:, :],
                                            bass.IndirectOffsetOnAxis(ap=idx_from[:, t.k:t.k + 1], axis=0)
                                            ).then_inc(g_in[t.k], 16)

                def store(t):
                    if t is None:
                        return
                    seen(pool, g_ktc, t)
                    seen(pool, g_vtc, t)
                    seen(pool, g_qc, t)
                    seen(pool, g_out, t.at(-2), 16)
                    settle(pool)
                    pool.tensor_copy(idx_to[:, t.k:t.k + 1], to_i[:, ds(t.t, 1)]).then_inc(g_iy[t.k], 1)
                    seen(pool, g_iy, t)
                    settle(pool)
                    pool.indirect_dma_start(tab_d[:, :], bass.IndirectOffsetOnAxis(ap=idx_to[:, t.k:t.k + 1], axis=0),
                                            tab[:, t.k, :], None).then_inc(g_out[t.k], 16)

                def body(t):
                    load(t.at(1))
                    store(t.at(-2))

                load(Tile(0, 0, NS))
                over(pool, NS, body)
                store(Tile((NS - 2) // 2, 0, NS))
                store(Tile((NS - 1) // 2, 1, NS))
                seen_all(pool, g_out, NS, 16)

            @block.scalar
            def _(act):
                def front(t):
                    if t is None:
                        return
                    seen(act, T_ps, t.at(-2))
                    seen(act, xn_done, t)
                    settle(act)
                    act.activation(xs[:, ds(t.k, 1), :], rows[:, ds(t.t, 1), :], ACT.Copy).then_inc(xs_done[t.k], 1)
                    seen(act, k_ps, t.at(-2))
                    seen(act, T_ps, t)
                    act.activation(xT_s[:, t.k, :], ps[t.k][:, 0:D], ACT.Copy).then_inc(xT_done[t.k], 1)
                    act.activation(cols[:, :, ds(t.t * P, P)], chunks(ps[t.k][:, 0:D]), ACT.Copy).then_inc(cols_done[t.k], 1)

                def body(t):
                    front(t.at(1))
                    seen(act, acc_done, t.at(-2))
                    seen(act, k_ps, t)
                    act.activation(vf[t.k][:, :, 0:P], chunks(ps[4 + t.k][:, 0:D]), ACT.Copy).then_inc(v_done[t.k], 1)
                    seen(act, kf_done, t.at(-2))
                    seen(act, min_done, t)
                    act.activation(kexp[:, t.k, :], kmin[:, t.k, :], ACT.Exp).then_inc(exp_done[t.k], 1)

                act.wait_ge(s_zero, 1)
                front(Tile(0, 0, NT))
                over(act, NT, body)

                def turn_in(t):
                    if t is None:
                        return
                    seen(act, g_kv, t.at(-2))
                    seen(act, g_T, t)
                    act.activation(xgT[:, t.k, :], ps[0][:, 0:D], ACT.Copy).then_inc(g_Tc[t.k], 1)

                def v_out(t):
                    if t is None:
                        return
                    seen(act, g_out, t.at(-2), 16)
                    seen(act, g_tab, t)
                    for ch in range(C):
                        ins = act.activation(
                            tab[:, t.k, ETY * D:2 * ETY * D].rearrange("p (t d) -> p t d", d=D)[:, :, ch * P:(ch + 1) * P],
                            ps[6 + ch][:, 0:ETY * P].rearrange("p (t n) -> p t n", t=ETY), ACT.Copy)
                    ins.then_inc(g_vtc[t.k], 1)

                def tables(t):
                    seen(act, g_kvT, t.at(-2))
                    seen(act, g_kv, t)
                    act.activation(kv_s[:, t.k, :], ps[1][:, :], ACT.Copy).then_inc(g_kvc[t.k], 1)
                    seen(act, g_out, t.at(-2), 16)
                    settle(act)
                    act.activation(tab[:, t.k, 2 * ETY * D:TW], ps[2][:, 0:D], ACT.Copy).then_inc(g_qc[t.k], 1)
                    v_out(t.at(-1))
                    turn_in(t.at(1))

                seen_all(act, acc_done, NT)
                act.wait_ge(s_kvd, 1)
                turn_in(Tile(0, 0, NS))
                over(act, NS, tables)
                v_out(Tile((NS - 1) // 2, 1, NS))

            @block.tensor
            def _(pe):
                pe.wait_ge(s_const, 1)
                pe.wait_ge(s_tyf, 1)
                pe.transpose(ps[7][:, 0:NT], typ_t[0:NT, :], ident[0:NT, 0:NT]).then_inc(s_tyT, 1)
                pe.wait_ge(s_isty, 1)
                flat = is_ty.rearrange("p y t -> p (y t)")
                pe.matmul(ps[7][:, 0:NTY * NT], tri, flat, start=True, stop=True)
                pe.matmul(ps[7][:, 256:256 + NTY * NT], ones[:, :], flat, start=True, stop=True).then_inc(s_tysum, 1)
                pe.wait_ge(s_rawf, 1)
                for j in range(3):
                    for b in range(ERAW):
                        r = min(P, ET - b * P)
                        ins = pe.transpose(ps[j][:, b * P:b * P + r], rawf[0:r, j, b * P:(b + 1) * P], ident[0:r, 0:r])
                ins.then_inc(s_eT, 1)
                pe.wait_ge(s_edge, 1)
                pe.matmul(ps[3][:, 0:NG], ones[0:1, :], dstf[0:1, :].rearrange("p (g k) -> p g k", k=EG)[:, :, 0],
                          start=True, stop=True).then_inc(s_bb, 1)
                pe.wait_ge(s_bad, 1)
                pe.wait_ge(s_zero, 1)
                pe.wait_ge(s_vec, 16 * (1 + 1 + len(vec_names) + 6))
                pe.matmul(ps[6][:, 0:2 * 129], zero[:, 0:P], zero[:, 0:2 * 129], start=True, stop=False)

                def front(t):
                    if t is None:
                        return
                    seen(pe, xs_done, t)
                    seen(pe, cols_done, t.at(-2))
                    for ch in range(C):
                        ins = pe.transpose(ps[t.k][:, ch * P:(ch + 1) * P], xs[:, t.k, ch * P:(ch + 1) * P], ident[:, :])
                    ins.then_inc(T_ps[t.k], 1)

                def back(t, n=P):
                    if t is None:
                        return
                    seen(pe, kf_done, t)
                    seen(pe, v_done, t)
                    for ch in range(C):
                        ins = pe.matmul(ps[6][:, ch * 129:(ch + 1) * 129], kf[0:n, t.k, ch * P:(ch + 1) * P],
                                        vf[t.k][0:n, ch, :], start=False, stop=False, skip_group_check=True)
                    ins.then_inc(acc_done[t.k], 1)

                def body(t):
                    front(t.at(1))
                    seen(pe, xT_done, t)
                    seen(pe, kf_done, t.at(-2))
                    seen(pe, v_done, t.at(-2))
                    for j in range(2):
                        for ch in range(C):
                            ins = pe.matmul(ps[2 + 2 * j + t.k][:, 0:D], xT_s[:, t.k, ch * P:(ch + 1) * P],
                                            wqkvT[:, ch, (1 + j) * D:(2 + j) * D], start=(ch == 0), stop=(ch == C - 1))
                    ins.then_inc(k_ps[t.k], 1)
                    back(t.at(-1))

                front(Tile(0, 0, NT))
                over(pe, NT, body)
                back(Tile((NT - 1) // 2, 0, NT), LAST)
                pe.matmul(ps[6][:, 0:2 * 129], zero[:, 0:P], zero[:, 0:2 * 129], start=False, stop=True).then_inc(s_closed, 1)

                pe.wait_ge(s_permf, 1)
                pe.transpose(ps[7][:, 0:NS], perm_f[0:NS, :], ident[0:NS, 0:NS]).then_inc(s_permT, 1)
                pe.wait_ge(s_perm, 1)
                pe.wait_ge(s_kvd, 1)
                pe.wait_ge(s_w, 48)
                pe.wait_ge(s_bias, 48)
                pe.wait_ge(s_bd, 16 * 8)

                def turn_in(t):
                    if t is None:
                        return
                    seen(pe, g_Tc, t.at(-1))
                    seen(pe, g_in, t, 16)
                    settle(pe)
                    for ch in range(C):
                        ins = pe.transpose(ps[0][:, ch * P:(ch + 1) * P], xg[:, t.k, ch * P:(ch + 1) * P], ident[:, :])
                    ins.then_inc(g_T[t.k], 1)

                def per_edge_type(t):
                    if t is None:
                        return
                    seen(pe, g_ktc, t.at(-1))
                    seen(pe, g_vtc, t.at(-1))
                    seen(pe, g_kvTc, t)
                    for n, m in ((0, bd_a), (1, bd_m)):
                        for ch in range(C):
                            ins = pe.matmul(ps[4 + 2 * n + ch][:, 0:ETY * P], kvT[:, t.k, (2 * n + ch) * P:(2 * n + ch + 1) * P],
                                            m[:, :, :].rearrange("p t m -> p (t m)"), start=True, stop=True)
                    ins.then_inc(g_tab[t.k], 1)

                def tables(t):
                    ty = pe.value_load(slot_tyi[0:1, ds(t.t, 1)], min_val=0, max_val=NTY - 1)
                    seen(pe, g_Tc, t)
                    seen(pe, g_oh, t)
                    seen(pe, g_kvc, t.at(-1))
                    seen(pe, g_qc, t.at(-1))
                    settle(pe)
                    for dst, lo, hi in ((ps[1][:, :], 0, 2 * D), (ps[2][:, 0:D], 2 * D, 3 * D)):
                        pe.matmul(dst, oh6[0:NTY, t.k, :], bias6[:, lo:hi], start=True, stop=False)
                        for ch in range(C):
                            ins = pe.matmul(dst, xgT[:, t.k, ch * P:(ch + 1) * P], wall[:, ds(ty, 1), ch, lo:hi]
                                            .rearrange("p a o -> p (a o)"), start=False, stop=(ch == C - 1))
                    ins.then_inc(g_kv[t.k], 1)
                    per_edge_type(t.at(-1))
                    turn_in(t.at(1))
                    seen(pe, g_kvTc, t.at(-1))
                    seen(pe, g_kvc, t)
                    for f in range(4):
                        ins = pe.transpose(ps[3][:, f * P:(f + 1) * P], kv_s[:, t.k, f * P:(f + 1) * P], ident[:, :])
                    ins.then_inc(g_kvT[t.k], 1)

                turn_in(Tile(0, 0, NS))
                over(pe, NS, tables)
                per_edge_type(Tile((NS - 1) // 2, 1, NS))

            @block.vector
            def _(dve):
                c = Chain(dve, vc)
                dve.wait_ge(s_types, 32)
                dve.wait_ge(s_const, 1)
                dve.tensor_copy(typ_t[0:NT, :], typ_i[0:NT, :]).then_inc(s_tyf, 1)
                dve.wait_ge(s_tyT, 1)
                for y in range(NTY):
                    ins = dve.tensor_scalar(is_ty[:, y, :], ps[7][:, 0:NT], float(y), None, ALU.is_equal)
                ins.then_inc(s_isty, 1)
                dve.wait_ge(s_tysum, 1)
                v3 = "p (y t) -> p y t"
                dve.tensor_copy(before_ty, ps[7][:, 0:NTY * NT].rearrange(v3, y=NTY))
                dve.tensor_copy(total_ty, ps[7][:, 256:256 + NTY * NT].rearrange(v3, y=NTY))
                c(dve.tensor_copy(scan[0], ps[7][:, 256:256 + NTY * NT].rearrange(v3, y=NTY)))
                step, at = 1, 0
                while step < NT:
                    dve.tensor_copy(scan[1 - at][:, :, 0:step], scan[at][:, :, 0:step])
                    c(dve.tensor_tensor(scan[1 - at][:, :, step:NT], scan[at][:, :, step:NT], scan[at][:, :, 0:NT - step],
                                        ALU.add))
                    step, at = 2 * step, 1 - at
                c(dve.tensor_scalar(tiles_i, scan[at][:, :, NT - 1], float(P - 1), None, ALU.add))
                c(dve.tensor_scalar(tiles_i, tiles_i, 7, None, ALU.arith_shift_right))
                assert P == 1 << 7
                c(dve.tensor_copy(tiles_f, tiles_i))
                c(dve.memset(start_f[:, 0:1], 0.0))
                for y in range(NTY):
                    c(dve.tensor_tensor(start_f[:, y + 1:y + 2], start_f[:, y:y + 1], tiles_f[:, y:y + 1], ALU.add))
                c(dve.tensor_tensor(before_ty, before_ty, scan[at], ALU.add))
                c(dve.tensor_tensor(before_ty, before_ty, total_ty, ALU.subtract))
                c(dve.scalar_tensor_tensor(before_ty,
                                           start_f[:, 0:NTY].rearrange("p (y t) -> p y t", t=1).to_broadcast([P, NTY, NT]),
                                           float(P), before_ty, ALU.mult, ALU.add))
                c(dve.tensor_tensor(before_ty, before_ty, is_ty, ALU.mult))
                c(dve.tensor_reduce(pos_f, before_ty.rearrange("p y t -> p t y"), AX, ALU.add))
                dve.tensor_copy(pos_i[:, :], pos_f).then_inc(s_pos, 1)
                c(dve.memset(slot_ty[:, :], 0.0))
                for y in range(NTY - 1):
                    c(dve.scalar_tensor_tensor(slot_ty[:, :], slot_j, start_f[:, y + 1:y + 2], slot_ty[:, :], ALU.is_ge,
                                               ALU.add))
                c(dve.tensor_copy(slot_tyi[:, :], slot_ty[:, :]))

                for t in range(NT):
                    if t % 5 == 0:
                        dve.wait_ge(s_xc[t // 5], 16)
                    if t == NT - 1:
                        dve.wait_ge(s_x, 16)
                    ins = dve.bn_stats(stats[:, t, :], rows[:, t, :])
                c(ins)
                for t in range(NT):
                    ins = dve.bn_aggr(mv_all[:, t, :], stats[:, t, :])
                ins.then_inc(s_var, 1)

                dve.wait_ge(s_edges, 16 * 9)
                dve.tensor_copy(rawf.rearrange("p a b -> p (a b)"), raw.rearrange("p a b c -> p (a b c)")).then_inc(s_rawf, 1)
                dve.wait_ge(s_eT, 1)
                c(dve.tensor_copy(typf[:, :], ps[2][:, 0:ET]))
                c(dve.tensor_scalar(rel[:, :], typf[:, :], float(ETY - 1), None, ALU.min))
                c(dve.scalar_tensor_tensor(rel[:, :], ps[0][:, 0:ET], float(2 * ETY + 1), rel[:, :], ALU.mult, ALU.add))
                c(dve.tensor_copy(idx_k[:, :], rel[:, :]))
                c(dve.tensor_scalar(idx_v[:, :], rel[:, :], float(ETY), None, ALU.add))
                dve.tensor_copy(dstf[:, :], ps[1][:, 0:ET]).then_inc(s_edge, 1)
                dve.wait_ge(s_edge, 1)
                dve.wait_ge(s_const2, 2)
                dve.wait_ge(s_bb, 1)
                c(dve.tensor_copy(base0[:, :], ps[3][:, 0:NG]))
                c(relative(base0))
                c(dve.tensor_tensor(rel[:, :], rel[:, :], valid, ALU.mult))
                c(dve.tensor_reduce(bad[:, 2:3], rel[:, :], AX, ALU.max))
                c(dve.tensor_reduce(bad[:, 3:4], rel[:, :], AX, ALU.min))
                c(dve.tensor_scalar(bad[:, 2:3], bad[:, 2:3], float(WIN), None, ALU.is_ge))
                c(dve.tensor_scalar(bad[:, 3:4], bad[:, 3:4], 0.0, None, ALU.is_lt))
                dve.tensor_tensor(bad[:, 0:1], bad[:, 2:3], bad[:, 3:4], ALU.max).then_inc(s_bad, 1)
                c(dve.memset(off[:, :], 0.0))
                dve.memset(vf[0][:, :, P:P + 1], 1.0)
                dve.memset(vf[1][:, :, P:P + 1], 1.0)
                dve.memset(zero, 0.0).then_inc(s_zero, 1)

                dve.wait_ge(s_rstd, 1)

                def front(t):
                    if t is None:
                        return
                    row = rows[:, ds(t.t, 1), :]
                    dve.tensor_scalar(row, row, mv_all[:, ds(t.t, 1), 0:1].rearrange("p a b -> p (a b)"),
                                      rstd_all[:, ds(t.t, 1)], ALU.subtract, ALU.mult).then_inc(xn_done[t.k], 1)

                def back(t):
                    if t is None:
                        return
                    seen(dve, acc_done, t.at(-2))
                    seen(dve, exp_done, t)
                    dve.scalar_tensor_tensor(kf[:, t.k, :], ps[2 + t.k][:, 0:D], 0.0, kexp[:, t.k, :], ALU.max, ALU.add
                                             ).then_inc(kf_done[t.k], 1)

                def body(t):
                    front(t.at(1))
                    seen(dve, k_ps, t)
                    seen(dve, exp_done, t.at(-2))
                    dve.tensor_scalar(kmin[:, t.k, :], ps[2 + t.k][:, 0:D], 0.0, None, ALU.min).then_inc(min_done[t.k], 1)
                    back(t.at(-1))

                front(Tile(0, 0, NT))
                over(dve, NT, body)
                back(Tile((NT - 1) // 2, 0, NT))

                dve.wait_ge(s_badall, 1)
                c(dve.tensor_scalar(good[:, :], bad[:, 1:2], -1.0, 1.0, ALU.mult, ALU.add))
                c(dve.tensor_scalar(npass_i[:, :], bad[:, 1:2], float(NPASS - 1), 1.0, ALU.mult, ALU.add))
                dve.wait_ge(s_pback, 16)
                dve.tensor_copy(perm_f[0:NS, :], perm_i[0:NS, :]).then_inc(s_permf, 1)
                dve.wait_ge(s_closed, 1)
                for ch in range(C):
                    c(dve.tensor_tensor(kvd[:, ch, 0:P], ps[6][:, ch * 129:ch * 129 + P], hmask[:, 0:P], ALU.mult))
                    c(dve.tensor_copy(zero[:, ch:ch + 1], ps[6][:, ch * 129 + P:ch * 129 + P + 1]))
                    c(dve.tensor_scalar(kvd[:, ch, P:P + 4], hmask[:, P:P + 4], zero[:, ch:ch + 1], None, ALU.mult))
                dve.wait_ge(s_permT, 1)
                c(dve.tensor_copy(to_i[:, :], ps[7][:, 0:NS]))
                c(dve.tensor_scalar(from_i[:, :], ps[7][:, 0:NS], float(N - 1), None, ALU.min))
                dve.wait_ge(s_vec, 16 * (1 + 1 + len(vec_names) + 6))
                c(dve.tensor_scalar(pri[:, :], pri[:, :], float(1.0 / np.sqrt(DK).astype(np.float32)), None, ALU.mult))
                seen_all(dve, xT_done, NT)
                dve.sem_inc(s_perm, 1)
                dve.sem_inc(s_kvd, 1)

                def one_hot(t):
                    if t is None:
                        return
                    seen(dve, g_kv, t.at(-2))
                    settle(dve)
                    dve.tensor_scalar(oh6[0:NTY, t.k, :], slot_ty[0:NTY, ds(t.t, 1)].to_broadcast([NTY, P]),
                                      iota_p[0:NTY, :], None, ALU.is_equal).then_inc(g_oh[t.k], 1)

                def k_out(t):
                    if t is None:
                        return
                    seen(dve, g_out, t.at(-2), 16)
                    seen(dve, g_tab, t)
                    for ch in range(C):
                        ins = dve.tensor_tensor(
                            tab[:, t.k, 0:ETY * D].rearrange("p (t h d) -> p t h d", t=ETY, d=DK)[:, :, 4 * ch:4 * ch + 4, :],
                            ps[4 + ch][:, 0:ETY * P].rearrange("p (t h d) -> p t h d", t=ETY, d=DK),
                            pri[:, :].rearrange("p (t h d) -> p t h d", t=ETY, d=1)[:, :, 4 * ch:4 * ch + 4, :]
                            .to_broadcast([P, ETY, 4, DK]), ALU.mult)
                    ins.then_inc(g_ktc[t.k], 1)

                def tables(t):
                    one_hot(t.at(1))
                    k_out(t.at(-1))
                    seen(dve, g_tab, t.at(-2))
                    seen(dve, g_kvT, t)
                    dve.tensor_copy(kvT[:, t.k, :], ps[3][:, :]).then_inc(g_kvTc[t.k], 1)

                one_hot(Tile(0, 0, NS))
                over(dve, NS, tables)
                k_out(Tile((NS - 1) // 2, 1, NS))

        new_stage()
        vc, vs, vm, vd = sem("score_step"), sem("softmax_step"), sem("message_step"), sem("mix_step")
        vb = sem("mix_step_ends")
        e1_base, e2_base, e1_end, e2_end = sem("bases_1"), sem("bases_2"), sem("scored"), sem("summed")
        e1_idx, e2_idx = [sem(f"index_1{g}") for g in range(GB)], [sem(f"index_2{g}") for g in range(GB)]
        e1_got, e2_got = [sem(f"row_1{k}") for k in range(EB)], [sem(f"row_2{k}") for k in range(EB)]
        pool_turn = sem("pool_turn")
        win_in, dstb_in, dist_done, oh_done, oh2, msg_done, agg_ps, agg_add = (
            [sem(f"{n}{g}") for g in range(GB)] for n in ("window", "targets", "distance", "onehotT", "onehot", "message",
                                                          "agg_ps", "agg_added"))
        q_done, prod_done = ([sem(f"{n}{p}") for p in range(2 * GB)] for n in ("q_rows", "product"))
        s_max, s_gmax, s_neg, s_exp, s_gsum, s_alpha = (sem(n) for n in (
            "maxima", "maxima_all", "maxima_negated", "exponentials", "sums_all", "weights_ready"))
        s_fw = sem("ffn_weights_in")
        m_xa, m_T, m_Tc, m_q, m_h, m_min, m_exp, m_gelu, m_kf, m_t, m_y, m_var, m_sd, m_x1, m_x1k, m_fin, m_tx = (
            sem(n) for n in ("mix_xn", "mix_T", "mix_Tc", "mix_q", "mix_h", "mix_min", "mix_exp", "mix_gelu", "mix_kf",
                             "mix_t", "mix_y", "mix_var", "mix_sd", "mix_x1", "mix_x1_kept", "mix_fin", "mix_tx"))

        def passes(eng, first, again):
            n = eng.value_load(npass_i[0:1, 0:1], min_val=1, max_val=NPASS)
            first()
            with eng.If(n > 1):
                with eng.Fori(1, n) as r:
                    again(r)
            return n

        def once(eng, event, t):
            if not (isinstance(t, int) and t < 0):
                eng.wait_ge(event, t + 1)

        def bodies(eng, body):
            for b in range(4):
                body(b, True)
            with eng.Fori(4, NT) as b:
                body(b, True)
            for b in range(NT, NT + 3):
                body(b, True)
            with eng.Fori(NT + 3, NB) as b:
                body(b, False)

        def tile_of(b, back):
            t = b - back
            return None if isinstance(t, int) and not 0 <= t < NT else t

        with nc.Block() as block:
            @block.sync
            def _(sp):
                def scan_pass(r):
                    sp.wait_ge(e1_base, r + 1)
                    settle(sp)
                    with sp.Fori(0, NB) as b:
                        i = r * NB + b
                        for g in range(GB):
                            at = sp.value_load(base_i[0:1, ds(b * GB + g, 1)], min_val=0, max_val=NP - WIN)
                            sp.wait_ge(oh_done[g], i + 1)
                            settle(sp)
                            sp.dma_start(dst_b[0:WIN, g, :],
                                         dst_d.rearrange("(g k) c -> g (k c)", k=EG)[ds(b * GB + g, 1), :]
                                         .to_broadcast([WIN, EG * P])).then_inc(dstb_in[g], 16)
                            sp.wait_ge(q_done[2 * g + 1], i + 1)
                            settle(sp)
                            sp.dma_start(qwin[0:WIN, g, :], tab_d[ds(at, WIN), 2 * ETY * D:TW]).then_inc(win_in[g], 16)

                passes(sp, lambda: scan_pass(0), scan_pass)
                sp.wait_ge(s_alpha, 1)
                sp.dma_start(fw1, a["L0_ffn_w1"].rearrange("(c p) f -> p c f", p=P)).then_inc(s_fw, 16)
                sp.dma_start(fw2, a["L0_ffn_w2"].rearrange("(j p) d -> p j d", p=P)).then_inc(s_fw, 16)
                sp.wait_ge(s_fw, 32)

            @block.gpsimd
            def _(pool):
                def gathers(index, idx_sem, got, dst, free):
                    def scan_pass(r):
                        with pool.Fori(0, NB) as b:
                            i = r * NB + b
                            for g in range(GB):
                                for s in sorted({free(EG * g + k) for k in range(EG)}, key=lambda s: s[0]):
                                    pool.wait_ge(s[1], i + 1)
                                settle(pool)
                                pool.tensor_copy(idxb[:, g, :], index[:, ds(b * EB + g * EG, EG)]).then_inc(idx_sem[g], 1)
                                pool.wait_ge(idx_sem[g], i + 1)
                                pool.sem_inc(pool_turn, 1)
                                for k in range(EG):
                                    pool.indirect_dma_start(dst[:, EG * g + k, :], None, table,
                                                            bass.IndirectOffsetOnAxis(ap=idxb[:, g, k:k + 1], axis=0)
                                                            ).then_inc(got[EG * g + k], 16)
                    return passes(pool, lambda: scan_pass(0), scan_pass)

                table = tab_d[0:N, :].rearrange("n (s d) -> (n s) d", d=D)
                gathers(idx_k, e1_idx, e1_got, gath, lambda k: (k // 2, prod_done[k // 2]))
                pool.wait_ge(s_max, 1)
                pool.partition_all_reduce(gmax[:, :], smax[:, :], P, RMAX).then_inc(s_gmax, 1)
                pool.wait_ge(s_exp, ETY * H)
                pool.partition_all_reduce(gsum[:, :], ssum[:, :], P, RADD).then_inc(s_gsum, 1)
                gathers(idx_v, e2_idx, e2_got, gath2, lambda k: (k // EG, msg_done[k // EG]))

            @block.scalar
            def _(act):
                for g in range(GB):
                    act.sem_inc(oh_done[g], 1)

                def scan_pass(r):
                    act.wait_ge(e1_base, r + 1)
                    settle(act)
                    with act.Fori(0, NB) as b:
                        i = r * NB + b
                        for g in range(GB):
                            act.wait_ge(oh_done[g], i + 1)
                            act.wait_ge(dstb_in[g], 16 * (i + 1))
                            settle(act)
                            act.activation(dist[0:WIN, g, :], dst_b[0:WIN, g, :], ACT.Abs,
                                           bias=base_n[0:WIN, ds(b * GB + g, 1)]).then_inc(dist_done[g], 1)
                            act.wait_ge(q_done[2 * g + 1], i + 1)
                            act.wait_ge(dist_done[g], i + 1)
                            act.activation(ohT[0:WIN, g, :], dist[0:WIN, g, :], ACT.Relu, bias=ones[0:WIN, 0:1],
                                           scale=-1.0).then_inc(oh_done[g], 1)

                passes(act, lambda: scan_pass(0), scan_pass)

                act.wait_ge(s_neg, 1)
                for t in range(ETY):
                    for h in range(H):
                        j = t * H + h
                        act.activation(sty[t][:, :, h], sty[t][:, :, h], ACT.Exp, bias=smax[:, j:j + 1],
                                       accum_out=ssum[:, j:j + 1]).then_inc(s_exp, 1)

                act.wait_ge(s_alpha, 1)

                def body(b, mix):
                    if not mix:
                        return
                    t0, t1, t2, t3 = (tile_of(b, n) for n in range(4))
                    if t0 is not None:
                        once(act, m_T, b - 1)
                        settle(act)
                        act.activation(xa.rearrange("p (a d) -> p a d", a=1), rows[:, ds(t0, 1), :], ACT.Copy).then_inc(m_xa, 1)
                    if t1 is not None or t3 is not None:
                        lo, hi = (0 if t1 is not None else 1), (2 if t3 is not None else 1)
                        once(act, m_var, b - 1)
                        act.activation(sd[:, lo:hi], mvs[:, lo:hi, 1], ACT.Sqrt, bias=eps[:, :]).then_inc(m_sd, 1)
                    if t0 is not None or t2 is not None:
                        lo, hi = (0 if t0 is not None else D), (2 * D if t2 is not None else D)
                        once(act, m_q, b - 1 if t0 is not None else NT - 1)
                        once(act, m_h, b - 3)
                        once(act, m_T, b)
                        act.activation(xT2[:, lo:hi], ps[5][:, lo:hi], ACT.Copy).then_inc(m_Tc, 1)
                    if t1 is not None:
                        once(act, m_x1, t1)
                        settle(act)
                        act.activation(rows[:, ds(t1, 1), :], x1.rearrange("p (a d) -> p a d", a=1), ACT.Copy
                                       ).then_inc(m_x1k, 1)
                    if t2 is not None:
                        once(act, m_y, t2 - 1)
                        once(act, m_h, t2)
                        for j in range(C):
                            ins = act.activation(hT[:, j * P:(j + 1) * P], ps[6][:, j * P:(j + 1) * P], ACT.Gelu,
                                                 bias=b1c[:, j:j + 1])
                        ins.then_inc(m_gelu, 1)
                    if t0 is not None:
                        once(act, m_kf, t0 - 1)
                        once(act, m_min, t0)
                        act.activation(qexp, qmin, ACT.Exp).then_inc(m_exp, 1)

                bodies(act, body)

            @block.tensor
            def _(pe):
                for s in q_done:
                    pe.sem_inc(s, 1)

                def scan_pass(r):
                    with pe.Fori(0, NB) as b:
                        i = r * NB + b
                        for g in range(GB):
                            pe.wait_ge(oh_done[g], i + 2)
                            pe.wait_ge(win_in[g], 16 * (i + 1))
                            for u in range(2):
                                pe.wait_ge(prod_done[2 * g + u], i + 1)
                                for k in range(2):
                                    e = 2 * u + k
                                    ins = pe.matmul(ps[2 * g + u][:, k * D:(k + 1) * D], ohT[0:WIN, g, e * P:(e + 1) * P],
                                                    qwin[0:WIN, g, :], start=True, stop=True)
                                ins.then_inc(q_done[2 * g + u], 1)

                passes(pe, lambda: scan_pass(0), scan_pass)
                pe.wait_ge(s_alpha, 1)

                def sums(i, g):
                    pe.wait_ge(oh2[g], i + 1)
                    pe.wait_ge(msg_done[g], i + 2)
                    pe.wait_ge(agg_add[g], i + 1)
                    for ch in range(C):
                        for k in range(EG):
                            ins = pe.matmul(ps[g][:, ch * WIN:(ch + 1) * WIN], msgs[g][:, k, ch * P:(ch + 1) * P],
                                            onehot[g][:, k, :], start=(k == 0), stop=(k == EG - 1))
                    ins.then_inc(agg_ps[g], 1)

                def body(b, mix):
                    t0, t1, t2, t3 = (tile_of(b, n) if mix else None for n in range(4))
                    sums(b, 0)
                    if t1 is not None:
                        once(pe, m_x1, t1 - 1)
                        once(pe, m_kf, t1)
                        for ch in range(C):
                            ins = pe.matmul(ps[4][:, ch * 132:(ch + 1) * 132], qf[:, ch * P:(ch + 1) * P], kvd[:, ch, :],
                                            start=True, stop=True)
                        ins.then_inc(m_t, 1)
                    if t3 is not None:
                        once(pe, m_fin, t3 - 1)
                        once(pe, m_gelu, t3)
                        for ch in range(C):
                            ins = pe.matmul(ps[7][:, 0:D], hT[:, ch * P:(ch + 1) * P], w2T[:, ch, :],
                                            start=(ch == 0), stop=(ch == C - 1))
                        ins.then_inc(m_y, 1)
                    sums(b, 1)
                    if t0 is not None or t2 is not None:
                        once(pe, m_Tc, b - 1)
                        if t0 is not None:
                            once(pe, m_xa, t0)
                        if t2 is not None:
                            once(pe, m_x1, t2)
                        settle(pe)
                        for src, lo, t in ((xa, 0, t0), (x1, D, t2)):
                            if t is not None:
                                for ch in range(C):
                                    ins = pe.transpose(ps[5][:, lo + ch * P:lo + (ch + 1) * P], src[:, ch * P:(ch + 1) * P],
                                                       ident[:, :])
                        ins.then_inc(m_T, 1)
                    sums(b, 2)
                    if t0 is not None:
                        once(pe, m_kf, t0 - 1)
                        once(pe, m_Tc, b)
                        for o in range(C):
                            for ch in range(C):
                                ins = pe.matmul(ps[3][:, o * P:(o + 1) * P], wqkvT[:, ch, o * P:(o + 1) * P],
                                                xT2[:, ch * P:(ch + 1) * P], start=(ch == 0), stop=(ch == C - 1))
                        ins.then_inc(m_q, 1)
                    if t2 is not None:
                        once(pe, m_gelu, t2 - 1)
                        once(pe, m_Tc, b)
                        for o in range(C):
                            for ch in range(C):
                                ins = pe.matmul(ps[6][:, o * P:(o + 1) * P], w1T[:, ch, o * P:(o + 1) * P],
                                                xT2[:, D + ch * P:D + (ch + 1) * P], start=(ch == 0), stop=(ch == C - 1))
                        ins.then_inc(m_h, 1)

                def again(r):
                    with pe.Fori(0, NB) as b:
                        for g in range(GB):
                            sums(r * NB + b, g)

                passes(pe, lambda: bodies(pe, body), again)

            @block.vector
            def _(dve):
                n = dve.value_load(npass_i[0:1, 0:1], min_val=1, max_val=NPASS)
                for s in prod_done + msg_done + agg_ps + agg_add:
                    dve.sem_inc(s, 1)
                c = Chain(dve, vc)
                c(dve.memset(eps[:, :], EPS_LN))
                c(dve.memset(scores, 0.0))
                c.straight()
                start = c.start

                def windows(base_sem):
                    c(dve.tensor_scalar(base_f[:, :], base0[:, :], good[:, :], off[:, :], ALU.mult, ALU.add))
                    c(relative(base_f))
                    c(dve.tensor_scalar(base_n[:, :], base_f[:, :], iota_p[:, :], -1.0, ALU.add, ALU.mult))
                    c(dve.scalar_tensor_tensor(off[:, :], bad[:, 1:2], float(WIN), off[:, :], ALU.mult, ALU.add))
                    dve.tensor_copy(base_i[:, :], base_f[:, :]).then_inc(base_sem, 1)

                def scan_pass(r):
                    c.base, c.n = start + r * (4 + 2 * GB * NB), 0
                    windows(e1_base)
                    with dve.Fori(0, NB) as b:
                        i = r * NB + b
                        c.base, c.n = start + r * (4 + 2 * GB * NB) + 4 + b * 2 * GB, 0
                        for q in range(2 * GB):
                            for k in range(2):
                                dve.wait_ge(e1_got[2 * q + k], 16 * (i + 1))
                            dve.wait_ge(q_done[q], i + 2)
                            dve.tensor_tensor(prod[:, q % 2, :], gath[:, 2 * q:2 * q + 2, :].rearrange("p k d -> p (k d)"),
                                              ps[q][:, :], ALU.mult).then_inc(prod_done[q], 1)
                            dve.wait_ge(prod_done[q], i + 2)
                            c(dve.tensor_reduce(part[:, q % 2, :], prod[:, q % 2, :].rearrange("p (s d) -> p s d", d=DK),
                                                AX, ALU.add))
                            sc = scores[:, ds(b * EB + 2 * q, 2), :]
                            ins = dve.tensor_tensor(sc, sc, part[:, q % 2, :].rearrange("p (k h) -> p k h", k=2), ALU.add)
                        ins.then_inc(e1_end, 1)

                scan_pass(0)
                with dve.If(n > 1):
                    with dve.Fori(1, n) as r:
                        scan_pass(r)
                dve.wait_ge(e1_end, n * NB)

                c = Chain(dve, vs)
                for t in range(ETY):
                    c(dve.tensor_scalar(rel[:, :], typf[:, :], float(t), BIG, ALU.not_equal, ALU.mult))
                    for h in range(H):
                        ins = dve.tensor_tensor_reduce(sty[t][:, :, h], scores[:, :, h], rel[:, :], 1.0, BIG, ALU.add,
                                                       ALU.max, smax[:, t * H + h:t * H + h + 1])
                    c(ins)
                dve.sem_inc(s_max, 1)
                dve.wait_ge(s_gmax, 1)
                dve.tensor_scalar(smax[:, :], gmax[:, :], -1.0, None, ALU.mult).then_inc(s_neg, 1)
                dve.wait_ge(s_gsum, 1)
                c(dve.tensor_scalar(gsum[:, :], gsum[:, :], 1.0e-30, None, ALU.max))
                c(dve.reciprocal(ssum[:, :], gsum[:, :]))

                def inverse(t):
                    return ssum[:, t * H:(t + 1) * H].rearrange("p (a h) -> p a h", a=1).to_broadcast([P, ET, H])

                c(dve.tensor_tensor(scores, sty[0], inverse(0), ALU.mult))
                for t in range(1, ETY):
                    c(dve.tensor_tensor(sty[t], sty[t], inverse(t), ALU.mult))
                    c(dve.tensor_tensor(scores, scores, sty[t], ALU.add))
                c(dve.memset(off[:, :], 0.0))
                dve.sem_inc(s_alpha, 1)

                c = Chain(dve, vm)
                windows(e2_base)
                dve.wait_ge(e2_base, 1)
                c.straight()
                again_start = c.start

                def messages(i, b, g):
                    dve.wait_ge(agg_ps[g], i + 1)
                    settle(dve)
                    dve.tensor_tensor(onehot[g], iota_w[:, :].rearrange("p (a w) -> p a w", a=1).to_broadcast([P, EG, WIN]),
                                      rel[:, ds(b * EB + g * EG, EG)].rearrange("p (k w) -> p k w", w=1)
                                      .to_broadcast([P, EG, WIN]), ALU.is_equal).then_inc(oh2[g], 1)
                    for k in range(EG):
                        dve.wait_ge(e2_got[EG * g + k], 16 * (i + 1))
                    settle(dve)
                    dve.tensor_tensor(msgs[g].rearrange("p k (h d) -> p k h d", d=DK),
                                      gath2[:, EG * g:EG * (g + 1), :].rearrange("p k (h d) -> p k h d", d=DK),
                                      scores[:, ds(b * EB + EG * g, EG), :].rearrange("p k (h d) -> p k h d", d=1)
                                      .to_broadcast([P, EG, H, DK]), ALU.mult).then_inc(msg_done[g], 1)

                def add(i, g, at):
                    dve.wait_ge(agg_add[(g - 1) % GB], i + 1 + (g > 0))
                    dve.wait_ge(agg_ps[g], i + 2)
                    settle(dve)
                    win = cols[:, :, ds(at, WIN)]
                    dve.tensor_tensor(win, win, ps[g][:, 0:C * WIN].rearrange("p (c w) -> p c w", c=C), ALU.add
                                      ).then_inc(agg_add[g], 1)

                cs, cd = Chain(dve, vb), Chain(dve, vd)

                def body(b, mix):
                    t0, t1, t2, t3 = (tile_of(b, k) if mix else None for k in range(4))
                    m = cs
                    if mix and not isinstance(b, int):
                        m = cd
                        m.turn(b - 4, 8)
                    at = [dve.value_load(base_i[0:1, ds(b * GB + g, 1)], min_val=0, max_val=NP - WIN) for g in range(GB)]
                    messages(b, b, 0)
                    if t1 is not None:
                        once(dve, m_t, t1 - 1)
                        once(dve, m_exp, t1)
                        dve.scalar_tensor_tensor(qf, ps[3][:, 0:D], 0.0, qexp, ALU.max, ALU.add).then_inc(m_kf, 1)
                    messages(b, b, 1)
                    add(b, 0, at[0])
                    if t1 is not None:
                        once(dve, m_t, t1)
                        t3d = ps[4][:, 0:2 * 132].rearrange("p (c m) -> p c m", c=C)
                        m(dve.tensor_scalar(den.rearrange("p (c h) -> p c h", c=C), t3d[:, :, P:P + 4], EPS_ATTN, None, ALU.add))
                        m(dve.reciprocal(den, den))
                        m(dve.tensor_tensor(tx.rearrange("p (c h d) -> p c h d", c=C, d=DK),
                                            t3d[:, :, 0:P].rearrange("p c (h d) -> p c h d", d=DK),
                                            den.rearrange("p (c h d) -> p c h d", c=C, d=1).to_broadcast([P, C, 4, DK]),
                                            ALU.mult))
                        txa = tx.rearrange("p (a d) -> p a d", a=1)
                        dve.tensor_tensor(txa, txa, rows[:, ds(t1, 1), :], ALU.add).then_inc(m_tx, 1)
                    if t3 is not None:
                        once(dve, m_y, t3)
                        m(dve.tensor_tensor(x2m, ps[7][:, 0:D], vecs["L0_mix_b2"][:, :], ALU.add))
                        xm = x2m.rearrange("p (a d) -> p a d", a=1)
                        once(dve, m_x1k, t3)
                        settle(dve)
                        m(dve.tensor_tensor(xm, xm, rows[:, ds(t3, 1), :], ALU.add))
                    if t1 is not None:
                        once(dve, m_tx, t1)
                        settle(dve)
                        ins = dve.bn_stats(sts[:, 0, :], tx)
                    if t3 is not None:
                        ins = dve.bn_stats(sts[:, 1, :], x2m)
                    if t1 is not None or t3 is not None:
                        m(ins)
                        settle(dve)
                    if t1 is not None:
                        ins = dve.bn_aggr(mvs[:, 0, :], sts[:, 0, :])
                    if t3 is not None:
                        ins = dve.bn_aggr(mvs[:, 1, :], sts[:, 1, :])
                    if t1 is not None or t3 is not None:
                        ins.then_inc(m_var, 1)
                    messages(b, b, 2)
                    add(b, 1, at[1])
                    if t1 is not None or t3 is not None:
                        lo, hi = (0 if t1 is not None else 1), (2 if t3 is not None else 1)
                        once(dve, m_sd, b - 1)
                        m(dve.reciprocal(rss[:, lo:hi], sd[:, lo:hi]))
                    if t1 is not None:
                        dve.scalar_tensor_tensor(tx, tx, mvs[:, 0, 0:1], vecs["L0_mix_ln1_g"][:, :], ALU.subtract, ALU.mult)
                    if t3 is not None:
                        ins = dve.scalar_tensor_tensor(x2m, x2m, mvs[:, 1, 0:1], vecs["L0_mix_ln2_g"][:, :], ALU.subtract,
                                                       ALU.mult)
                        m(ins)
                    elif t1 is not None:
                        m(dve.tensor_copy(den[:, 0:1], den[:, 0:1]))
                    if t1 is not None:
                        once(dve, m_T, b if t2 is not None or t0 is not None else b - 1)
                        once(dve, m_x1k, t1 - 1)
                        dve.scalar_tensor_tensor(x1, tx, rss[:, 0:1], vecs["L0_mix_ln1_b"][:, :], ALU.mult, ALU.add
                                                 ).then_inc(m_x1, 1)
                    if t3 is not None:
                        dve.scalar_tensor_tensor(rows[:, ds(t3, 1), :], x2m.rearrange("p (a d) -> p a d", a=1), rss[:, 1:2],
                                                 vecs["L0_mix_ln2_b"][:, :].rearrange("p (a d) -> p a d", a=1), ALU.mult,
                                                 ALU.add).then_inc(m_fin, 1)
                    if t0 is not None:
                        once(dve, m_exp, t0 - 1)
                        once(dve, m_q, t0)
                        dve.tensor_scalar(qmin, ps[3][:, 0:D], 0.0, None, ALU.min).then_inc(m_min, 1)
                    add(b, 2, at[2])
                    if m is cd:
                        assert m.n == 8, m.n

                bodies(dve, body)

                def again(r):
                    c.base, c.n = again_start + (r - 1) * 4, 0
                    windows(e2_base)
                    dve.wait_ge(e2_base, r + 1)
                    settle(dve)
                    with dve.Fori(0, NB) as b:
                        i = r * NB + b
                        at = [dve.value_load(base_i[0:1, ds(b * GB + g, 1)], min_val=0, max_val=NP - WIN)
                              for g in range(GB)]
                        for g in range(GB):
                            messages(i, b, g)
                        for g in range(GB):
                            add(i, g, at[g])

                with dve.If(n > 1):
                    with dve.Fori(1, n) as r:
                        again(r)
                dve.wait_ge(agg_add[GB - 1], n * NB + 1)
                settle(dve)

        new_stage()
        vc, pc, vf3 = sem("vector_step"), sem("pool_step"), sem("closing_ends")
        s_ffd, s_ffe = sem("ffn_step"), sem("ffn_ends")
        x_in, ga_in, ga_T, ln3_var, ln3_rs, ln4_var, ln4_rs, gb_ok, x3_ok, x3_T, x3_Tc, gate_ok = (pair(n) for n in (
            "x_in", "agg_copied", "agg_turned", "gnn_var", "gnn_rstd", "ffn_var", "ffn_rstd", "sum_done", "xf",
            "xf_turned", "xf_copied", "gate"))
        s_before, s_before0, s_gT, s_gTc, s_gst, s_gin, s_nw = (sem(n) for n in (
            "before_ready", "before_cleared", "gates_turned", "gates_copied", "gates_stored", "gates_in", "gates_negated"))
        h_ps, h_ok, y_ps, y_ok, cnt_ok, out_ok, out_st = (pair(n) for n in (
            "h_ps", "h", "y_ps", "y", "larger_counted", "out", "out_stored"))

        with nc.Block() as block:
            @block.sync
            def _(sp):
                def load(t, n=P):
                    seen(sp, gb_ok, t.at(-2))
                    settle(sp)
                    sp.dma_start(xo[0:n, t.k, :], x_d[ds(t.t * P, n), :]).then_inc(x_in[t.k], 16)

                over(sp, NT, lambda t: load(t, LAST if isinstance(t.t, int) and t.t == NT - 1 else P))
                sp.wait_ge(s_gTc, 1)
                sp.dma_start(w_d, w_t[0:NT, :]).then_inc(s_gst, 16)
                sp.wait_ge(s_gst, 16)
                sp.dma_start(w_b, w_d.rearrange("(r t) n -> r (t n)", r=1).to_broadcast([P, NP])).then_inc(s_gin, 16)

                def store(t):
                    n = LAST if isinstance(t.t, int) and t.t == NT - 1 else P
                    seen(sp, out_ok, t)
                    settle(sp)
                    sp.dma_start(out[ds(t.t * P, n), :],
                                 rows[0:n, ds(t.t, 1), :].rearrange("p a d -> p (a d)")).then_inc(out_st[t.k], 16)

                over(sp, NT, store)
                seen_all(sp, out_st, NT, 16)

            @block.gpsimd
            def _(pool):
                c = Chain(pool, pc)
                pool.memset(before[:, :], 0.5).then_inc(s_before0, 1)
                pool.wait_ge(s_before0, 1)
                pool.affine_select(out=before[:, :], in_=before[:, :], compare_op=ALU.is_ge, fill=-0.5,
                                   base=(NT - 1) * P - 1, pattern=[[-1, (2 * NT - 1) * P]], channel_multiplier=1
                                   ).then_inc(s_before, 1)

                def rsqrt(t, mv, rs, var, done):
                    if t is None:
                        return
                    seen(pool, var, t)
                    settle(pool)
                    pool.tensor_scalar(rs[:, t.k, 1:2], mv[:, t.k, 1:2], EPS_LN, None, ALU.add).then_inc(done[t.k], 1)
                    pool.wait_ge(done[t.k], 2 * t.i + 1)
                    pool.tensor_tensor(rs[:, t.k, 0:1], rs[:, t.k, 1:2], nhalf[:, 0:1], ALU.pow).then_inc(done[t.k], 1)

                def body(t):
                    rsqrt(t.at(-1), mv4, rs4, ln4_var, ln4_rs)
                    rsqrt(t, mv3, rs3, ln3_var, ln3_rs)

                over(pool, NT, body)
                rsqrt(Tile((NT - 1) // 2, 0, NT), mv4, rs4, ln4_var, ln4_rs)

            @block.scalar
            def _(act):
                def take(t):
                    if t is None:
                        return
                    seen(act, ga_T, t.at(-2))
                    settle(act)
                    act.activation(chunks(ga[:, t.k, :]), cols[:, :, ds(t.t * P, P)], ACT.Copy).then_inc(ga_in[t.k], 1)

                def put(t):
                    if t is None:
                        return
                    seen(act, x3_T, t)
                    settle(act)
                    act.activation(cols[:, :, ds(t.t * P, P)], chunks(ps[2 + t.k][:, 0:D]), ACT.Copy).then_inc(x3_Tc[t.k], 1)

                def body(t):
                    take(t.at(1))
                    put(t.at(-2))

                take(Tile(0, 0, NT))
                over(act, NT, body)
                put(Tile((NT - 2) // 2, 1, NT))
                put(Tile((NT - 1) // 2, 0, NT))
                act.wait_ge(s_gT, 1)
                act.activation(w_t[0:NT, :], ps[4][0:NT, 0:P], ACT.Copy).then_inc(s_gTc, 1)
                act.wait_ge(s_gin, 16)
                act.wait_ge(s_nw, 1)
                act.wait_ge(s_gst, 16)

                def ffn(t):
                    seen(act, out_ok, t.at(-2))
                    seen(act, cnt_ok, t.at(-1))
                    settle(act)
                    act.activation(scr_a[:, 0:N], w_b[:, 0:N], ACT.Sign, bias=nw[:, ds(t.t, 1)],
                                   accum_out=rank[:, t.k, 0:1]).then_inc(cnt_ok[t.k], 1)
                    seen(act, y_ps, t.at(-2))
                    seen(act, h_ps, t)
                    for j in range(FJ):
                        ins = act.activation(fh[:, t.k, j * P:(j + 1) * P], ps[2 * t.k + j // 4][:, (j % 4) * P:(j % 4 + 1) * P],
                                             ACT.Gelu_apprx_tanh, bias=fb1[:, j:j + 1])
                    ins.then_inc(h_ok[t.k], 1)

                over(act, NT, ffn)

            @block.tensor
            def _(pe):
                def turn(t, src, event, ready, used, bank):
                    if t is None:
                        return
                    seen(pe, ready, t)
                    seen(pe, used, t.at(-2))
                    settle(pe)
                    for ch in range(C):
                        ins = pe.transpose(ps[bank + t.k][:, ch * P:(ch + 1) * P], src[:, t.k, ch * P:(ch + 1) * P],
                                           ident[:, :])
                    ins.then_inc(event[t.k], 1)

                def body(t):
                    turn(t.at(-2), x3, x3_T, x3_ok, x3_Tc, 2)
                    turn(t, ga, ga_T, ga_in, gb_ok, 0)

                over(pe, NT, body)
                turn(Tile((NT - 2) // 2, 1, NT), x3, x3_T, x3_ok, x3_Tc, 2)
                turn(Tile((NT - 1) // 2, 0, NT), x3, x3_T, x3_ok, x3_Tc, 2)
                seen_all(pe, gate_ok, NT)
                pe.transpose(ps[4][0:NT, 0:P], w_all[:, :], ident[:, :]).then_inc(s_gT, 1)
                seen_all(pe, x3_Tc, NT)
                seen_all(pe, gb_ok, NT)

                def up(t):
                    if t is None:
                        return
                    seen(pe, h_ok, t.at(-2))
                    settle(pe)
                    for j in range(FJ):
                        for ch in range(C):
                            ins = pe.matmul(ps[2 * t.k + j // 4][:, (j % 4) * P:(j % 4 + 1) * P],
                                            fw1[:, ch, j * P:(j + 1) * P], cols[:, ch, ds(t.t * P, P)],
                                            start=(ch == 0), stop=(ch == C - 1))
                    ins.then_inc(h_ps[t.k], 1)

                def ffn(t):
                    up(t.at(1))
                    seen(pe, h_ok, t)
                    seen(pe, out_ok, t.at(-2))
                    for j in range(FJ):
                        ins = pe.matmul(ps[6 + t.k][:, 0:D], fh[:, t.k, j * P:(j + 1) * P], fw2[:, j, :],
                                        start=(j == 0), stop=(j == FJ - 1))
                    ins.then_inc(y_ps[t.k], 1)

                up(Tile(0, 0, NT))
                over(pe, NT, ffn)

            @block.vector
            def _(dve):
                c = Chain(dve, vc)

                def finish(t):
                    if t is None:
                        return
                    seen(dve, x3_T, t.at(-2))
                    dve.wait_ge(ln4_rs[t.k], 2 * t.i + 2)
                    dve.tensor_scalar(x3[:, t.k, :], gb[:, t.k, :], mv4[:, t.k, 0:1], rs4[:, t.k, 0:1], ALU.subtract,
                                      ALU.mult).then_inc(x3_ok[t.k], 1)
                    seen(dve, x3_ok, t)
                    settle(dve)
                    dve.tensor_tensor(rows[:, ds(t.t, 1), :], gb[:, ds(t.k, 1), :], x3[:, ds(t.k, 1), :], ALU.add)
                    c(dve.tensor_tensor_reduce(xo2, x3[:, t.k, :], wr[:, :], 1.0, 0.0, ALU.mult, ALU.add,
                                               gate[:, t.k, 0:1]))
                    settle(dve)
                    dve.tensor_tensor(w_all[:, ds(t.t, 1)], gate[:, t.k, 0:1], br[:, :], ALU.add).then_inc(gate_ok[t.k], 1)

                def combine(t):
                    if t is None:
                        return
                    dve.wait_ge(ln3_rs[t.k], 2 * t.i + 2)
                    g = gb[:, t.k, :]
                    c(dve.scalar_tensor_tensor(g, ps[t.k][:, 0:D], mv3[:, t.k, 0:1], vecs["L0_gnn_ln_g"][:, :],
                                               ALU.subtract, ALU.mult))
                    c(dve.scalar_tensor_tensor(g, g, rs3[:, t.k, 0:1], vecs["L0_gnn_ln_b"][:, :], ALU.mult, ALU.add))
                    seen(dve, x_in, t, 16)
                    c(dve.tensor_tensor(g, g, xo[:, t.k, :], ALU.add))
                    settle(dve)
                    ga3 = gb[:, ds(t.k, 1), :]
                    dve.tensor_tensor(ga3, ga3, rows[:, ds(t.t, 1), :], ALU.add).then_inc(gb_ok[t.k], 1)
                    seen(dve, gb_ok, t)
                    settle(dve)
                    c(dve.bn_stats(st4[:, t.k, :], g))
                    settle(dve)
                    dve.bn_aggr(mv4[:, t.k, :], st4[:, t.k, :]).then_inc(ln4_var[t.k], 1)

                cd3, cs3 = Chain(dve, vc), Chain(dve, vf3)

                def body(t):
                    nonlocal c
                    dynamic = not isinstance(t.t, int)
                    c = cd3 if dynamic else cs3
                    if dynamic:
                        c.turn(t.t - 2, 6)
                    finish(t.at(-2))
                    combine(t.at(-1))
                    seen(dve, ga_T, t)
                    settle(dve)
                    c(dve.bn_stats(st3[:, t.k, :], ps[t.k][:, 0:D]))
                    settle(dve)
                    dve.bn_aggr(mv3[:, t.k, :], st3[:, t.k, :]).then_inc(ln3_var[t.k], 1)
                    assert not dynamic or c.n == 6, c.n

                over(dve, NT, body)
                finish(Tile((NT - 2) // 2, 1, NT))
                combine(Tile((NT - 1) // 2, 0, NT))
                finish(Tile((NT - 1) // 2, 0, NT))
                seen_all(dve, gate_ok, NT)
                dve.tensor_scalar(nw, w_all[:, :], -1.0, None, ALU.mult).then_inc(s_nw, 1)
                seen_all(dve, x3_T, NT)
                dve.wait_ge(s_gin, 16)
                dve.wait_ge(s_before, 1)
                cf, ce = Chain(dve, s_ffd), Chain(dve, s_ffe)

                def ffn(t):
                    dynamic = not isinstance(t.t, int)
                    c = cf if dynamic else ce
                    if dynamic:
                        c.turn(t.t - 2, 4)
                    w_i = w_all[:, ds(t.t, 1)]
                    c(dve.scalar_tensor_tensor(scr_d[:, 0:N], w_b[:, 0:N], w_i, before[:, ds((NT - 1 - t.t) * P, N)],
                                               ALU.is_equal, ALU.mult, accum_out=rank[:, t.k, 1:2]))
                    seen(dve, cnt_ok, t)
                    settle(dve)
                    c(dve.scalar_tensor_tensor(rank[:, t.k, 1:2], rank[:, t.k, 0:1], 0.5, rank[:, t.k, 1:2], ALU.mult, ALU.add))
                    settle(dve)
                    c(dve.scalar_tensor_tensor(sel[:, ds(t.t, 1)], rank[:, t.k, 1:2], KSEL - 0.5 * N, w_i, ALU.is_lt,
                                               ALU.mult))
                    seen(dve, y_ps, t)
                    c(dve.tensor_tensor(yb[:, t.k, :], ps[6 + t.k][:, 0:D], vecs["L0_ffn_b2"][:, :], ALU.add))
                    settle(dve)
                    dve.scalar_tensor_tensor(rows[:, ds(t.t, 1), :], yb[:, ds(t.k, 1), :], sel[:, ds(t.t, 1)],
                                             rows[:, ds(t.t, 1), :], ALU.mult, ALU.add).then_inc(out_ok[t.k], 1)
                    assert not dynamic or c.n == 4, c.n

                over(dve, NT, ffn)

_INS = ["x", "src", "dst", "edge_type_3", "node_type_6", "L0_gnn_Wk", "L0_gnn_bk", "L0_gnn_Wq", "L0_gnn_bq",
        "L0_gnn_Wv", "L0_gnn_bv", "L0_gnn_relation_pri", "L0_gnn_Wa", "L0_gnn_Wm", "L0_gnn_ln_g", "L0_gnn_ln_b",
        "L0_mix_ln1_g", "L0_mix_ln1_b", "L0_mix_b2", "L0_mix_ln2_g", "L0_mix_ln2_b", "L0_ffn_wr", "L0_ffn_br",
        "L0_ffn_w1", "L0_ffn_w2", "L0_ffn_b2"]


def kernel(**inputs):
    import concourse.bacc as _bacc
    from concourse.bass_utils import run_bass_kernel_spmd as _run

    nc = _bacc.Bacc("TRN2", target_bir_lowering=False, num_devices=1)
    lay = {name: np.ascontiguousarray(inputs[name]) for name in _INS}
    lay["mix_WqkvT"] = np.ascontiguousarray(np.asarray(inputs["L0_mix_Wqkv"]).T)
    lay["mix_W1T"] = np.ascontiguousarray(np.asarray(inputs["L0_mix_W1"]).T)
    lay["mix_W2T"] = np.ascontiguousarray(np.asarray(inputs["L0_mix_W2"]).T)
    lay["mix_b1_cols"] = np.ascontiguousarray(np.asarray(inputs["L0_mix_b1"]).reshape(-1, P).T)
    lay["ffn_b1_cols"] = np.ascontiguousarray(np.asarray(inputs["L0_ffn_b1"]).reshape(-1, P).T)
    arrays, args = {}, {}
    for name, v in lay.items():
        arrays[f"in_{name}"] = v
        args[name] = nc.dram_tensor(f"in_{name}", v.shape, mybir.dt.from_np(v.dtype), kind="ExternalInput").ap()
    out = nc.dram_tensor("out_0", (N, D), F32, kind="ExternalOutput").ap()
    build(nc, args, out)
    r = _run(nc, [arrays], core_ids=[0])
    return r.results[0]["out_0"]
```

```python
from contextlib import ExitStack

import numpy as np

import concourse.bass as bass
import concourse.mybir as mybir

F32 = mybir.dt.float32
I32 = mybir.dt.int32
ALU = mybir.AluOpType
ACT = mybir.ActivationFunctionType
AX = mybir.AxisListType.X
RMAX = bass.bass_isa.ReduceOp.max
RADD = bass.bass_isa.ReduceOp.add
ds = bass.ds

P = 128
N, D = 3125, 256
C = D // P
H, DK = 8, 32
NTY, ETY = 6, 3
NT = -(-N // P)
NP = NT * P
LAST = N - (NT - 1) * P
NS = (N + NTY * (P - 1)) // P
TW = (2 * ETY + 2) * D
QC = 2 * ETY * D
E = 50000
EG = 4
EV = 2
GB = 3
EB = EG * GB
NB = -(-E // (P * EB))
ET = NB * EB
NG = ET // EG
WIN = 64
NPASS = -(-N // WIN)
ERAW = -(-ET // P)
F = 4 * D
FJ = F // P
KSEL = max(1, int(0.5 * N)) - 1
EPS_LN, EPS_ATTN = 1e-5, 1e-6
BIG = -3.0e38
BITS, ROUNDS = 4, 8


def build(nc, a, out):
    def scratch(name, shape, dt=F32):
        return nc.dram_tensor(name, shape, dt, kind="Internal").ap()

    tab_d = scratch("table_scratch", (NP + NS * P, TW))
    xn_d = scratch("xn_scratch", (NP, D))
    v_d = scratch("edge_v_scratch", (NG, P, EV * D))
    dst_d = scratch("dst_scratch", (ET, P), I32)
    perm_d = scratch("perm_scratch", (NS * P, 1), I32)
    x_d = a["x"]

    with ExitStack() as ctx:
        def sb(name, shape, dt=F32):
            return ctx.enter_context(nc.sbuf_tensor(name, shape, dt))

        class Arena:

            def __init__(self, name, size):
                self.t, self.size, self.at = sb(name, [P, size]), size, 0

            def reset(self):
                self.at = 0

            def take(self, *shape):
                n = int(np.prod(shape))
                v = self.t[:, self.at:self.at + n]
                self.at += n
                assert self.at <= self.size, self.at
                if len(shape) == 2:
                    return v.rearrange("p (a b) -> p a b", b=shape[1])
                if len(shape) == 3:
                    return v.rearrange("p (a b c) -> p a b c", b=shape[1], c=shape[2])
                return v

        rows = sb("rows", [P, NT, D])
        cols = sb("cols", [P, C, NP])
        big = Arena("big", ETY * ET * H)
        work = Arena("work", 11072)

        ident = sb("ident", [P, P])
        ones = sb("ones", [P, P])
        wqkvT = sb("wqkvT", [P, C, 3 * D])
        w1T = sb("w1T", [P, C, D])
        w2T = sb("w2T", [P, C, D])
        vec_names = ["L0_gnn_ln_g", "L0_gnn_ln_b", "L0_mix_ln1_g", "L0_mix_ln1_b", "L0_mix_ln2_g",
                     "L0_mix_ln2_b", "L0_mix_b2", "L0_ffn_b2"]
        vecs = {n: sb("v_" + n, [P, D]) for n in vec_names}
        wr = sb("wr", [P, D])
        br = sb("br", [P, 1])
        b1c = sb("b1c", [P, C])
        fb1 = sb("fb1", [P, FJ])
        pri = sb("pri", [P, ETY * H])
        bd_a = sb("bd_a", [P, ETY, P])
        bd_m = sb("bd_m", [P, ETY, P])
        iota_p = sb("iota_p", [P, 1])
        iota_w = sb("iota_w", [P, WIN])
        nhalf = sb("nhalf", [P, NT])
        idx_1 = sb("idx_1", [P, ET], I32)
        idx_v = sb("idx_v", [P, ET], I32)
        dstf = sb("dstf", [P, ET])
        typf = sb("typf", [P, ET])
        rel = sb("rel", [P, ET])
        base0 = sb("base0", [P, NG])
        base_f = sb("base_f", [P, NG])
        base_n = sb("base_n", [P, NG])
        base_i = sb("base_i", [P, NB, 4], I32)
        bad = sb("bad", [P, 4])
        good = sb("good", [P, 1])
        eps = sb("eps", [P, 1])
        off = sb("off", [P, 1])
        npass_i = sb("npass_i", [P, 1], I32)
        kvd = sb("kvd", [P, C, 132])
        w_all = sb("w_all", [P, NT])
        sel = sb("sel", [P, NT])
        idxb = sb("idxb", [P, GB, EG], I32)

        wall = big.take(NTY, C, 3 * D)
        big.reset()
        sty = [big.take(ET, H) for _ in range(ETY)]
        big.reset()
        fw1 = big.take(C, F)
        fw2 = big.take(FJ, D)
        scores = sb("scores", [P, ET * H])[:, :].rearrange("p (e h) -> p e h", h=H)

        raw = work.take(3 * ERAW * P).bitcast(I32).rearrange("p (a b c) -> p a b c", b=ERAW, c=P)
        rawf = work.take(3, ERAW * P)
        valid = work.take(ET)
        iota_wi = work.take(WIN).bitcast(I32)
        iota_pi = work.take(1).bitcast(I32)
        perm_i = work.take(P).bitcast(I32)
        perm_f = work.take(P)
        hmask = work.take(132)
        tri = work.take(P)
        slot_i = work.take(NS).bitcast(I32)
        slot_j = work.take(NS)
        typ_i = work.take(P).bitcast(I32)
        typ_t = work.take(P)
        is_ty = work.take(NTY, NT)
        before_ty = work.take(NTY, NT)
        total_ty = work.take(NTY, NT)
        scan = [work.take(NTY, NT) for _ in range(2)]
        tiles_i = work.take(NTY).bitcast(I32)
        tiles_f = work.take(NTY)
        start_f = work.take(NTY + 1)
        pos_f = work.take(NT)
        node_i = work.take(NT).bitcast(I32)
        stats = work.take(NT, 6)
        mv_all = work.take(NT, 2)
        var_all = work.take(NT)
        rstd_all = work.take(NT)
        xs = work.take(2, D)
        xT_s = work.take(2, D)
        kmin = work.take(2, D)
        kexp = work.take(2, D)
        kf = work.take(2, D)
        vf = [work.take(C, 129) for _ in range(2)]
        zero = work.take(2 * 132)
        work.reset()
        xg = work.take(2, D)
        xgT = work.take(2, D)
        wcur = [work.take(C, 2 * D) for _ in range(2)]
        kvT = work.take(2, 2 * D)
        tab = work.take(2, TW)
        q_bias = work.take(NTY, D)
        work.reset()
        smax, gmax, nmax, ssum, gsum = (sb(n, [P, ETY * H]) for n in ("smax", "gmax", "nmax", "ssum", "gsum"))
        pos_i = sb("pos_i", [P, NT], I32)
        slot_ty = sb("slot_ty", [P, NS])
        slot_tyi = sb("slot_tyi", [P, NS], I32)
        from_i = sb("from_i", [P, NS], I32)
        to_i = sb("to_i", [P, NS], I32)
        idx_from = sb("idx_from", [P, 2], I32)
        idx_to = sb("idx_to", [P, 2], I32)
        kv_bias = sb("kv_bias", [P, NTY, 2 * C])
        gathp = work.take(GB, EV * 2 * D).rearrange("p g (k s) -> p g k s", k=EV)
        gathk = work.take(GB, (EG - EV) * D).rearrange("p g (k s) -> p g k s", s=D)
        qwin = work.take(GB, D)
        dst_b = work.take(GB, EG * P).bitcast(I32)
        dist = work.take(GB, EG * P)
        ohT = work.take(GB, EG * P)
        prod = work.take(2, 2 * D)
        part = work.take(2, 2 * H)
        work.reset()
        gath2 = work.take(EB, D)
        onehot = [work.take(EG, WIN) for _ in range(GB)]
        msgs = [work.take(EG, D) for _ in range(GB)]
        qmin = work.take(D)
        qexp = work.take(D)
        qf = work.take(D)
        tx = work.take(D)
        x1 = work.take(D)
        hT = work.take(D)
        x2m = work.take(D)
        xa = work.take(D)
        xT2 = work.take(2 * D)
        den = work.take(H)
        sts, mvs, sd, rss = work.take(2, 6), work.take(2, 2), work.take(2), work.take(2)
        work.reset()
        ga = work.take(2, D)
        gb = work.take(2, D)
        xo = work.take(2, D)
        x3 = work.take(2, D)
        st3, mv3, rs3 = work.take(2, 6), work.take(2, 2), work.take(2, 2)
        st4, mv4, rs4 = work.take(2, 6), work.take(2, 2), work.take(2, 2)
        gate = work.take(2, 2)
        xo2 = work.take(D)
        fh = work.take(2, F)
        tri3 = work.take(P)
        limit, room = work.take(1), work.take(1)
        digits_i, cand_i, bits_i = (work.take(15).bitcast(I32) for _ in range(3))
        flip_i, top_i, digit_i, theta_i = (work.take(1).bitcast(I32) for _ in range(4))
        reach = work.take(15, NT)
        counts, enough = work.take(15), work.take(15)
        marks = work.take(2, NT)
        ahead = work.take(NT)
        run = [work.take(NT) for _ in range(2)]

        ps = [ctx.enter_context(nc.psum_tensor(f"ps{i}", [P, 512], F32)) for i in range(8)]

        stage_sems, stage_no, settled = [], [0], [None]

        def sem(name):
            stage_sems.append(nc.alloc_semaphore(name=f"s{stage_no[0]}_{name}"))
            return stage_sems[-1]

        def pair(name):
            return [sem(f"{name}0"), sem(f"{name}1")]

        def new_stage():
            if stage_sems:
                nc.clear_and_free_semaphores(stage_sems)
                nc.all_engine_barrier()
            stage_sems.clear()
            stage_no[0] += 1
            settled[0] = sem("settled")

        def settle(eng):
            eng.sem_inc(settled[0], 1)

        class Tile:

            def __init__(self, i, k, n):
                self.i, self.k, self.n, self.t = i, k, n, 2 * i + k

            def at(self, d):
                j = self.k + d
                v = Tile(self.i + j // 2, j % 2, self.n)
                return None if isinstance(v.t, int) and not 0 <= v.t < self.n else v

        def over(eng, n, body, first=1, more=0, ahead=1):
            for t in range(2 * first):
                body(Tile(t // 2, t % 2, n))
            end = (n - ahead) // 2
            with eng.Fori(first, end) as i:
                body(Tile(i, 0, n))
                body(Tile(i, 1, n))
            for t in range(2 * end, n + more):
                body(Tile(t // 2, t % 2, n))

        def seen(eng, event, tile, unit=1):
            if tile is not None:
                eng.wait_ge(event[tile.k], unit * (tile.i + 1))

        def seen_all(eng, event, n, unit=1):
            seen(eng, event, Tile((n - 1) // 2, (n - 1) % 2, n), unit)
            seen(eng, event, Tile((n - 2) // 2, (n - 2) % 2, n), unit)

        class Chain:

            def __init__(self, eng, s):
                self.eng, self.s, self.base, self.n, self.start = eng, s, 0, 0, 0

            def __call__(self, ins):
                self.start_step(ins)
                self.due()

            def start_step(self, ins):
                ins.then_inc(self.s, 1)
                self.n += 1

            def due(self):
                self.eng.wait_ge(self.s, self.base + self.n)

            def turn(self, t, per):
                self.base, self.n = self.start + t * per, 0

            def straight(self):
                self.start = self.base + self.n
                self.base, self.n = self.start, 0

        def chunks(v):
            return v.rearrange("p (c n) -> p c n", c=C)

        def grouped(v):
            return v.rearrange("p (g k) -> p g k", k=EG)

        def relative(bases):
            return nc.vector.tensor_tensor(grouped(rel[:, :]), grouped(dstf[:, :]),
                                           bases[:, :].rearrange("p (g k) -> p g k", k=1).to_broadcast([P, NG, EG]),
                                           ALU.subtract)

        new_stage()
        vc, pc = sem("vector_step"), sem("pool_step")
        s_const, s_clear, s_const2 = sem("constants"), sem("cleared"), sem("masks")
        s_edges, s_types, s_x, s_w, s_bias, s_bd, s_vec = (sem(n) for n in (
            "edges_in", "types_in", "x_in", "weights_in", "bias_in", "blocks_in", "vectors_in"))
        s_xc = [sem(f"x_in{j}") for j in range(5)]
        s_dst, s_pinit, s_scat, s_pback, s_xnst = (sem(n) for n in (
            "dst_stored", "slots_cleared", "slots_scattered", "slots_back", "xn_stored"))
        s_tyf, s_tyT, s_isty, s_tysum, s_pos = (sem(n) for n in (
            "types_float", "types_turned", "types_marked", "types_summed", "slots_known"))
        s_rawf, s_eT, s_edge, s_bb, s_bad, s_badall = (sem(n) for n in (
            "edges_float", "edges_turned", "edges_ready", "bases_spread", "bad_marked", "bad_reduced"))
        s_permf, s_permT, s_perm = sem("slots_float"), sem("slots_turned"), sem("slots_ready")
        s_var, s_rstd = sem("variances"), sem("rstds")
        s_zero, s_closed, s_kvd, s_qb = sem("zeroed"), sem("state_summed"), sem("state_ready"), sem("q_bias_in")
        xn_done, xs_done, T_ps, xT_done, cols_done, k_ps, v_done, min_done, exp_done, kf_done, acc_done = (
            pair(n) for n in ("xn", "xs", "xT_ps", "xT", "cols", "kv_ps", "v", "kmin", "kexp", "kf", "acc"))
        g_in, g_T, g_Tc, g_q, g_w, g_qc, g_kvT, g_kvTc, g_tab, g_ktc, g_vtc, g_out, g_ix, g_iy = (
            pair(n) for n in ("g_rows", "g_T", "g_Tc", "g_q", "g_weights", "g_qc", "g_kvT", "g_kvTc", "g_tab", "g_ktc",
                              "g_vtc", "g_stored", "g_index", "g_index_out"))

        with nc.Block() as block:
            @block.sync
            def _(sp):
                sp.wait_ge(s_clear, 1)
                sp.dma_start(typ_i[0:NT - 1, :], a["node_type_6"][0:(NT - 1) * P].rearrange("(r c) -> r c", c=P)
                             ).then_inc(s_types, 16)
                sp.dma_start(typ_i[NT - 1:NT, 0:LAST], a["node_type_6"][(NT - 1) * P:N].rearrange("(r c) -> r c", r=1)
                             ).then_inc(s_types, 16)
                for j in range(5):
                    n = 5 if j < 4 else 4
                    sp.dma_start(rows[:, 5 * j:5 * j + n, :],
                                 x_d[5 * j * P:(5 * j + n) * P, :].rearrange("(t p) d -> p t d", p=P)).then_inc(s_xc[j], 16)
                sp.dma_start(rows[0:LAST, NT - 1, :], x_d[(NT - 1) * P:N, :]).then_inc(s_x, 16)
                full, per = (ERAW - 1) * P * P, ERAW - 1
                rest = (E - full) // P
                tail = E - full - rest * P
                for j, name in enumerate(("src", "dst", "edge_type_3")):
                    flat = a[name]
                    sp.dma_start(raw[:, j, 0:per, :], flat[0:full].rearrange("(b r c) -> r b c", r=P, c=P)
                                 ).then_inc(s_edges, 16)
                    sp.dma_start(raw[0:rest, j, per, :], flat[full:full + rest * P].rearrange("(r c) -> r c", c=P)
                                 ).then_inc(s_edges, 16)
                    sp.dma_start(raw[rest:rest + 1, j, per, 0:tail],
                                 flat[full + rest * P:E].rearrange("(r c) -> r c", r=1)).then_inc(s_edges, 16)
                sp.wait_ge(s_const2, 1)
                sp.dma_start(perm_d.rearrange("(j p) o -> j (p o)", p=P), perm_i[0:NS, :]).then_inc(s_pinit, 16)
                sp.dma_start(wqkvT[:, :, :], a["mix_WqkvT"].rearrange("(c p) o -> p c o", p=P)).then_inc(s_vec, 16)
                for n, name in enumerate(("L0_gnn_Wk", "L0_gnn_Wv", "L0_gnn_Wq")):
                    sp.dma_start(wall[:, :, :, n * D:(n + 1) * D].rearrange("p t c o -> p (t c) o"),
                                 a[name].rearrange("t (c p) o -> p (t c) o", p=P)).then_inc(s_w, 16)
                for n, name in enumerate(("gnn_bk_cols", "gnn_bv_cols")):
                    sp.dma_start(kv_bias[:, :, n * C:(n + 1) * C], a[name]).then_inc(s_bias, 16)
                for m, name in ((bd_a, "L0_gnn_Wa"), (bd_m, "L0_gnn_Wm")):
                    for g in range(P // DK):
                        sp.dma_start(m[g * DK:(g + 1) * DK, :, g * DK:(g + 1) * DK],
                                     a[name].rearrange("t d k -> d t k")).then_inc(s_bd, 16)

                def spread(dst, src, n):
                    sp.dma_start(dst, src.to_broadcast([P, n])).then_inc(s_vec, 16)

                spread(pri[:, :], a["L0_gnn_relation_pri"].rearrange("(r t) h -> r (t h)", r=1), ETY * H)
                for n in vec_names:
                    spread(vecs[n][:, :], a[n].rearrange("(r d) -> r d", r=1), D)
                spread(wr[:, :], a["L0_ffn_wr"].rearrange("(r d) o -> r (d o)", r=1), D)
                spread(br[:, :], a["L0_ffn_br"].rearrange("(r d) -> r d", r=1), 1)
                sp.dma_start(b1c[:, :], a["mix_b1_cols"]).then_inc(s_vec, 16)
                sp.dma_start(fb1[:, :], a["ffn_b1_cols"]).then_inc(s_vec, 16)
                sp.dma_start(w1T[:, :, :], a["mix_W1T"].rearrange("(c p) o -> p c o", p=P)).then_inc(s_vec, 16)
                sp.dma_start(w2T[:, :, :], a["mix_W2T"].rearrange("(c p) o -> p c o", p=P)).then_inc(s_vec, 16)
                sp.wait_ge(s_edges, 16 * 9)
                sp.dma_start(dst_d[0:per * P, :].rearrange("(b r) c -> r b c", r=P), raw[:, 1, 0:per, :]).then_inc(s_dst, 16)
                sp.dma_start(dst_d[per * P:ET, :], raw[0:ET - per * P, 1, per, :]).then_inc(s_dst, 16)
                for j in range(5):
                    last = 5 * j + 4
                    sp.wait_ge(xn_done[last % 2], last // 2 + 1)
                    sp.wait_ge(xn_done[1 - last % 2], (last - 1) // 2 + 1)
                    sp.dma_start(xn_d[5 * j * P:(5 * j + 5) * P, :].rearrange("(t p) d -> p t d", p=P),
                                 rows[:, 5 * j:5 * j + 5, :]).then_inc(s_xnst, 16)
                sp.dma_start(tab_d[N:NP, QC:QC + D], rows[LAST:P, NT - 1, :]).then_inc(s_xnst, 16)
                sp.wait_ge(s_scat, 16 * NT)
                sp.dma_start(perm_i[0:NS, :], perm_d.rearrange("(j p) o -> j (p o)", p=P)).then_inc(s_pback, 16)
                sp.wait_ge(s_perm, 1)
                seen_all(sp, acc_done, NT)
                sp.dma_start(q_bias.rearrange("p t d -> p (t d)"),
                             a["L0_gnn_bq"].rearrange("(r t) d -> r (t d)", r=1).to_broadcast([P, NTY * D])).then_inc(s_qb, 16)
                sp.wait_ge(s_qb, 16)
                sp.wait_ge(s_dst, 32)
                sp.wait_ge(s_xnst, 16 * 6)

            @block.gpsimd
            def _(pool):
                c = Chain(pool, pc)
                pool.memset(raw[:, 0:2, ERAW - 1, :], 0)
                pool.memset(raw[:, 2, ERAW - 1, :], ETY)
                pool.memset(typ_i[:, :], NTY)
                pool.memset(rows[:, NT - 1, :], 0.0).then_inc(s_clear, 1)
                pool.memset(bd_a[:, :, :], 0.0)
                pool.memset(bd_m[:, :, :], 0.0)
                pool.memset(ones[:, :], 1.0)
                pool.memset(nhalf[:, :], -0.5)
                c(pool.memset(ident[:, :], 0.0))
                c(pool.affine_select(out=ident[:, :], in_=ident[:, :], compare_op=ALU.not_equal, fill=1.0, base=0,
                                     pattern=[[-1, P]], channel_multiplier=1))
                c(pool.memset(tri, 1.0))
                c(pool.affine_select(out=tri, in_=tri, compare_op=ALU.is_ge, fill=0.0, base=-1,
                                     pattern=[[1, P]], channel_multiplier=-1))
                c(pool.iota(iota_pi, pattern=[[0, 1]], base=0, channel_multiplier=1))
                c(pool.iota(slot_i, pattern=[[1, NS]], base=0, channel_multiplier=0))
                c(pool.iota(node_i, pattern=[[P, NT]], base=0, channel_multiplier=1))
                pool.tensor_copy(slot_j, slot_i)
                pool.tensor_copy(iota_p[:, :], iota_pi).then_inc(s_const, 1)
                pool.iota(perm_i, pattern=[[1, P]], base=NP, channel_multiplier=P).then_inc(s_const2, 1)
                c(pool.memset(valid, 1.0))
                c(pool.affine_select(out=valid, in_=valid, compare_op=ALU.is_ge, fill=0.0, base=E - 1,
                                     pattern=[[-P, ET]], channel_multiplier=-1))
                c(pool.memset(hmask, 1.0))
                for v, pat in ((hmask[:, 0:P].rearrange("p (g m) -> p g m", m=DK), [[-DK, 4], [0, DK]]),
                               (hmask[:, P:P + 4], [[-DK, 4]])):
                    c(pool.affine_select(out=v, in_=v, compare_op=ALU.is_ge, fill=0.0, base=0, pattern=pat,
                                         channel_multiplier=1))
                    c(pool.affine_select(out=v, in_=v, compare_op=ALU.is_ge, fill=0.0, base=DK - 1,
                                         pattern=[[-q[0], q[1]] for q in pat], channel_multiplier=-1))
                c(pool.iota(iota_wi, pattern=[[1, WIN]], base=0, channel_multiplier=0))
                pool.tensor_copy(iota_w[:, :], iota_wi).then_inc(s_const2, 1)

                pool.wait_ge(s_pos, 1)
                pool.wait_ge(s_pinit, 16)
                for t in range(NT):
                    n = P if t < NT - 1 else LAST
                    pool.indirect_dma_start(perm_d[:, :], bass.IndirectOffsetOnAxis(ap=pos_i[0:n, t:t + 1], axis=0),
                                            node_i[0:n, t:t + 1], None).then_inc(s_scat, 16)
                    if t == 1:
                        pool.wait_ge(s_var, 1)
                        c(pool.tensor_scalar(var_all, mv_all[:, :, 1], EPS_LN, None, ALU.add))
                        pool.tensor_tensor(rstd_all, var_all, nhalf[:, :], ALU.pow).then_inc(s_rstd, 1)
                pool.wait_ge(s_bad, 1)
                pool.partition_all_reduce(bad[:, 1:2], bad[:, 0:1], P, RMAX).then_inc(s_badall, 1)

                pool.wait_ge(s_perm, 1)
                pool.wait_ge(s_xnst, 16 * 6)
                seen_all(pool, acc_done, NT)
                pool.wait_ge(s_kvd, 1)

                def load(t):
                    if t is None:
                        return
                    seen(pool, g_T, t.at(-2))
                    settle(pool)
                    pool.tensor_copy(idx_from[:, t.k:t.k + 1], from_i[:, ds(t.t, 1)]).then_inc(g_ix[t.k], 1)
                    seen(pool, g_ix, t)
                    settle(pool)
                    pool.indirect_dma_start(xg[:, t.k, :], None, xn_d[:, :],
                                            bass.IndirectOffsetOnAxis(ap=idx_from[:, t.k:t.k + 1], axis=0)
                                            ).then_inc(g_in[t.k], 16)

                def store(t):
                    if t is None:
                        return
                    seen(pool, g_ktc, t)
                    seen(pool, g_vtc, t)
                    seen(pool, g_qc, t)
                    seen(pool, g_out, t.at(-2), 16)
                    settle(pool)
                    pool.tensor_copy(idx_to[:, t.k:t.k + 1], to_i[:, ds(t.t, 1)]).then_inc(g_iy[t.k], 1)
                    seen(pool, g_iy, t)
                    settle(pool)
                    pool.indirect_dma_start(tab_d[:, :], bass.IndirectOffsetOnAxis(ap=idx_to[:, t.k:t.k + 1], axis=0),
                                            tab[:, t.k, :], None).then_inc(g_out[t.k], 16)

                def body(t):
                    load(t.at(1))
                    store(t.at(-2))

                load(Tile(0, 0, NS))
                over(pool, NS, body, first=2)
                store(Tile((NS - 2) // 2, 0, NS))
                store(Tile((NS - 1) // 2, 1, NS))
                seen_all(pool, g_out, NS, 16)

            @block.scalar
            def _(act):
                def fixed(t):
                    if t is None:
                        return
                    seen(act, T_ps, t.at(-2))
                    seen(act, xn_done, t)
                    settle(act)
                    act.activation(xs[:, ds(t.k, 1), :], rows[:, ds(t.t, 1), :], ACT.Copy).then_inc(xs_done[t.k], 1)

                def front(t):
                    if t is None:
                        return
                    seen(act, k_ps, t.at(-2))
                    seen(act, T_ps, t)
                    act.activation(xT_s[:, t.k, :], ps[t.k][:, 0:D], ACT.Copy).then_inc(xT_done[t.k], 1)
                    act.activation(cols[:, :, ds(t.t * P, P)], chunks(ps[t.k][:, 0:D]), ACT.Copy).then_inc(cols_done[t.k], 1)

                def body(t):
                    front(t.at(1))
                    fixed(t.at(2))
                    seen(act, acc_done, t.at(-2))
                    seen(act, k_ps, t)
                    act.activation(vf[t.k][:, :, 0:P], chunks(ps[4 + t.k][:, 0:D]), ACT.Copy).then_inc(v_done[t.k], 1)
                    seen(act, kf_done, t.at(-2))
                    seen(act, min_done, t)
                    act.activation(kexp[:, t.k, :], kmin[:, t.k, :], ACT.Exp).then_inc(exp_done[t.k], 1)

                act.wait_ge(s_zero, 1)
                fixed(Tile(0, 0, NT))
                fixed(Tile(0, 1, NT))
                front(Tile(0, 0, NT))
                over(act, NT, body, ahead=2)

                def turn_in(t):
                    if t is None:
                        return
                    seen(act, g_q, t.at(-2))
                    seen(act, g_T, t)
                    act.activation(xgT[:, t.k, :], ps[0][:, 0:D], ACT.Copy).then_inc(g_Tc[t.k], 1)

                def v_out(t):
                    if t is None:
                        return
                    seen(act, g_out, t.at(-2), 16)
                    seen(act, g_tab, t)
                    for ch in range(C):
                        ins = act.activation(
                            tab[:, t.k, 0:QC].rearrange("p (t s d) -> p t s d", s=2, d=D)[:, :, 1, ch * P:(ch + 1) * P],
                            ps[6 + ch][:, 0:ETY * P].rearrange("p (t n) -> p t n", t=ETY), ACT.Copy)
                    ins.then_inc(g_vtc[t.k], 1)

                def weights(t):
                    if t is None:
                        return
                    ty = act.value_load(slot_tyi[0:1, ds(t.t, 1)], min_val=0, max_val=NTY - 1)
                    seen(act, g_kvT, t.at(-2))
                    settle(act)
                    act.activation(wcur[t.k], wall[:, ds(ty, 1), :, 0:2 * D].rearrange("p a c o -> p (a c) o"), ACT.Copy
                                   ).then_inc(g_w[t.k], 1)

                def tables(t):
                    weights(t.at(1))
                    turn_in(t.at(1))
                    v_out(t.at(-1))

                seen_all(act, acc_done, NT)
                act.wait_ge(s_kvd, 1)
                act.wait_ge(s_w, 48)
                act.wait_ge(s_perm, 1)
                weights(Tile(0, 0, NS))
                turn_in(Tile(0, 0, NS))
                over(act, NS, tables, first=2)
                v_out(Tile((NS - 1) // 2, 1, NS))

            @block.tensor
            def _(pe):
                pe.wait_ge(s_const, 1)
                pe.wait_ge(s_tyf, 1)
                pe.transpose(ps[7][:, 0:NT], typ_t[0:NT, :], ident[0:NT, 0:NT]).then_inc(s_tyT, 1)
                pe.wait_ge(s_isty, 1)
                flat = is_ty.rearrange("p y t -> p (y t)")
                pe.matmul(ps[7][:, 0:NTY * NT], tri, flat, start=True, stop=True)
                pe.matmul(ps[7][:, 256:256 + NTY * NT], ones[:, :], flat, start=True, stop=True).then_inc(s_tysum, 1)
                pe.wait_ge(s_rawf, 1)
                for j in range(3):
                    for b in range(ERAW):
                        r = min(P, ET - b * P)
                        ins = pe.transpose(ps[j][:, b * P:b * P + r], rawf[0:r, j, b * P:(b + 1) * P], ident[0:r, 0:r])
                ins.then_inc(s_eT, 1)
                pe.wait_ge(s_edge, 1)
                pe.matmul(ps[3][:, 0:NG], ones[0:1, :], dstf[0:1, :].rearrange("p (g k) -> p g k", k=EG)[:, :, 0],
                          start=True, stop=True).then_inc(s_bb, 1)
                pe.wait_ge(s_bad, 1)
                pe.wait_ge(s_zero, 1)
                pe.wait_ge(s_vec, 16 * (1 + 1 + len(vec_names) + 6))
                pe.matmul(ps[6][:, 0:2 * 129], zero[:, 0:P], zero[:, 0:2 * 129], start=True, stop=False)

                def front(t):
                    if t is None:
                        return
                    seen(pe, xs_done, t)
                    seen(pe, cols_done, t.at(-2))
                    for ch in range(C):
                        ins = pe.transpose(ps[t.k][:, ch * P:(ch + 1) * P], xs[:, t.k, ch * P:(ch + 1) * P], ident[:, :])
                    ins.then_inc(T_ps[t.k], 1)

                def back(t, n=P):
                    if t is None:
                        return
                    seen(pe, kf_done, t)
                    seen(pe, v_done, t)
                    for ch in range(C):
                        ins = pe.matmul(ps[6][:, ch * 129:(ch + 1) * 129], kf[0:n, t.k, ch * P:(ch + 1) * P],
                                        vf[t.k][0:n, ch, :], start=False, stop=False, skip_group_check=True)
                    ins.then_inc(acc_done[t.k], 1)

                def body(t):
                    front(t.at(1))
                    back(t.at(-2))
                    seen(pe, xT_done, t)
                    seen(pe, kf_done, t.at(-2))
                    seen(pe, v_done, t.at(-2))
                    for j in range(2):
                        for ch in range(C):
                            ins = pe.matmul(ps[2 + 2 * j + t.k][:, 0:D], xT_s[:, t.k, ch * P:(ch + 1) * P],
                                            wqkvT[:, ch, (1 + j) * D:(2 + j) * D], start=(ch == 0), stop=(ch == C - 1))
                    ins.then_inc(k_ps[t.k], 1)

                front(Tile(0, 0, NT))
                over(pe, NT, body)
                back(Tile((NT - 2) // 2, 1, NT))
                back(Tile((NT - 1) // 2, 0, NT), LAST)
                pe.matmul(ps[6][:, 0:2 * 129], zero[:, 0:P], zero[:, 0:2 * 129], start=False, stop=True).then_inc(s_closed, 1)

                pe.wait_ge(s_permf, 1)
                pe.transpose(ps[7][:, 0:NS], perm_f[0:NS, :], ident[0:NS, 0:NS]).then_inc(s_permT, 1)
                pe.wait_ge(s_perm, 1)
                pe.wait_ge(s_kvd, 1)
                pe.wait_ge(s_w, 48)
                pe.wait_ge(s_bd, 16 * 8)

                def turn_in(t):
                    if t is None:
                        return
                    seen(pe, g_Tc, t.at(-1))
                    seen(pe, g_in, t, 16)
                    settle(pe)
                    for ch in range(C):
                        ins = pe.transpose(ps[0][:, ch * P:(ch + 1) * P], xg[:, t.k, ch * P:(ch + 1) * P], ident[:, :])
                    ins.then_inc(g_T[t.k], 1)

                def per_edge_type(t):
                    if t is None:
                        return
                    seen(pe, g_ktc, t.at(-1))
                    seen(pe, g_vtc, t.at(-1))
                    seen(pe, g_kvTc, t)
                    for n, m in ((0, bd_a), (1, bd_m)):
                        for ch in range(C):
                            ins = pe.matmul(ps[4 + 2 * n + ch][:, 0:ETY * P], kvT[:, t.k, (2 * n + ch) * P:(2 * n + ch + 1) * P],
                                            m[:, :, :].rearrange("p t m -> p (t m)"), start=True, stop=True)
                    ins.then_inc(g_tab[t.k], 1)

                def tables(t):
                    ty = pe.value_load(slot_tyi[0:1, ds(t.t, 1)], min_val=0, max_val=NTY - 1)
                    seen(pe, g_Tc, t)
                    seen(pe, g_w, t)
                    seen(pe, g_kvTc, t.at(-2))
                    for o in range(2 * C):
                        for ch in range(C):
                            ins = pe.matmul(ps[1 + 2 * t.k][:, o * P:(o + 1) * P], wcur[t.k][:, ch, o * P:(o + 1) * P],
                                            xgT[:, t.k, ch * P:(ch + 1) * P], start=(ch == 0), stop=(ch == C - 1))
                    ins.then_inc(g_kvT[t.k], 1)
                    per_edge_type(t.at(-1))
                    turn_in(t.at(1))
                    seen(pe, g_qc, t.at(-1))
                    settle(pe)
                    for ch in range(C):
                        ins = pe.matmul(ps[2][:, 0:D], xgT[:, t.k, ch * P:(ch + 1) * P], wall[:, ds(ty, 1), ch, 2 * D:3 * D]
                                        .rearrange("p a o -> p (a o)"), start=(ch == 0), stop=(ch == C - 1))
                    ins.then_inc(g_q[t.k], 1)

                turn_in(Tile(0, 0, NS))
                over(pe, NS, tables)
                per_edge_type(Tile((NS - 1) // 2, 1, NS))

            @block.vector
            def _(dve):
                c = Chain(dve, vc)
                dve.wait_ge(s_types, 32)
                dve.wait_ge(s_const, 1)
                dve.tensor_copy(typ_t[0:NT, :], typ_i[0:NT, :]).then_inc(s_tyf, 1)
                dve.wait_ge(s_tyT, 1)
                for y in range(NTY):
                    ins = dve.tensor_scalar(is_ty[:, y, :], ps[7][:, 0:NT], float(y), None, ALU.is_equal)
                ins.then_inc(s_isty, 1)
                dve.wait_ge(s_tysum, 1)
                v3 = "p (y t) -> p y t"
                dve.tensor_copy(before_ty, ps[7][:, 0:NTY * NT].rearrange(v3, y=NTY))
                dve.tensor_copy(total_ty, ps[7][:, 256:256 + NTY * NT].rearrange(v3, y=NTY))
                c(dve.tensor_copy(scan[0], ps[7][:, 256:256 + NTY * NT].rearrange(v3, y=NTY)))
                step, at = 1, 0
                while step < NT:
                    dve.tensor_copy(scan[1 - at][:, :, 0:step], scan[at][:, :, 0:step])
                    c(dve.tensor_tensor(scan[1 - at][:, :, step:NT], scan[at][:, :, step:NT], scan[at][:, :, 0:NT - step],
                                        ALU.add))
                    step, at = 2 * step, 1 - at
                c(dve.tensor_scalar(tiles_i, scan[at][:, :, NT - 1], float(P - 1), None, ALU.add))
                c(dve.tensor_scalar(tiles_i, tiles_i, 7, None, ALU.arith_shift_right))
                assert P == 1 << 7
                c(dve.tensor_copy(tiles_f, tiles_i))
                c(dve.memset(start_f[:, 0:1], 0.0))
                for y in range(NTY):
                    c(dve.tensor_tensor(start_f[:, y + 1:y + 2], start_f[:, y:y + 1], tiles_f[:, y:y + 1], ALU.add))
                c(dve.tensor_tensor(before_ty, before_ty, scan[at], ALU.add))
                c(dve.tensor_tensor(before_ty, before_ty, total_ty, ALU.subtract))
                c(dve.scalar_tensor_tensor(before_ty,
                                           start_f[:, 0:NTY].rearrange("p (y t) -> p y t", t=1).to_broadcast([P, NTY, NT]),
                                           float(P), before_ty, ALU.mult, ALU.add))
                c(dve.tensor_tensor(before_ty, before_ty, is_ty, ALU.mult))
                c(dve.tensor_reduce(pos_f, before_ty.rearrange("p y t -> p t y"), AX, ALU.add))
                dve.tensor_copy(pos_i[:, :], pos_f).then_inc(s_pos, 1)
                c(dve.memset(slot_ty[:, :], 0.0))
                for y in range(NTY - 1):
                    c(dve.scalar_tensor_tensor(slot_ty[:, :], slot_j, start_f[:, y + 1:y + 2], slot_ty[:, :], ALU.is_ge,
                                               ALU.add))
                c(dve.tensor_copy(slot_tyi[:, :], slot_ty[:, :]))

                for t in range(NT):
                    if t % 5 == 0:
                        dve.wait_ge(s_xc[t // 5], 16)
                    if t == NT - 1:
                        dve.wait_ge(s_x, 16)
                    ins = dve.bn_stats(stats[:, t, :], rows[:, t, :])
                c(ins)
                for t in range(NT):
                    ins = dve.bn_aggr(mv_all[:, t, :], stats[:, t, :])
                ins.then_inc(s_var, 1)

                dve.wait_ge(s_edges, 16 * 9)
                dve.tensor_copy(rawf.rearrange("p a b -> p (a b)"), raw.rearrange("p a b c -> p (a b c)")).then_inc(s_rawf, 1)
                dve.wait_ge(s_eT, 1)
                c(dve.tensor_copy(typf[:, :], ps[2][:, 0:ET]))
                c(dve.tensor_scalar(rel[:, :], typf[:, :], float(ETY - 1), None, ALU.min))
                c(dve.scalar_tensor_tensor(rel[:, :], ps[0][:, 0:ET], float(TW // (2 * D)), rel[:, :], ALU.mult, ALU.add))
                c(dve.tensor_copy(grouped(idx_1[:, :])[:, :, 0:EV], grouped(rel[:, :])[:, :, 0:EV]))
                c(dve.tensor_scalar(grouped(idx_1[:, :])[:, :, EV:EG], grouped(rel[:, :])[:, :, EV:EG], 2.0, None, ALU.mult))
                c(dve.tensor_scalar(idx_v[:, :], rel[:, :], 2.0, 1.0, ALU.mult, ALU.add))
                dve.tensor_copy(dstf[:, :], ps[1][:, 0:ET]).then_inc(s_edge, 1)
                dve.wait_ge(s_edge, 1)
                dve.wait_ge(s_const2, 2)
                dve.wait_ge(s_bb, 1)
                c(dve.tensor_copy(base0[:, :], ps[3][:, 0:NG]))
                c(relative(base0))
                c(dve.tensor_tensor(rel[:, :], rel[:, :], valid, ALU.mult))
                c(dve.tensor_reduce(bad[:, 2:3], rel[:, :], AX, ALU.max))
                c(dve.tensor_reduce(bad[:, 3:4], rel[:, :], AX, ALU.min))
                c(dve.tensor_scalar(bad[:, 2:3], bad[:, 2:3], float(WIN), None, ALU.is_ge))
                c(dve.tensor_scalar(bad[:, 3:4], bad[:, 3:4], 0.0, None, ALU.is_lt))
                dve.tensor_tensor(bad[:, 0:1], bad[:, 2:3], bad[:, 3:4], ALU.max).then_inc(s_bad, 1)
                c(dve.memset(off[:, :], 0.0))
                dve.memset(vf[0][:, :, P:P + 1], 1.0)
                dve.memset(vf[1][:, :, P:P + 1], 1.0)
                dve.memset(zero, 0.0).then_inc(s_zero, 1)

                dve.wait_ge(s_rstd, 1)

                def front(t):
                    if t is None:
                        return
                    row = rows[:, ds(t.t, 1), :]
                    dve.tensor_scalar(row, row, mv_all[:, ds(t.t, 1), 0:1].rearrange("p a b -> p (a b)"),
                                      rstd_all[:, ds(t.t, 1)], ALU.subtract, ALU.mult).then_inc(xn_done[t.k], 1)

                def back(t):
                    if t is None:
                        return
                    seen(dve, acc_done, t.at(-2))
                    seen(dve, exp_done, t)
                    dve.scalar_tensor_tensor(kf[:, t.k, :], ps[2 + t.k][:, 0:D], 0.0, kexp[:, t.k, :], ALU.max, ALU.add
                                             ).then_inc(kf_done[t.k], 1)

                def body(t):
                    front(t.at(2))
                    back(t.at(-1))
                    seen(dve, k_ps, t)
                    seen(dve, exp_done, t.at(-2))
                    dve.tensor_scalar(kmin[:, t.k, :], ps[2 + t.k][:, 0:D], 0.0, None, ALU.min).then_inc(min_done[t.k], 1)

                front(Tile(0, 0, NT))
                front(Tile(0, 1, NT))
                over(dve, NT, body, first=2, ahead=2)
                back(Tile((NT - 1) // 2, 0, NT))

                dve.wait_ge(s_badall, 1)
                c(dve.tensor_scalar(good[:, :], bad[:, 1:2], -1.0, 1.0, ALU.mult, ALU.add))
                c(dve.tensor_scalar(npass_i[:, :], bad[:, 1:2], float(NPASS - 1), 1.0, ALU.mult, ALU.add))
                dve.wait_ge(s_pback, 16)
                dve.tensor_copy(perm_f[0:NS, :], perm_i[0:NS, :]).then_inc(s_permf, 1)
                dve.wait_ge(s_closed, 1)
                for ch in range(C):
                    c(dve.tensor_tensor(kvd[:, ch, 0:P], ps[6][:, ch * 129:ch * 129 + P], hmask[:, 0:P], ALU.mult))
                    c(dve.tensor_copy(zero[:, ch:ch + 1], ps[6][:, ch * 129 + P:ch * 129 + P + 1]))
                    c(dve.tensor_scalar(kvd[:, ch, P:P + 4], hmask[:, P:P + 4], zero[:, ch:ch + 1], None, ALU.mult))
                dve.wait_ge(s_permT, 1)
                c(dve.tensor_copy(to_i[:, :], ps[7][:, 0:NS]))
                c(dve.tensor_scalar(from_i[:, :], ps[7][:, 0:NS], float(N - 1), None, ALU.min))
                dve.wait_ge(s_vec, 16 * (1 + 1 + len(vec_names) + 6))
                c(dve.tensor_scalar(pri[:, :], pri[:, :], float(1.0 / np.sqrt(DK).astype(np.float32)), None, ALU.mult))
                seen_all(dve, xT_done, NT)
                dve.sem_inc(s_perm, 1)
                dve.sem_inc(s_kvd, 1)

                def k_out(t):
                    if t is None:
                        return
                    seen(dve, g_out, t.at(-2), 16)
                    seen(dve, g_tab, t)
                    for ch in range(C):
                        ins = dve.tensor_tensor(
                            tab[:, t.k, 0:QC].rearrange("p (t s h d) -> p t s h d", t=ETY, s=2, d=DK)[:, :, 0, 4 * ch:4 * ch + 4, :],
                            ps[4 + ch][:, 0:ETY * P].rearrange("p (t h d) -> p t h d", t=ETY, d=DK),
                            pri[:, :].rearrange("p (t h d) -> p t h d", t=ETY, d=1)[:, :, 4 * ch:4 * ch + 4, :]
                            .to_broadcast([P, ETY, 4, DK]), ALU.mult)
                    ins.then_inc(g_ktc[t.k], 1)

                def tables(t):
                    ty = dve.value_load(slot_tyi[0:1, ds(t.t, 1)], min_val=0, max_val=NTY - 1)
                    seen(dve, g_tab, t.at(-2))
                    seen(dve, g_kvT, t)
                    settle(dve)
                    dve.tensor_tensor(kvT[:, t.k, :].rearrange("p (o n) -> p o n", n=P),
                                      ps[1 + 2 * t.k][:, :].rearrange("p (o n) -> p o n", n=P),
                                      kv_bias[:, ds(ty, 1), :].rearrange("p a (o n) -> p (a o) n", n=1)
                                      .to_broadcast([P, 2 * C, P]), ALU.add).then_inc(g_kvTc[t.k], 1)
                    k_out(t.at(-1))
                    seen(dve, g_out, t.at(-2), 16)
                    seen(dve, g_q, t)
                    settle(dve)
                    dve.tensor_tensor(tab[:, t.k, QC:QC + D].rearrange("p (a d) -> p a d", a=1),
                                      ps[2][:, 0:D].rearrange("p (a d) -> p a d", a=1), q_bias[:, ds(ty, 1), :],
                                      ALU.add).then_inc(g_qc[t.k], 1)

                c(dve.memset(tab[:, :, QC + D:TW], 0.0))
                dve.wait_ge(s_qb, 16)
                dve.wait_ge(s_bias, 32)
                over(dve, NS, tables, first=2)
                k_out(Tile((NS - 1) // 2, 1, NS))

        new_stage()
        vc, vs, vm, vd = sem("score_step"), sem("softmax_step"), sem("message_step"), sem("mix_step")
        vb = sem("mix_step_ends")
        e1_base, e2_base, e1_end = sem("bases_1"), sem("bases_2"), sem("scored")
        e1_idx, e2_idx = [sem(f"index_1{g}") for g in range(GB)], [sem(f"index_2{g}") for g in range(GB)]
        e1_got, e2_got = [sem(f"row_1{k}") for k in range(EB)], [sem(f"row_2{k}") for k in range(EB)]
        v_out, v_in = [sem(f"v_kept{g}") for g in range(GB)], [sem(f"v_in{g}") for g in range(GB)]
        win_in, dstb_in, dist_done, oh_done, oh2, msg_done, agg_ps, agg_add = (
            [sem(f"{n}{g}") for g in range(GB)] for n in ("window", "targets", "distance", "onehotT", "onehot", "message",
                                                          "agg_ps", "agg_added"))
        q_done, prod_done = ([sem(f"{n}{p}") for p in range(2 * GB)] for n in ("q_rows", "product"))
        s_max, s_gmax, s_neg, s_exp, s_gsum, s_alpha = (sem(n) for n in (
            "maxima", "maxima_all", "maxima_negated", "exponentials", "sums_all", "weights_ready"))
        s_fw = sem("ffn_weights_in")
        m_xa, m_T, m_Tc, m_q, m_h, m_min, m_exp, m_gelu, m_kf, m_t, m_y, m_var, m_sd, m_x1, m_x1k, m_fin, m_tx, m_rt, m_sc = (
            sem(n) for n in ("mix_xn", "mix_T", "mix_Tc", "mix_q", "mix_h", "mix_min", "mix_exp", "mix_gelu", "mix_kf",
                             "mix_t", "mix_y", "mix_var", "mix_centred_2", "mix_x1", "mix_x1_kept", "mix_fin", "mix_tx", "mix_roots", "mix_centred_1"))

        def passes_of(eng):
            return eng.value_load(npass_i[0:1, 0:1], min_val=1, max_val=NPASS)

        def passes(eng, first, again):
            n = passes_of(eng)
            first()
            with eng.If(n > 1):
                with eng.Fori(1, n) as r:
                    again(r)
            return n

        def window_starts(eng, b):
            return nc.values_load_multi_w_load_instructions(
                base_i[0:1, ds(b, 1), 0:GB].rearrange("p b g -> p (b g)"), engines=(eng.engine,),
                min_val=0, max_val=NP - WIN)[1]

        def of_type(t):
            return slice(t * H, (t + 1) * H)

        def once(eng, event, t):
            if not (isinstance(t, int) and t < 0):
                eng.wait_ge(event, t + 1)

        def bodies(eng, body):
            for b in range(6):
                body(b, True)
            with eng.Fori(6, NT) as b:
                body(b, True)
            for b in range(NT, NT + 5):
                body(b, True)
            with eng.Fori(NT + 5, NB) as b:
                body(b, False)

        def tile_of(b, back):
            t = b - back
            return None if isinstance(t, int) and not 0 <= t < NT else t

        with nc.Block() as block:
            @block.sync
            def _(sp):
                def scan_pass(r):
                    sp.wait_ge(e1_base, r + 1)
                    settle(sp)
                    with sp.Fori(0, NB) as b:
                        i = r * NB + b
                        at = window_starts(sp, b)
                        for g in range(GB):
                            sp.wait_ge(oh_done[g], i + 1)
                            settle(sp)
                            sp.dma_start(dst_b[0:WIN, g, :],
                                         dst_d.rearrange("(g k) c -> g (k c)", k=EG)[ds(b * GB + g, 1), :]
                                         .to_broadcast([WIN, EG * P])).then_inc(dstb_in[g], 16)
                            sp.wait_ge(q_done[2 * g + 1], i + 1)
                            settle(sp)
                            sp.dma_start(qwin[0:WIN, g, :], tab_d[ds(at[g], WIN), QC:QC + D]).then_inc(win_in[g], 16)

                passes(sp, lambda: scan_pass(0), scan_pass)
                n = passes_of(sp)
                for g in range(GB):
                    sp.wait_ge(v_out[g], 16 * n * NB)
                settle(sp)
                sp.wait_ge(e1_end, n * NB)
                settle(sp)

                def v_pass(r):
                    with sp.Fori(0, NB) as b:
                        for g in range(GB):
                            sp.wait_ge(msg_done[g], r * NB + b + 1)
                            settle(sp)
                            sp.dma_start(gath2[:, EG * g:EG * g + EV, :].rearrange("p k d -> p (k d)"),
                                         v_d[ds(b * GB + g, 1), :, :].rearrange("g p d -> p (g d)")).then_inc(v_in[g], 16)

                passes(sp, lambda: v_pass(0), v_pass)
                sp.wait_ge(s_alpha, 1)
                sp.dma_start(fw1, a["L0_ffn_w1"].rearrange("(c p) f -> p c f", p=P)).then_inc(s_fw, 16)
                sp.dma_start(fw2, a["L0_ffn_w2"].rearrange("(j p) d -> p j d", p=P)).then_inc(s_fw, 16)
                sp.wait_ge(s_fw, 32)

            @block.gpsimd
            def _(pool):
                def gather(dst, table, index, got):
                    pool.indirect_dma_start(dst, None, table, bass.IndirectOffsetOnAxis(ap=index, axis=0)).then_inc(got, 16)

                pairs = tab_d[0:N, :].rearrange("n (s d) -> (n s) d", d=2 * D)
                singles = tab_d[0:N, :].rearrange("n (s d) -> (n s) d", d=D)

                def loop1(r, b, kept):
                    i = r * NB + b
                    for g in range(GB):
                        pool.wait_ge(prod_done[2 * g], i + 1)
                        pool.wait_ge(prod_done[2 * g + 1], i + 1)
                        if kept:
                            pool.wait_ge(v_out[g], 16 * i)
                        settle(pool)
                        pool.tensor_copy(idxb[:, g, :], idx_1[:, ds(b * EB + g * EG, EG)]).then_inc(e1_idx[g], 1)
                        pool.wait_ge(e1_idx[g], i + 1)
                        settle(pool)
                        for k in range(EG):
                            if k < EV:
                                gather(gathp[:, g, k, :], pairs, idxb[:, g, k:k + 1], e1_got[EG * g + k])
                            else:
                                gather(gathk[:, g, k - EV, :], singles, idxb[:, g, k:k + 1], e1_got[EG * g + k])

                def first1():
                    loop1(0, 0, False)
                    with pool.Fori(1, NB) as b:
                        loop1(0, b, True)

                def again1(r):
                    with pool.Fori(0, NB) as b:
                        loop1(r, b, True)

                def loop2(r):
                    with pool.Fori(0, NB) as b:
                        i = r * NB + b
                        for g in range(GB):
                            pool.wait_ge(msg_done[g], i + 1)
                            settle(pool)
                            pool.tensor_copy(idxb[:, g, EV:EG], idx_v[:, ds(b * EB + g * EG + EV, EG - EV)]
                                             ).then_inc(e2_idx[g], 1)
                            pool.wait_ge(e2_idx[g], i + 1)
                            settle(pool)
                            for k in range(EV, EG):
                                gather(gath2[:, EG * g + k, :], singles, idxb[:, g, k:k + 1], e2_got[EG * g + k])

                n = passes(pool, first1, again1)
                for t in range(ETY):
                    pool.wait_ge(s_max, t + 1)
                    pool.partition_all_reduce(gmax[:, of_type(t)], smax[:, of_type(t)], P, RMAX).then_inc(s_gmax, 1)
                    pool.wait_ge(s_gmax, t + 1)
                    pool.tensor_scalar(nmax[:, of_type(t)], gmax[:, of_type(t)], -1.0, None, ALU.mult).then_inc(s_neg, 1)
                for t in range(ETY):
                    pool.wait_ge(s_exp, (t + 1) * H)
                    pool.partition_all_reduce(gsum[:, of_type(t)], ssum[:, of_type(t)], P, RADD).then_inc(s_gsum, 1)
                for g in range(GB):
                    pool.wait_ge(v_out[g], 16 * n * NB)
                settle(pool)
                passes(pool, lambda: loop2(0), loop2)

            @block.scalar
            def _(act):
                for g in range(GB):
                    act.sem_inc(oh_done[g], 1)

                def keep_v(i, b, g):
                    for k in range(EV):
                        act.wait_ge(e1_got[EG * g + k], 16 * (i + 1))
                    settle(act)
                    act.dma_start(v_d[ds(b * GB + g, 1), :, :].rearrange("g p (k d) -> p (g k) d", k=EV),
                                  gathp[:, g, :, D:2 * D]).then_inc(v_out[g], 16)

                def scan_pass(r):
                    act.wait_ge(e1_base, r + 1)
                    settle(act)
                    with act.Fori(0, NB) as b:
                        i = r * NB + b
                        for g in range(GB):
                            act.wait_ge(oh_done[g], i + 1)
                            act.wait_ge(dstb_in[g], 16 * (i + 1))
                            settle(act)
                            act.activation(dist[0:WIN, g, :], dst_b[0:WIN, g, :], ACT.Abs,
                                           bias=base_n[0:WIN, ds(b * GB + g, 1)]).then_inc(dist_done[g], 1)
                            act.wait_ge(q_done[2 * g + 1], i + 1)
                            act.wait_ge(dist_done[g], i + 1)
                            act.activation(ohT[0:WIN, g, :], dist[0:WIN, g, :], ACT.Relu, bias=ones[0:WIN, 0:1],
                                           scale=-1.0).then_inc(oh_done[g], 1)
                            if g > 0:
                                keep_v(i, b, g - 1)
                        keep_v(i, b, GB - 1)

                passes(act, lambda: scan_pass(0), scan_pass)

                for t in range(ETY):
                    act.wait_ge(s_neg, t + 1)
                    for h in range(H):
                        j = t * H + h
                        act.activation(sty[t][:, :, h], sty[t][:, :, h], ACT.Exp, bias=nmax[:, j:j + 1],
                                       accum_out=ssum[:, j:j + 1]).then_inc(s_exp, 1)

                act.wait_ge(s_alpha, 1)

                def body(b, mix):
                    if not mix:
                        return
                    t0, t1, t2, t3, t4, t5 = (tile_of(b, n) for n in range(6))
                    if t0 is not None:
                        once(act, m_T, b - 1)
                        settle(act)
                        act.activation(xa.rearrange("p (a d) -> p a d", a=1), rows[:, ds(t0, 1), :], ACT.Copy).then_inc(m_xa, 1)
                    if t1 is not None:
                        once(act, m_exp, t1 - 1)
                        once(act, m_q, t1)
                        act.activation(qmin, ps[3][:, 0:D], ACT.Relu, scale=-1.0).then_inc(m_min, 1)
                        once(act, m_kf, t1 - 1)
                        once(act, m_min, t1)
                        act.activation(qexp, qmin, ACT.Exp, scale=-1.0).then_inc(m_exp, 1)
                    if t4 is not None:
                        once(act, m_y, t4 - 1)
                        once(act, m_h, t4)
                        for j in range(C):
                            ins = act.activation(hT[:, j * P:(j + 1) * P], ps[6][:, j * P:(j + 1) * P], ACT.Gelu,
                                                 bias=b1c[:, j:j + 1])
                        ins.then_inc(m_gelu, 1)
                    if t3 is not None:
                        once(act, m_x1, t3)
                        settle(act)
                        act.activation(rows[:, ds(t3, 1), :], x1.rearrange("p (a d) -> p a d", a=1), ACT.Copy
                                       ).then_inc(m_x1k, 1)
                    if t0 is not None or t3 is not None:
                        lo, hi = (0 if t0 is not None else D), (2 * D if t3 is not None else D)
                        if t0 is not None:
                            once(act, m_q, b - 1)
                        if t3 is not None:
                            once(act, m_h, t3 - 1)
                        once(act, m_T, b)
                        act.activation(xT2[:, lo:hi], ps[5][:, lo:hi], ACT.Copy).then_inc(m_Tc, 1)
                    if t2 is not None or t4 is not None:
                        lo, hi = (0 if t2 is not None else 1), (2 if t4 is not None else 1)
                        once(act, m_var, b - 2)
                        act.activation(sd[:, lo:hi], mvs[:, lo:hi, 1], ACT.Sqrt, bias=eps[:, :]).then_inc(m_rt, 1)

                bodies(act, body)

            @block.tensor
            def _(pe):
                for s in q_done:
                    pe.sem_inc(s, 1)

                def scan_pass(r):
                    with pe.Fori(0, NB) as b:
                        i = r * NB + b
                        for g in range(GB):
                            pe.wait_ge(oh_done[g], i + 2)
                            pe.wait_ge(win_in[g], 16 * (i + 1))
                            for u in range(2):
                                pe.wait_ge(prod_done[2 * g + u], i + 1)
                                for k in range(2):
                                    e = 2 * u + k
                                    ins = pe.matmul(ps[2 * g + u][:, k * D:(k + 1) * D], ohT[0:WIN, g, e * P:(e + 1) * P],
                                                    qwin[0:WIN, g, :], start=True, stop=True)
                                ins.then_inc(q_done[2 * g + u], 1)

                passes(pe, lambda: scan_pass(0), scan_pass)
                pe.wait_ge(s_alpha, 1)

                def sums(i, g):
                    pe.wait_ge(oh2[g], i + 1)
                    pe.wait_ge(msg_done[g], i + 2)
                    pe.wait_ge(agg_add[g], i + 1)
                    for ch in range(C):
                        for k in range(EG):
                            ins = pe.matmul(ps[g][:, ch * WIN:(ch + 1) * WIN], msgs[g][:, k, ch * P:(ch + 1) * P],
                                            onehot[g][:, k, :], start=(k == 0), stop=(k == EG - 1))
                    ins.then_inc(agg_ps[g], 1)

                def body(b, mix):
                    t0, t1, t2, t3, t4, t5 = (tile_of(b, n) if mix else None for n in range(6))
                    if t2 is not None:
                        once(pe, m_tx, t2 - 1)
                        once(pe, m_kf, t2)
                        for ch in range(C):
                            ins = pe.matmul(ps[4][:, ch * 132:(ch + 1) * 132], qf[:, ch * P:(ch + 1) * P], kvd[:, ch, :],
                                            start=True, stop=True)
                        ins.then_inc(m_t, 1)
                    sums(b, 0)
                    if t4 is not None:
                        once(pe, m_sd, t4 - 1)
                        once(pe, m_gelu, t4)
                        for ch in range(C):
                            ins = pe.matmul(ps[7][:, 0:D], hT[:, ch * P:(ch + 1) * P], w2T[:, ch, :],
                                            start=(ch == 0), stop=(ch == C - 1))
                        ins.then_inc(m_y, 1)
                    sums(b, 1)
                    if t0 is not None or t3 is not None:
                        once(pe, m_Tc, b - 1)
                        if t0 is not None:
                            once(pe, m_xa, t0)
                        if t3 is not None:
                            once(pe, m_x1, t3)
                        settle(pe)
                        for src, lo, t in ((xa, 0, t0), (x1, D, t3)):
                            if t is not None:
                                for ch in range(C):
                                    ins = pe.transpose(ps[5][:, lo + ch * P:lo + (ch + 1) * P], src[:, ch * P:(ch + 1) * P],
                                                       ident[:, :])
                        ins.then_inc(m_T, 1)
                    sums(b, 2)
                    if t0 is not None:
                        once(pe, m_kf, t0 - 1)
                        once(pe, m_Tc, b)
                        for o in range(C):
                            for ch in range(C):
                                ins = pe.matmul(ps[3][:, o * P:(o + 1) * P], wqkvT[:, ch, o * P:(o + 1) * P],
                                                xT2[:, ch * P:(ch + 1) * P], start=(ch == 0), stop=(ch == C - 1))
                        ins.then_inc(m_q, 1)
                    if t3 is not None:
                        once(pe, m_gelu, t3 - 1)
                        once(pe, m_Tc, b)
                        for o in range(C):
                            for ch in range(C):
                                ins = pe.matmul(ps[6][:, o * P:(o + 1) * P], w1T[:, ch, o * P:(o + 1) * P],
                                                xT2[:, D + ch * P:D + (ch + 1) * P], start=(ch == 0), stop=(ch == C - 1))
                        ins.then_inc(m_h, 1)

                def again(r):
                    with pe.Fori(0, NB) as b:
                        for g in range(GB):
                            sums(r * NB + b, g)

                passes(pe, lambda: bodies(pe, body), again)

            @block.vector
            def _(dve):
                n = dve.value_load(npass_i[0:1, 0:1], min_val=1, max_val=NPASS)
                for s in prod_done + msg_done + agg_ps + agg_add:
                    dve.sem_inc(s, 1)
                c = Chain(dve, vc)
                c(dve.memset(eps[:, :], EPS_LN))
                c(dve.memset(scores, 0.0))
                c.straight()
                start = c.start

                def windows(base_sem):
                    c(dve.tensor_scalar(base_f[:, :], base0[:, :], good[:, :], off[:, :], ALU.mult, ALU.add))
                    c(relative(base_f))
                    c(dve.tensor_scalar(base_n[:, :], base_f[:, :], iota_p[:, :], -1.0, ALU.add, ALU.mult))
                    c(dve.scalar_tensor_tensor(off[:, :], bad[:, 1:2], float(WIN), off[:, :], ALU.mult, ALU.add))
                    dve.tensor_copy(base_i[:, :, 0:GB], base_f[:, :].rearrange("p (b g) -> p b g", g=GB)).then_inc(base_sem, 1)

                def scan_pass(r):
                    c.base, c.n = start + r * (4 + 2 * GB * NB), 0
                    windows(e1_base)
                    with dve.Fori(0, NB) as b:
                        i = r * NB + b
                        c.base, c.n = start + r * (4 + 2 * GB * NB) + 4 + b * 2 * GB, 0
                        for q in range(2 * GB):
                            for k in range(2):
                                dve.wait_ge(e1_got[2 * q + k], 16 * (i + 1))
                            dve.wait_ge(q_done[q], i + 2)
                            k_rows = gathp[:, q // 2, :, 0:D] if q % 2 == 0 else gathk[:, q // 2, :, :]
                            dve.tensor_tensor(prod[:, q % 2, :].rearrange("p (k d) -> p k d", k=2), k_rows,
                                              ps[q][:, :].rearrange("p (k d) -> p k d", k=2), ALU.mult
                                              ).then_inc(prod_done[q], 1)
                            dve.wait_ge(prod_done[q], i + 2)
                            c(dve.tensor_reduce(part[:, q % 2, :], prod[:, q % 2, :].rearrange("p (s d) -> p s d", d=DK),
                                                AX, ALU.add))
                            sc = scores[:, ds(b * EB + 2 * q, 2), :]
                            ins = dve.tensor_tensor(sc, sc, part[:, q % 2, :].rearrange("p (k h) -> p k h", k=2), ALU.add)
                        ins.then_inc(e1_end, 1)

                scan_pass(0)
                with dve.If(n > 1):
                    with dve.Fori(1, n) as r:
                        scan_pass(r)
                dve.wait_ge(e1_end, n * NB)

                c = Chain(dve, vs)
                for t in range(ETY):
                    c(dve.tensor_scalar(rel[:, :], typf[:, :], float(t), BIG, ALU.not_equal, ALU.mult))
                    for h in range(H):
                        ins = dve.tensor_tensor_reduce(sty[t][:, :, h], scores[:, :, h], rel[:, :], 1.0, BIG, ALU.add,
                                                       ALU.max, smax[:, t * H + h:t * H + h + 1])
                    c(ins)
                    dve.sem_inc(s_max, 1)
                for t in range(ETY):
                    dve.wait_ge(s_gsum, t + 1)
                    c(dve.tensor_scalar(gsum[:, of_type(t)], gsum[:, of_type(t)], 1.0e-30, None, ALU.max))
                    c(dve.reciprocal(ssum[:, of_type(t)], gsum[:, of_type(t)]))
                    inverse = ssum[:, of_type(t)].rearrange("p (a h) -> p a h", a=1).to_broadcast([P, ET, H])
                    c(dve.tensor_tensor(scores if t == 0 else sty[t], sty[t], inverse, ALU.mult))
                    if t > 0:
                        c(dve.tensor_tensor(scores, scores, sty[t], ALU.add))
                c(dve.memset(off[:, :], 0.0))
                dve.sem_inc(s_alpha, 1)

                c = Chain(dve, vm)
                windows(e2_base)
                dve.wait_ge(e2_base, 1)
                c.straight()
                again_start = c.start

                def messages(i, b, g):
                    dve.wait_ge(agg_ps[g], i + 1)
                    settle(dve)
                    dve.tensor_tensor(onehot[g], iota_w[:, :].rearrange("p (a w) -> p a w", a=1).to_broadcast([P, EG, WIN]),
                                      rel[:, ds(b * EB + g * EG, EG)].rearrange("p (k w) -> p k w", w=1)
                                      .to_broadcast([P, EG, WIN]), ALU.is_equal).then_inc(oh2[g], 1)
                    dve.wait_ge(v_in[g], 16 * (i + 1))
                    for k in range(EV, EG):
                        dve.wait_ge(e2_got[EG * g + k], 16 * (i + 1))
                    settle(dve)
                    dve.tensor_tensor(msgs[g].rearrange("p k (h d) -> p k h d", d=DK),
                                      gath2[:, EG * g:EG * (g + 1), :].rearrange("p k (h d) -> p k h d", d=DK),
                                      scores[:, ds(b * EB + EG * g, EG), :].rearrange("p k (h d) -> p k h d", d=1)
                                      .to_broadcast([P, EG, H, DK]), ALU.mult).then_inc(msg_done[g], 1)

                def add(i, g, at):
                    dve.wait_ge(agg_add[(g - 1) % GB], i + 1 + (g > 0))
                    dve.wait_ge(agg_ps[g], i + 2)
                    settle(dve)
                    win = cols[:, :, ds(at, WIN)]
                    dve.tensor_tensor(win, win, ps[g][:, 0:C * WIN].rearrange("p (c w) -> p c w", c=C), ALU.add
                                      ).then_inc(agg_add[g], 1)

                cs, cd = Chain(dve, vb), Chain(dve, vd)

                def body(b, mix):
                    t0, t1, t2, t3, t4, t5 = (tile_of(b, k) if mix else None for k in range(6))
                    m = cs
                    if mix and not isinstance(b, int):
                        m = cd
                        m.turn(b - 6, 7)
                    def add_last(g):
                        if not (isinstance(b, int) and b == 0):
                            add(b - 1, g, at[g])

                    messages(b, b, 0)
                    if not (isinstance(b, int) and b == 0):
                        at = window_starts(dve, b - 1)
                    if t3 is not None or t5 is not None:
                        lo, hi = (0 if t3 is not None else 1), (2 if t5 is not None else 1)
                        once(dve, m_rt, b - 3)
                        m.start_step(dve.reciprocal(rss[:, lo:hi], sd[:, lo:hi]))
                    add_last(0)
                    if t3 is not None or t5 is not None:
                        m.due()
                    if t3 is not None:
                        once(dve, m_sc, t3)
                        if t4 is not None:
                            once(dve, m_T, b - 1)
                            once(dve, m_x1k, t4)
                        dve.scalar_tensor_tensor(x1, tx, rss[:, 0:1], vecs["L0_mix_ln1_b"][:, :], ALU.mult, ALU.add
                                                 ).then_inc(m_x1, 1)
                    if t5 is not None:
                        once(dve, m_sd, t5)
                        dve.scalar_tensor_tensor(rows[:, ds(t5, 1), :], x2m.rearrange("p (a d) -> p a d", a=1), rss[:, 1:2],
                                                 vecs["L0_mix_ln2_b"][:, :].rearrange("p (a d) -> p a d", a=1), ALU.mult,
                                                 ALU.add).then_inc(m_fin, 1)
                    add_last(1)
                    messages(b, b, 1)
                    if t1 is not None:
                        once(dve, m_t, t1 - 1)
                        once(dve, m_exp, t1)
                        dve.scalar_tensor_tensor(qf, ps[3][:, 0:D], 0.0, qexp, ALU.max, ALU.add).then_inc(m_kf, 1)
                    if t2 is not None:
                        once(dve, m_t, t2)
                        t3d = ps[4][:, 0:2 * 132].rearrange("p (c m) -> p c m", c=C)
                        m.start_step(dve.tensor_scalar(den.rearrange("p (c h) -> p c h", c=C), t3d[:, :, P:P + 4], EPS_ATTN,
                                                       None, ALU.add))
                    add_last(2)
                    if t2 is not None:
                        m.due()
                        settle(dve)
                        m.start_step(dve.reciprocal(den, den))
                    messages(b, b, 2)
                    if t2 is not None:
                        m.due()
                        settle(dve)
                        m.start_step(dve.tensor_tensor(tx.rearrange("p (c h d) -> p c h d", c=C, d=DK),
                                                       t3d[:, :, 0:P].rearrange("p c (h d) -> p c h d", d=DK),
                                                       den.rearrange("p (c h d) -> p c h d", c=C, d=1)
                                                       .to_broadcast([P, C, 4, DK]), ALU.mult))
                    if t4 is not None:
                        once(dve, m_y, t4)
                        m.start_step(dve.tensor_tensor(x2m, ps[7][:, 0:D], vecs["L0_mix_b2"][:, :], ALU.add))
                    if t2 is not None or t4 is not None:
                        m.due()
                    if t2 is not None:
                        settle(dve)
                        txa = tx.rearrange("p (a d) -> p a d", a=1)
                        dve.tensor_tensor(txa, txa, rows[:, ds(t2, 1), :], ALU.add).then_inc(m_tx, 1)
                    if t4 is not None:
                        xm = x2m.rearrange("p (a d) -> p a d", a=1)
                        once(dve, m_x1k, t4)
                        settle(dve)
                        m.start_step(dve.tensor_tensor(xm, xm, rows[:, ds(t4, 1), :], ALU.add))
                    if t2 is not None:
                        once(dve, m_tx, t2)
                        settle(dve)
                        ins = dve.bn_stats(sts[:, 0, :], tx)
                    if t4 is not None:
                        m.due()
                        settle(dve)
                        ins = dve.bn_stats(sts[:, 1, :], x2m)
                    if t2 is not None or t4 is not None:
                        lo, hi = (0 if t2 is not None else 1), (2 if t4 is not None else 1)
                        m(ins)
                        settle(dve)
                        for k in range(lo, hi):
                            ins = dve.bn_aggr(mvs[:, k, :], sts[:, k, :])
                        ins.then_inc(m_var, 1)
                    if t2 is not None or t4 is not None:
                        once(dve, m_var, b - 2)
                    if t2 is not None:
                        dve.scalar_tensor_tensor(tx, tx, mvs[:, 0, 0:1], vecs["L0_mix_ln1_g"][:, :], ALU.subtract, ALU.mult
                                                 ).then_inc(m_sc, 1)
                    if t4 is not None:
                        dve.scalar_tensor_tensor(x2m, x2m, mvs[:, 1, 0:1], vecs["L0_mix_ln2_g"][:, :], ALU.subtract,
                                                 ALU.mult).then_inc(m_sd, 1)
                    assert m is not cd or m.n == 7, m.n

                bodies(dve, body)
                at = window_starts(dve, NB - 1)
                for g in range(GB):
                    add(NB - 1, g, at[g])

                def again(r):
                    c.base, c.n = again_start + (r - 1) * 4, 0
                    windows(e2_base)
                    dve.wait_ge(e2_base, r + 1)
                    settle(dve)
                    with dve.Fori(0, NB) as b:
                        i = r * NB + b
                        at = window_starts(dve, b)
                        for g in range(GB):
                            messages(i, b, g)
                        for g in range(GB):
                            add(i, g, at[g])

                with dve.If(n > 1):
                    with dve.Fori(1, n) as r:
                        again(r)
                dve.wait_ge(agg_add[GB - 1], n * NB + 1)
                settle(dve)

        new_stage()
        vc, vf3, vsel, pc = sem("closing_step"), sem("closing_ends"), sem("select_step"), sem("pool_step")
        x_in, ga_in, ga_T, ln3_var, ln3_rs, ln4_var, ln4_rs, gb_ok, x3_ok, x3_T, x3_Tc, gate_ok = (pair(n) for n in (
            "x_in", "agg_copied", "agg_turned", "gnn_var", "gnn_rstd", "ffn_var", "ffn_rstd", "sum_done", "xf",
            "xf_turned", "xf_copied", "gate"))
        ha_ps, hb_ps, ha_ok, hb_ok, y_ps, y_ok, out_ok, out_st = (pair(n) for n in (
            "h_ps_first", "h_ps_second", "h_first", "h_second", "y_ps", "y", "out", "out_stored"))
        s_const3, s_cnt, s_tot, s_eq, s_eqsum = (sem(n) for n in (
            "select_constants", "counted", "counts_summed", "equals_marked", "equals_summed"))
        HF = FJ // 2

        def stores(eng, k):
            def store(t):
                if t.k == k:
                    n = LAST if isinstance(t.t, int) and t.t == NT - 1 else P
                    seen(eng, out_ok, t)
                    settle(eng)
                    eng.dma_start(out[ds(t.t * P, n), :],
                                  rows[0:n, ds(t.t, 1), :].rearrange("p a d -> p (a d)")).then_inc(out_st[k], 16)

            over(eng, NT, store)
            eng.wait_ge(out_st[k], 16 * ((NT + 1 - k) // 2))

        with nc.Block() as block:
            @block.sync
            def _(sp):
                def load(t, n=P):
                    seen(sp, gb_ok, t.at(-2))
                    settle(sp)
                    sp.dma_start(xo[0:n, t.k, :], x_d[ds(t.t * P, n), :]).then_inc(x_in[t.k], 16)

                over(sp, NT, lambda t: load(t, LAST if isinstance(t.t, int) and t.t == NT - 1 else P))

                stores(sp, 0)

            @block.gpsimd
            def _(pool):
                c = Chain(pool, pc)
                pool.iota(digits_i, pattern=[[1, 15]], base=1, channel_multiplier=0)
                pool.memset(flip_i, -1)
                pool.memset(top_i, -2 ** 31)
                pool.memset(limit, -BIG)
                c(pool.memset(tri3, 1.0))
                c(pool.affine_select(out=tri3, in_=tri3, compare_op=ALU.is_ge, fill=0.0, base=-1,
                                     pattern=[[1, P]], channel_multiplier=-1))
                pool.affine_select(out=limit, in_=limit, compare_op=ALU.is_ge, fill=BIG, base=LAST - 1,
                                   pattern=[[0, 1]], channel_multiplier=-1).then_inc(s_const3, 1)

                def rsqrt(t, mv, rs, var, done):
                    if t is None:
                        return
                    seen(pool, var, t)
                    settle(pool)
                    pool.tensor_scalar(rs[:, t.k, 1:2], mv[:, t.k, 1:2], EPS_LN, None, ALU.add).then_inc(done[t.k], 1)
                    pool.wait_ge(done[t.k], 2 * t.i + 1)
                    pool.tensor_tensor(rs[:, t.k, 0:1], rs[:, t.k, 1:2], nhalf[:, 0:1], ALU.pow).then_inc(done[t.k], 1)

                def body(t):
                    rsqrt(t.at(-1), mv4, rs4, ln4_var, ln4_rs)
                    rsqrt(t.at(0), mv3, rs3, ln3_var, ln3_rs)

                over(pool, NT, body, more=1)

            @block.scalar
            def _(act):
                def take(t):
                    if t is None:
                        return
                    seen(act, ga_T, t.at(-2))
                    settle(act)
                    act.activation(chunks(ga[:, t.k, :]), cols[:, :, ds(t.t * P, P)], ACT.Copy).then_inc(ga_in[t.k], 1)

                def put(t):
                    if t is None:
                        return
                    seen(act, x3_T, t)
                    settle(act)
                    act.activation(cols[:, :, ds(t.t * P, P)], chunks(ps[2 + t.k][:, 0:D]), ACT.Copy).then_inc(x3_Tc[t.k], 1)

                def gelu(t):
                    if t is None:
                        return
                    seen(act, y_ps, t.at(-2))
                    for half, (ready, done) in enumerate(((ha_ps, ha_ok), (hb_ps, hb_ok))):
                        seen(act, ready, t)
                        for j in range(HF):
                            f = half * HF + j
                            ins = act.activation(fh[:, t.k, f * P:(f + 1) * P], ps[4 + half][:, j * P:(j + 1) * P],
                                                 ACT.Gelu_apprx_tanh, bias=fb1[:, f:f + 1])
                        ins.then_inc(done[t.k], 1)

                def body(t):
                    take(t.at(1))
                    gelu(t.at(-3))
                    put(t.at(-2))

                take(Tile(0, 0, NT))
                over(act, NT, body, first=3, more=3)
                stores(act, 1)

            @block.tensor
            def _(pe):
                def turn(t, src, event, ready, used, bank):
                    if t is None:
                        return
                    seen(pe, ready, t)
                    seen(pe, used, t.at(-2))
                    settle(pe)
                    for ch in range(C):
                        ins = pe.transpose(ps[bank + t.k][:, ch * P:(ch + 1) * P], src[:, t.k, ch * P:(ch + 1) * P],
                                           ident[:, :])
                    ins.then_inc(event[t.k], 1)

                def up(t):
                    if t is None:
                        return
                    seen(pe, x3_Tc, t)
                    for half, (used, done) in enumerate(((ha_ok, ha_ps), (hb_ok, hb_ps))):
                        seen(pe, used, t.at(-1))
                        settle(pe)
                        for j in range(HF):
                            f = half * HF + j
                            for ch in range(C):
                                ins = pe.matmul(ps[4 + half][:, j * P:(j + 1) * P], fw1[:, ch, f * P:(f + 1) * P],
                                                cols[:, ch, ds(t.t * P, P)], start=(ch == 0), stop=(ch == C - 1))
                        ins.then_inc(done[t.k], 1)

                def down(t):
                    if t is None:
                        return
                    seen(pe, hb_ok, t)
                    seen(pe, y_ok, t.at(-2))
                    for j in range(FJ):
                        ins = pe.matmul(ps[6 + t.k][:, 0:D], fh[:, t.k, j * P:(j + 1) * P], fw2[:, j, :],
                                        start=(j == 0), stop=(j == FJ - 1))
                    ins.then_inc(y_ps[t.k], 1)

                def body(t):
                    turn(t.at(0), ga, ga_T, ga_in, gb_ok, 0)
                    up(t.at(-3))
                    turn(t.at(-2), x3, x3_T, x3_ok, x3_Tc, 2)
                    down(t.at(-4))

                def count(r):
                    pe.wait_ge(s_cnt, r + 1)
                    pe.matmul(ps[0][:, 0:15], ones[:, :], counts, start=True, stop=True).then_inc(s_tot, 1)

                last = [Tile((NT - n) // 2, (NT - n) % 2, NT) for n in (1, 2)]
                over(pe, NT, body, first=3, more=2)
                count(0)
                up(last[0])
                count(1)
                down(last[1])
                count(2)
                down(last[0])
                for r in range(3, ROUNDS):
                    count(r)
                pe.wait_ge(s_eq, 1)
                pe.matmul(ps[0][:, 0:2 * NT], ones[:, :], marks.rearrange("p a t -> p (a t)"), start=True, stop=True)
                pe.matmul(ps[0][:, 64:64 + NT], tri3, marks[:, 0, :], start=True, stop=True).then_inc(s_eqsum, 1)

            @block.vector
            def _(dve):
                def finish(t):
                    if t is None:
                        return
                    seen(dve, x3_T, t.at(-2))
                    dve.wait_ge(ln4_rs[t.k], 2 * t.i + 2)
                    dve.tensor_scalar(x3[:, t.k, :], gb[:, t.k, :], mv4[:, t.k, 0:1], rs4[:, t.k, 0:1], ALU.subtract,
                                      ALU.mult).then_inc(x3_ok[t.k], 1)
                    seen(dve, x3_ok, t)
                    settle(dve)
                    dve.tensor_tensor(rows[:, ds(t.t, 1), :], gb[:, ds(t.k, 1), :], x3[:, ds(t.k, 1), :], ALU.add)
                    c(dve.tensor_tensor_reduce(xo2, x3[:, t.k, :], wr[:, :], 1.0, 0.0, ALU.mult, ALU.add,
                                               gate[:, t.k, 0:1]))
                    settle(dve)
                    dve.tensor_tensor(w_all[:, ds(t.t, 1)], gate[:, t.k, 0:1], br[:, :], ALU.add).then_inc(gate_ok[t.k], 1)

                def combine(t):
                    if t is None:
                        return
                    dve.wait_ge(ln3_rs[t.k], 2 * t.i + 2)
                    g = gb[:, t.k, :]
                    c(dve.scalar_tensor_tensor(g, ps[t.k][:, 0:D], mv3[:, t.k, 0:1], vecs["L0_gnn_ln_g"][:, :],
                                               ALU.subtract, ALU.mult))
                    c(dve.scalar_tensor_tensor(g, g, rs3[:, t.k, 0:1], vecs["L0_gnn_ln_b"][:, :], ALU.mult, ALU.add))
                    seen(dve, x_in, t, 16)
                    c(dve.tensor_tensor(g, g, xo[:, t.k, :], ALU.add))
                    settle(dve)
                    ga3 = gb[:, ds(t.k, 1), :]
                    dve.tensor_tensor(ga3, ga3, rows[:, ds(t.t, 1), :], ALU.add).then_inc(gb_ok[t.k], 1)
                    seen(dve, gb_ok, t)
                    settle(dve)
                    c(dve.bn_stats(st4[:, t.k, :], g))
                    settle(dve)
                    dve.bn_aggr(mv4[:, t.k, :], st4[:, t.k, :]).then_inc(ln4_var[t.k], 1)

                def stats(t):
                    if t is None:
                        return
                    seen(dve, ga_T, t)
                    settle(dve)
                    c(dve.bn_stats(st3[:, t.k, :], ps[t.k][:, 0:D]))
                    settle(dve)
                    dve.bn_aggr(mv3[:, t.k, :], st3[:, t.k, :]).then_inc(ln3_var[t.k], 1)

                def keep_y(t):
                    if t is None:
                        return
                    seen(dve, y_ps, t)
                    settle(dve)
                    dve.tensor_tensor(cols[:, :, ds(t.t * P, P)], chunks(ps[6 + t.k][:, 0:D]),
                                      chunks(vecs["L0_ffn_b2"][:, :]), ALU.add).then_inc(y_ok[t.k], 1)

                cd3, cs3 = Chain(dve, vc), Chain(dve, vf3)
                c = cs3

                def body(t):
                    nonlocal c
                    dynamic = not isinstance(t.t, int)
                    c = cd3 if dynamic else cs3
                    if dynamic:
                        c.turn(t.t - 6, 6)
                    keep_y(t.at(-5))
                    finish(t.at(-2))
                    combine(t.at(-1))
                    stats(t.at(0))
                    assert not dynamic or c.n == 6, c.n

                over(dve, NT, body, first=3, more=2)

                cs = Chain(dve, vsel)
                dve.wait_ge(s_const3, 1)
                seen_all(dve, gate_ok, NT)
                cs(dve.tensor_tensor(w_all[:, NT - 1:NT], w_all[:, NT - 1:NT], limit, ALU.min))

                def digit(r):
                    shift = 32 - BITS * (r + 1)
                    if r == 0:
                        def as_float(v, key, n):
                            cs(dve.tensor_scalar(v, key, 31, None, ALU.arith_shift_right))
                            cs(dve.tensor_tensor(v, v, flip_i.to_broadcast([P, n]), ALU.bitwise_xor))
                            cs(dve.tensor_tensor(v, v, top_i.to_broadcast([P, n]), ALU.bitwise_or))
                            cs(dve.tensor_tensor(v, v, key, ALU.bitwise_xor))

                        cs(dve.tensor_scalar(cand_i, digits_i, shift, None, ALU.logical_shift_left))
                        as_float(bits_i, cand_i, 15)
                    else:
                        cs(dve.scalar_tensor_tensor(bits_i, digits_i, shift, theta_i.to_broadcast([P, 15]),
                                                    ALU.logical_shift_left, ALU.bitwise_xor))
                    cs(dve.tensor_tensor(reach, w_all[:, :].rearrange("p (a t) -> p a t", a=1).to_broadcast([P, 15, NT]),
                                         bits_i.bitcast(F32).rearrange("p (a t) -> p a t", t=1).to_broadcast([P, 15, NT]),
                                         ALU.is_ge))
                    dve.tensor_reduce(counts, reach, AX, ALU.add).then_inc(s_cnt, 1)
                    dve.wait_ge(s_tot, r + 1)
                    cs(dve.scalar_tensor_tensor(enough, ps[0][:, 0:15], float(KSEL), ones[:, 0:15], ALU.is_ge, ALU.mult,
                                                accum_out=room))
                    cs(dve.tensor_copy(digit_i, room))
                    if r == 0:
                        cs(dve.tensor_scalar(digit_i, digit_i, shift, None, ALU.logical_shift_left))
                        as_float(theta_i, digit_i, 1)
                    else:
                        cs(dve.scalar_tensor_tensor(theta_i, digit_i, shift, theta_i, ALU.logical_shift_left,
                                                    ALU.bitwise_xor))

                tail = [Tile((NT - n) // 2, (NT - n) % 2, NT) for n in (1, 2, 3)]
                digit(0)
                keep_y(tail[2])
                digit(1)
                digit(2)
                keep_y(tail[1])
                for r in range(3, ROUNDS):
                    digit(r)
                theta = theta_i.bitcast(F32)
                dve.tensor_scalar(marks[:, 1, :], w_all[:, :], theta, None, ALU.is_gt)
                dve.tensor_scalar(marks[:, 0, :], w_all[:, :], theta, None, ALU.is_equal).then_inc(s_eq, 1)
                keep_y(tail[0])
                dve.wait_ge(s_eqsum, 1)
                cs(dve.tensor_reduce(room, ps[0][:, NT:2 * NT], AX, ALU.add))
                cs(dve.tensor_scalar(room, room, -1.0, float(KSEL), ALU.mult, ALU.add))
                cs(dve.tensor_copy(run[0], ps[0][:, 0:NT]))
                cs(dve.tensor_tensor(ahead, ps[0][:, 64:64 + NT], run[0], ALU.subtract))
                step, at = 1, 0
                while step < NT:
                    dve.tensor_copy(run[1 - at][:, 0:step], run[at][:, 0:step])
                    cs(dve.tensor_tensor(run[1 - at][:, step:NT], run[at][:, step:NT], run[at][:, 0:NT - step], ALU.add))
                    step, at = 2 * step, 1 - at
                cs(dve.tensor_tensor(ahead, ahead, run[at], ALU.add))
                cs(dve.scalar_tensor_tensor(ahead, ahead, room, marks[:, 0, :], ALU.is_lt, ALU.mult))
                cs(dve.tensor_tensor(ahead, ahead, marks[:, 1, :], ALU.add))
                cs(dve.tensor_tensor(sel[:, :], ahead, w_all[:, :], ALU.mult))

                def output(t):
                    row = rows[:, ds(t.t, 1), :].rearrange("p a (c n) -> p (a c) n", c=C)
                    dve.scalar_tensor_tensor(row, cols[:, :, ds(t.t * P, P)], sel[:, ds(t.t, 1)], row, ALU.mult, ALU.add
                                             ).then_inc(out_ok[t.k], 1)

                over(dve, NT, output)

_INS = ["x", "src", "dst", "edge_type_3", "node_type_6", "L0_gnn_Wk", "L0_gnn_Wq", "L0_gnn_bq",
        "L0_gnn_Wv", "L0_gnn_relation_pri", "L0_gnn_Wa", "L0_gnn_Wm", "L0_gnn_ln_g", "L0_gnn_ln_b",
        "L0_mix_ln1_g", "L0_mix_ln1_b", "L0_mix_b2", "L0_mix_ln2_g", "L0_mix_ln2_b", "L0_ffn_wr", "L0_ffn_br",
        "L0_ffn_w1", "L0_ffn_w2", "L0_ffn_b2"]


def kernel(**inputs):
    import concourse.bacc as _bacc
    from concourse.bass_utils import run_bass_kernel_spmd as _run

    nc = _bacc.Bacc("TRN2", target_bir_lowering=False, num_devices=1)
    lay = {name: np.ascontiguousarray(inputs[name]) for name in _INS}
    lay["mix_WqkvT"] = np.ascontiguousarray(np.asarray(inputs["L0_mix_Wqkv"]).T)
    lay["mix_W1T"] = np.ascontiguousarray(np.asarray(inputs["L0_mix_W1"]).T)
    lay["mix_W2T"] = np.ascontiguousarray(np.asarray(inputs["L0_mix_W2"]).T)
    lay["mix_b1_cols"] = np.ascontiguousarray(np.asarray(inputs["L0_mix_b1"]).reshape(-1, P).T)
    lay["ffn_b1_cols"] = np.ascontiguousarray(np.asarray(inputs["L0_ffn_b1"]).reshape(-1, P).T)
    for name in ("gnn_bk", "gnn_bv"):
        lay[name + "_cols"] = np.ascontiguousarray(np.asarray(inputs["L0_" + name]).reshape(NTY, C, P).transpose(2, 0, 1))
    arrays, args = {}, {}
    for name, v in lay.items():
        arrays[f"in_{name}"] = v
        args[name] = nc.dram_tensor(f"in_{name}", v.shape, mybir.dt.from_np(v.dtype), kind="ExternalInput").ap()
    out = nc.dram_tensor("out_0", (N, D), F32, kind="ExternalOutput").ap()
    build(nc, args, out)
    r = _run(nc, [arrays], core_ids=[0])
    return r.results[0]["out_0"]
```
